# Optimizing a Trainium2 kernel written in Bass

```python
import numpy as np
import jax
import jax.numpy as jnp

def _softmax(x, axis=-1):
    return jax.nn.softmax(x, axis=axis)

def _gelu(x):
    return jax.nn.gelu(x, approximate=True)

def _silu(x):
    return jax.nn.silu(x)

def _sigmoid(x):
    return jax.nn.sigmoid(x)

def _layernorm(x, axis=-1, eps=1e-05):
    m = jnp.mean(x, axis=axis, keepdims=True)
    v = jnp.var(x, axis=axis, keepdims=True)
    return (x - m) / jnp.sqrt(v + eps)

def _scatter_add(tgt, idx, src, axis=0):
    return tgt.at[idx].add(src)

def _segment_sum(src, seg, n):
    return jax.ops.segment_sum(src, seg, n)
kernel_name = 'mk_decoder_postln_d1_seqx_r8_119ccd'

def setup_inputs(seed: int=0):
    np.random.seed(seed)
    _w = jnp.asarray

    def _rec_inputs():
        import jax
        import jax.numpy as jnp
        _rk = jax.random.key(seed)
        x = 7.22e-05 + 1 * jax.random.normal(jax.random.fold_in(_rk, 1), (32, 56, 256), jnp.float32)
        _lenS = 56 - jax.random.randint(jax.random.fold_in(_rk, 7), (32,), 0, max(1, 56 // 4) + 1, jnp.int32)
        _lenS2 = 1500 - jax.random.randint(jax.random.fold_in(_rk, 8), (32,), 0, max(1, 1500 // 4) + 1, jnp.int32)
        _ctx_2048P = jax.random.normal(jax.random.fold_in(_rk, 11), (32, 16, 256), jnp.float32)
        _ctx_2048c = jax.random.dirichlet(jax.random.fold_in(_rk, 511), 0.3 * jnp.ones((16,), jnp.float32), (32, 1500))
        _ctx_2048t = jnp.einsum('bsk,bkd->bsd', _ctx_2048c, _ctx_2048P)
        _ctx_2048t = _ctx_2048t * jax.lax.rsqrt(jnp.mean(jnp.square(_ctx_2048t)) + 1e-12) * 0.953939
        ctx_2048 = 4.13588e-05 + 0.999923 * (_ctx_2048t + 0.3 * jax.random.normal(jax.random.fold_in(_rk, 611), (32, 1500, 256), jnp.float32))
        return (x, ctx_2048)
    x, ctx_2048 = _rec_inputs()

    def _L0_attn_setup():
        import jax, jax.numpy as jnp
        import numpy as np
        B, T, HID, H = (2, 256, 256, 16)
        D = HID // H

        def apply_rope(x):
            b, t, h, d = x.shape
            half = d // 2
            x1, x2 = (x[..., :half], x[..., half:])
            theta = 1.0 / 10000.0 ** (jnp.arange(0, half, 2, dtype=jnp.float32) / half)
            pos = jnp.arange(t, dtype=jnp.float32)
            freq = pos[:, None] * theta[None, :]
            sin = jnp.sin(freq)[None, :, None, :]
            cos = jnp.cos(freq)[None, :, None, :]
            x1e, x1o = (x1[..., ::2], x1[..., 1::2])
            x2e, x2o = (x2[..., ::2], x2[..., 1::2])
            x1r = jnp.concatenate([x1e * cos - x1o * sin, x1e * sin + x1o * cos], axis=-1)
            x2r = jnp.concatenate([x2e * cos - x2o * sin, x2e * sin + x2o * cos], axis=-1)
            return jnp.concatenate([x1r, x2r], axis=-1)
        key = jax.random.key(seed)
        ks = jax.random.split(key, 5)
        s = 0.02
        return {'hidden_states': jax.random.normal(ks[0], (B, T, HID), dtype=jnp.float32), 'Wq': jax.random.normal(ks[1], (HID, HID), dtype=jnp.float32) * s, 'Wk': jax.random.normal(ks[2], (D, HID), dtype=jnp.float32) * s, 'Wv': jax.random.normal(ks[3], (D, HID), dtype=jnp.float32) * s, 'Wo': jax.random.normal(ks[4], (HID, HID), dtype=jnp.float32) * s}
    _L0_attn_all = _L0_attn_setup()
    _L0_attn_in = {k: v for k, v in _L0_attn_all.items() if k in ('Wq', 'Wk', 'Wv', 'Wo')}
    del _L0_attn_all

    def _L0_xattn_setup():
        import math
        import jax, jax.numpy as jnp
        import numpy as np
        HEADS = 16
        MASKED_BIAS = -10000.0

        def _mha(q, k, v):
            B, Sq, D = q.shape
            Sk = k.shape[-2]
            hd = D // HEADS
            qh = q.reshape(B, Sq, HEADS, hd).transpose(0, 2, 1, 3)
            kh = k.reshape(B, Sk, HEADS, hd).transpose(0, 2, 1, 3)
            vh = v.reshape(B, Sk, HEADS, hd).transpose(0, 2, 1, 3)
            scores = jnp.einsum('bhqd,bhkd->bhqk', qh, kh) / math.sqrt(hd)
            qi = jnp.arange(Sq)[:, None] + (Sk - Sq)
            ki = jnp.arange(Sk)[None, :]
            causal = ki <= qi
            scores = jnp.where(causal[None, None], scores, jnp.asarray(MASKED_BIAS, scores.dtype))
            attn = jax.nn.softmax(scores, axis=-1)
            out = jnp.einsum('bhqk,bhkd->bhqd', attn, vh)
            return out.transpose(0, 2, 1, 3).reshape(B, Sq, D)
        key = jax.random.key(seed)
        kq, kk, kv = jax.random.split(key, 3)
        B, S, D = (4, 128, 256)
        q = jax.random.normal(kq, (B, S, D), dtype=jnp.float32)
        k = jax.random.normal(kk, (B, S, D), dtype=jnp.float32)
        v = jax.random.normal(kv, (B, S, D), dtype=jnp.float32)
        return {'q': q, 'k': k, 'v': v}
    _L0_xattn_all = _L0_xattn_setup()
    _L0_xattn_in = {k: v for k, v in _L0_xattn_all.items() if k in ()}
    del _L0_xattn_all

    def _L0_ffn_setup():
        import jax, jax.numpy as jnp
        import numpy as np
        TOP_K = 2
        LORA_SCALE = 32.0 / 16.0
        key = jax.random.key(seed)
        ks = jax.random.split(key, 11)
        B, S, D, F, E, R = (4, 128, 256, 704, 8, 16)
        sd, sf = (1.0 / np.sqrt(D), 1.0 / np.sqrt(F))
        return {'x': jax.random.normal(ks[0], (B, S, D), jnp.float32), 'gate_w': jax.random.normal(ks[1], (E, D), jnp.float32) * 0.02, 'w1': jax.random.normal(ks[2], (F, D), jnp.float32) * sd, 'w3': jax.random.normal(ks[3], (F, D), jnp.float32) * sd, 'w2': jax.random.normal(ks[4], (D, F), jnp.float32) * sf, 'a1': jax.random.normal(ks[5], (E, R, D), jnp.float32) * sd, 'b1': jax.random.normal(ks[6], (E, F, R), jnp.float32) * 0.01, 'a3': jax.random.normal(ks[7], (E, R, D), jnp.float32) * sd, 'b3': jax.random.normal(ks[8], (E, F, R), jnp.float32) * 0.01, 'a2': jax.random.normal(ks[9], (E, R, F), jnp.float32) * sf, 'b2': jax.random.normal(ks[10], (E, D, R), jnp.float32) * 0.01}
    _L0_ffn_all = _L0_ffn_setup()
    _L0_ffn_in = {k: v for k, v in _L0_ffn_all.items() if k in ('gate_w', 'w1', 'w3', 'w2', 'a1', 'b1', 'a3', 'b3', 'a2', 'b2')}
    del _L0_ffn_all
    return {'x': x, 'ctx_2048': ctx_2048, 'L0_attn_Wq': _L0_attn_in['Wq'], 'L0_attn_Wk': _L0_attn_in['Wk'], 'L0_attn_Wv': _L0_attn_in['Wv'], 'L0_attn_Wo': _L0_attn_in['Wo'], 'L0_ffn_gate_w': _L0_ffn_in['gate_w'], 'L0_ffn_w1': _L0_ffn_in['w1'], 'L0_ffn_w3': _L0_ffn_in['w3'], 'L0_ffn_w2': _L0_ffn_in['w2'], 'L0_ffn_a1': _L0_ffn_in['a1'], 'L0_ffn_b1': _L0_ffn_in['b1'], 'L0_ffn_a3': _L0_ffn_in['a3'], 'L0_ffn_b3': _L0_ffn_in['b3'], 'L0_ffn_a2': _L0_ffn_in['a2'], 'L0_ffn_b2': _L0_ffn_in['b2']}

def reference(x, ctx_2048, L0_attn_Wq, L0_attn_Wk, L0_attn_Wv, L0_attn_Wo, L0_ffn_gate_w, L0_ffn_w1, L0_ffn_w3, L0_ffn_w2, L0_ffn_a1, L0_ffn_b1, L0_ffn_a3, L0_ffn_b3, L0_ffn_a2, L0_ffn_b2):
    import jax
    import jax.numpy as jnp

    def _L0_attn_ref(hidden_states, Wq, Wk, Wv, Wo):
        import jax, jax.numpy as jnp
        import numpy as np
        B, T, HID, H = (2, 256, 256, 16)
        D = HID // H

        def apply_rope(x):
            b, t, h, d = x.shape
            half = d // 2
            x1, x2 = (x[..., :half], x[..., half:])
            theta = 1.0 / 10000.0 ** (jnp.arange(0, half, 2, dtype=jnp.float32) / half)
            pos = jnp.arange(t, dtype=jnp.float32)
            freq = pos[:, None] * theta[None, :]
            sin = jnp.sin(freq)[None, :, None, :]
            cos = jnp.cos(freq)[None, :, None, :]
            x1e, x1o = (x1[..., ::2], x1[..., 1::2])
            x2e, x2o = (x2[..., ::2], x2[..., 1::2])
            x1r = jnp.concatenate([x1e * cos - x1o * sin, x1e * sin + x1o * cos], axis=-1)
            x2r = jnp.concatenate([x2e * cos - x2o * sin, x2e * sin + x2o * cos], axis=-1)
            return jnp.concatenate([x1r, x2r], axis=-1)
        b, t, _ = hidden_states.shape
        scaling = D ** (-0.5)
        q = (hidden_states @ Wq.T).reshape(b, t, H, D).transpose(0, 2, 1, 3)
        k = hidden_states @ Wk.T
        v = hidden_states @ Wv.T
        q = apply_rope(q)
        k = apply_rope(k[:, None])
        v = v[:, None]
        scores = jnp.einsum('bhqd,bokd->bhqk', q, k) * scaling
        causal = jnp.tril(jnp.ones((t, t), dtype=bool))
        scores = jnp.where(causal[None, None], scores, -jnp.inf)
        probs = jax.nn.softmax(scores, axis=-1)
        attn = jnp.einsum('bhqk,bokd->bhqd', probs, v)
        attn = attn.transpose(0, 2, 1, 3).reshape(b, t, HID)
        return attn @ Wo.T

    def _L0_xattn_ref(q, k, v):
        import math
        import jax, jax.numpy as jnp
        import numpy as np
        HEADS = 16
        MASKED_BIAS = -10000.0

        def _mha(q, k, v):
            B, Sq, D = q.shape
            Sk = k.shape[-2]
            hd = D // HEADS
            qh = q.reshape(B, Sq, HEADS, hd).transpose(0, 2, 1, 3)
            kh = k.reshape(B, Sk, HEADS, hd).transpose(0, 2, 1, 3)
            vh = v.reshape(B, Sk, HEADS, hd).transpose(0, 2, 1, 3)
            scores = jnp.einsum('bhqd,bhkd->bhqk', qh, kh) / math.sqrt(hd)
            qi = jnp.arange(Sq)[:, None] + (Sk - Sq)
            ki = jnp.arange(Sk)[None, :]
            causal = ki <= qi
            scores = jnp.where(causal[None, None], scores, jnp.asarray(MASKED_BIAS, scores.dtype))
            attn = jax.nn.softmax(scores, axis=-1)
            out = jnp.einsum('bhqk,bhkd->bhqd', attn, vh)
            return out.transpose(0, 2, 1, 3).reshape(B, Sq, D)
        return _mha(q, k, v)

    def _L0_ffn_ref(x, gate_w, w1, w3, w2, a1, b1, a3, b3, a2, b2):
        import jax, jax.numpy as jnp
        import numpy as np
        TOP_K = 2
        LORA_SCALE = 32.0 / 16.0
        B, S, D = x.shape
        E = gate_w.shape[0]
        xf = x.reshape(B * S, D)
        N = xf.shape[0]
        logits = xf @ gate_w.T
        top_w, top_i = jax.lax.top_k(logits, TOP_K)
        routing = jax.nn.softmax(top_w, axis=-1)
        w_full = jnp.zeros((N, E), x.dtype).at[jnp.arange(N)[:, None], top_i].add(routing)
        base1 = xf @ w1.T
        base3 = xf @ w3.T

        def expert_step(acc, p):
            A1, B1, A3, B3, A2, B2, we = p
            h1 = base1 + xf @ A1.T @ B1.T * LORA_SCALE
            h3 = base3 + xf @ A3.T @ B3.T * LORA_SCALE
            act = jax.nn.silu(h1) * h3
            out = act @ w2.T + act @ A2.T @ B2.T * LORA_SCALE
            return (acc + we[:, None] * out, None)
        init = jnp.zeros((N, D), x.dtype)
        out, _ = jax.lax.scan(expert_step, init, (a1, b1, a3, b3, a2, b2, w_full.T))
        return out.reshape(B, S, D)
    x = _layernorm(x + _L0_attn_ref(x, L0_attn_Wq, L0_attn_Wk, L0_attn_Wv, L0_attn_Wo), axis=-1)
    x = _layernorm(x + _L0_xattn_ref(x, ctx_2048, ctx_2048), axis=-1)
    x = _layernorm(x + _L0_ffn_ref(x, L0_ffn_gate_w, L0_ffn_w1, L0_ffn_w3, L0_ffn_w2, L0_ffn_a1, L0_ffn_b1, L0_ffn_a3, L0_ffn_b3, L0_ffn_a2, L0_ffn_b2), axis=-1)
    return x

_drawn_inputs = setup_inputs


def setup_inputs(seed=0):
    import zlib

    import numpy as np

    out = dict(_drawn_inputs(seed))
    spreads = {}
    factors = {'L0_attn_Wq': 8.0, 'L0_attn_Wk': 8.0}
    for name, (base, spread) in spreads.items():
        noise = np.random.default_rng([zlib.crc32(name.encode()), seed]).standard_normal(out[name].shape)
        drawn = base * np.exp(spread * noise) if base else spread * noise
        out[name] = jnp.asarray(drawn.astype(out[name].dtype))
    for name, factor in factors.items():
        out[name] = (out[name] * factor).astype(out[name].dtype)
    return out
```

```python
import numpy as np
import concourse.bass as bass
from concourse import mybir
from contextlib import ExitStack

F32 = mybir.dt.float32
I32 = mybir.dt.int32
ALU = mybir.AluOpType
ACT = mybir.ActivationFunctionType
AX = mybir.AxisListType

B, T, D = 32, 56, 256
H, DH = 16, 16
SK = 1500
F, E, R = 704, 8, 16
EPS = 1e-5
MASKED = -10000.0
NEG = -1e30
P = 128
KD = D // P
HB = H // KD
GR = B // 2
SLOT = 64
NCH = 4
CB = B // NCH
CT = CB * T
CG = CB // 2
KT = 125
NT = SK // KT
UN = 500
NU = SK // UN
TU = UN // KT
NP = H // 2
PR = 2 * T
TAIL = T - 1
NF = -(-F // P)
FP = NF * P
FT = [(f, P) for f in range(0, FP, P)]

CONST = {}
_at = 0
for _name, _width in (("ident", P), ("head", HB), ("head4", HB), ("causal", T), ("tail", TAIL), ("cos", D),
                      ("sin", D), ("sel", 2 * SLOT), ("step", E), ("iota", E), ("expert", E), ("grp", CG),
                      ("own", 2 * 4)):
    CONST[_name] = (_at, _at + _width)
    _at += _width
CW = _at


def constants():
    c = np.zeros((P, CW), np.float32)
    row = np.arange(P)

    def put(name, a):
        lo, hi = CONST[name]
        c[:a.shape[0], lo:hi] = a

    put("ident", np.eye(P))
    head = (row[:, None] // DH == np.arange(HB)[None, :]).astype(np.float32)
    put("head", head)
    put("head4", head * np.float32(DH ** -0.5))
    q = row % SLOT
    put("causal", np.where((np.arange(T)[None, :] > q[:, None]) & (q[:, None] < T), NEG, 0.0))
    qq = np.arange(PR) % T
    put("tail", (np.arange(TAIL)[None, :] >= qq[:, None]).astype(np.float32))
    half = DH // 2
    theta = np.float32(1.0) / np.float32(10000.0) ** (np.arange(0, half, 2, dtype=np.float32) / np.float32(half))
    freq = np.arange(H, dtype=np.float32)[:, None] * theta.astype(np.float32)[None, :]
    d = np.arange(D) % DH
    angle = freq[np.arange(D) // DH, (d % half) // 2]
    put("cos", np.tile(np.cos(angle), (P, 1)))
    put("sin", np.tile(np.sin(angle) * np.where(d % 2 == 0, -1, 1), (P, 1)))
    sel = np.zeros((PR, 2, SLOT), np.float32)
    for par in range(2):
        for s in range(SLOT):
            sel[par * T + (s if s < T else 0), par, s] = 1.0
    put("sel", sel.reshape(PR, 2 * SLOT))
    e = row // R
    put("step", (e[:, None] == np.arange(E)).astype(np.float32) - (e[:, None] == np.arange(E) - 1))
    put("iota", np.tile(np.arange(E, dtype=np.float32), (P, 1)))
    ge = np.arange(CG * E)
    put("expert", (ge[:, None] % E == np.arange(E)).astype(np.float32))
    put("grp", (ge[:, None] // E == np.arange(CG)).astype(np.float32))
    put("own", np.tile((row[:, None] % 64 // DH == np.arange(4)).astype(np.float32), (1, 2)))
    return c


def self_attention(nc, a):
    with ExitStack() as ctx:
        def sb(name, shape, dt=F32):
            return ctx.enter_context(nc.sbuf_tensor(name, shape, dt))

        def sem(name):
            return ctx.enter_context(nc.semaphore(name))

        cst, X, X1T = a["cst"], a["X"], a["X1T"]
        ps = a["ps"]

        def C(name, rows=P):
            lo, hi = CONST[name]
            return cst[0:rows, lo:hi]

        xT = sb("xT", [P, KD, B * T])
        wq = sb("wq", [P, KD, 2, D])
        wqr = sb("wq_turned", [P, KD, D])
        wk = sb("wk", [P, KD, P])
        wv = sb("wv", [P, KD, 2, 2 * DH])
        wo = sb("wo", [P, KD, D])
        qT = sb("qT", [P, KD, B * T])
        kT = sb("kT", [P, 1, B * T])
        m1 = sb("wq_cos", [P, KD, D])
        m2 = sb("wq_sin", [P, KD, D])
        qs = sb("qs", [P, 2, KD, 2, SLOT])
        xs = sb("xs", [P, 2, KD, 2, SLOT])
        kbd = sb("kbd", [P, 2, 2, HB, T])
        sm = sb("sm", [P, H, T])
        mx = sb("mx1", [P, H])
        pe_ = sb("p_exp", [P, 2, H, T])
        den = sb("den1", [P, 2, H])
        rden = sb("rden1", [P, 2, H])
        pn = sb("p_norm", [P, 2, H, SLOT])
        vs = sb("vs", [P, 2, 2, 2 * DH])
        pts = sb("pts", [P, NP, P])
        at = sb("at", [P, KD, P])
        y = sb("y1", [P, D])
        st = sb("st1", [P, 6])
        mv = sb("mv1", [P, 2])
        va = sb("va1", [P, 1])
        mh = sb("mh1", [P, 1])
        rs = sb("rs1", [P, 1])
        xn = sb("xn1", [P, D])

        s_c, s_x, s_xt, s_w = sem("c_loaded"), sem("x_loaded"), sem("xT_loaded"), sem("wqk_loaded")
        s_wo = sem("wvo_loaded")
        s_x0, s_z = sem("x_padded"), sem("pads_zero")
        s_prj, s_rot, s_rope, s_cp = sem("projected"), sem("rotated"), sem("turned_weights"), sem("copied")

        with nc.Block() as block:
            @block.sync
            def _(sp):
                sp.dma_start(cst[:], a["consts"]).then_inc(s_c, 16)
                sp.dma_start(wq[:], a["wqT"].rearrange("(k p) v n -> p k v n", p=P)).then_inc(s_w, 16)
                sp.dma_start(wk[:], a["wkT"].rearrange("(k p) n -> p k n", p=P)).then_inc(s_w, 16)
                sp.dma_start(xT[:], a["xT"].rearrange("(k p) n -> p k n", p=P)).then_inc(s_xt, 16)
                sp.dma_start(wv[:], a["wvT"].rearrange("(k p) v n -> p k v n", p=P)).then_inc(s_wo, 16)
                sp.dma_start(wo[:], a["woT"].rearrange("(k p) n -> p k n", p=P)).then_inc(s_wo, 16)
                sp.wait_ge(s_x0, 1)
                xv = a["x"].rearrange("(g two) t d -> two t g d", two=2)
                for par in range(2):
                    sp.dma_start(X[SLOT * par:SLOT * par + T, :, :], xv[par]).then_inc(s_x, 16)
                sp.wait_ge(s_wo, 32)
                sp.wait_ge(s_x, 32)

            @block.tensor
            def _(pe):
                pe.wait_ge(s_xt, 16)
                pe.wait_ge(s_w, 32)
                pe.wait_ge(s_rope, 1)
                for c in range(NCH):
                    for t in range(3):
                        if c >= 2:
                            pe.wait_ge(s_cp, (c - 2) * 3 + t + 1)
                        for k in range(KD):
                            w = wqr[:, k, t * P:(t + 1) * P] if t < 2 else wk[:, k, :]
                            last = nc.tensor.matmul(ps[:, (c % 2) * 3 + t, 0:CT], w, xT[:, k, c * CT:(c + 1) * CT],
                                                    start=(k == 0), stop=(k == KD - 1))
                        last.then_inc(s_prj, 1)

            @block.vector
            def _(dve):
                nc.vector.memset(X[:], 0.0).then_inc(s_x0, 1)
                nc.vector.memset(mh[:], -0.5).then_inc(s_z, 1)
                dve.wait_ge(s_c, 16)
                dve.wait_ge(s_w, 32)
                for v, (dst, tab) in enumerate(((m1, "cos"), (m2, "sin"))):
                    nc.vector.tensor_tensor(dst[:], wq[:, :, v, :], C(tab).unsqueeze(1).to_broadcast([P, KD, D]),
                                            ALU.mult).then_inc(s_rot, 1)
                dve.wait_ge(s_rot, 2)
                nc.vector.tensor_tensor(wqr[:], m1[:], m2[:], ALU.add).then_inc(s_rope, 1)

            @block.scalar
            def _(act):
                for c in range(NCH):
                    for t in range(3):
                        act.wait_ge(s_prj, c * 3 + t + 1)
                        dst = qT[:, t, c * CT:(c + 1) * CT] if t < 2 else kT[:, 0, c * CT:(c + 1) * CT]
                        nc.scalar.activation(dst, ps[:, (c % 2) * 3 + t, 0:CT], ACT.Copy).then_inc(s_cp, 1)

            @block.gpsimd
            def _(pool):
                nc.gpsimd.memset(qs[:], 0.0)
                nc.gpsimd.memset(xs[:], 0.0)
                nc.gpsimd.memset(pn[:], 0.0)
                nc.gpsimd.memset(at[:], 0.0)

        s_st, s_kb = sem("staged"), sem("kbd_ready")
        s_s1, s_v = sem("scores1"), sem("values1")
        s_sm, s_mx, s_sb, s_ex = sem("masked1"), sem("max1"), sem("shifted1"), sem("exp1")
        s_dn, s_rd, s_pn = sem("den1s"), sem("rden1s"), sem("normed1")
        s_vs, s_t1, s_pt = sem("vs_ready"), sem("probs_turned"), sem("pts_ready")
        s_pv, s_at, s_y = sem("attended"), sem("at_ready"), sem("projected_out")
        s_ya, s_bn, s_ag, s_va, s_pw = sem("y1_ready"), sem("bn1"), sem("ag1"), sem("va1s"), sem("rstd1")
        s_xn, s_xst, s_xr, s_x1t = sem("xn1_ready"), sem("x1_stored"), sem("x1_turned"), sem("x1T_ready")

        with nc.Block() as block:
            @block.gpsimd
            def _(pool):
                def stage(i, par):
                    g = i * 2 + par
                    for dst, src in ((qs, qT), (xs, xT)):
                        for k in range(KD):
                            nc.gpsimd.tensor_copy(dst[:, par, k, :, 0:T],
                                                  src[:, k, bass.ds(g * PR, PR)].rearrange("p (b n) -> p b n", n=T)
                                                  ).then_inc(s_st, 1)
                    for b in range(2):
                        nc.gpsimd.tensor_tensor(
                            kbd[:, par, b, :, :],
                            kT[:, 0:1, bass.ds(g * PR + b * T, T)].to_broadcast([P, HB, T]),
                            C("head").unsqueeze(2).to_broadcast([P, HB, T]), ALU.mult).then_inc(s_kb, 1)

                def finish(i, par):
                    g = i * 2 + par
                    pool.wait_ge(s_rd, g + 1)
                    nc.gpsimd.tensor_tensor(pn[:, par, :, 0:T], pe_[:, par, :, :],
                                            rden[:, par, :].unsqueeze(2).to_broadcast([P, H, T]),
                                            ALU.mult).then_inc(s_pn, 1)
                    pool.wait_ge(s_va, g + 1)
                    nc.gpsimd.tensor_tensor(rs[:], va[:], mh[:], ALU.pow).then_inc(s_pw, 1)

                stage(0, 0)
                stage(0, 1)
                def body(i):
                    for par in range(2):
                        finish(i, par)
                        pool.wait_ge(s_v, 2 * i + par + 1)
                        stage(i + 1, par)

                body(0)
                with pool.Fori(1, GR // 2 - 1) as i:
                    body(i)
                for par in range(2):
                    finish(GR // 2 - 1, par)

            @block.tensor
            def _(pe):
                def scores(i, par):
                    g = i * 2 + par
                    pe.wait_ge(s_st, (g + 1) * 2 * KD)
                    pe.wait_ge(s_kb, (g + 1) * 2)
                    for k in range(KD):
                        for b in range(2):
                            last = nc.tensor.matmul(ps[SLOT * b:SLOT * (b + 1), 2 * par + k, 0:HB * T],
                                                    qs[:, par, k, b, :], kbd[:, par, b, :, :].rearrange("p h n -> p (h n)"),
                                                    start=True, stop=True)
                    last.then_inc(s_s1, 1)
                    pe.wait_ge(s_wo, 32)
                    pe.wait_ge(s_vs, g)
                    for b in range(2):
                        for hp in range(2):
                            for k in range(KD):
                                last = nc.tensor.matmul(
                                    ps[SLOT * hp:SLOT * (hp + 1), 6, 256 + 32 * b:256 + 32 * (b + 1)],
                                    xs[:, par, k, b, :], wv[:, k, hp, :], start=(k == 0), stop=(k == KD - 1),
                                    skip_group_check=True)
                    last.then_inc(s_v, 1)

                def rest(i, par):
                    g = i * 2 + par
                    pe.wait_ge(s_pn, g + 1)
                    for hp in range(NP):
                        last = nc.tensor.transpose(ps[:, 4 + hp // 4, (hp % 4) * P:(hp % 4 + 1) * P],
                                                   pn[:, par, 2 * hp:2 * hp + 2, :].rearrange("p h n -> p (h n)"),
                                                   C("ident"))
                        if hp % 4 == 3:
                            last.then_inc(s_t1, 1)
                    pe.wait_ge(s_vs, g + 1)
                    pe.wait_ge(s_pt, (g + 1) * 2)
                    for hp in range(NP):
                        for b in range(2):
                            q = 32 * (hp % 4)
                            o = (hp // 4) * P + b * SLOT
                            last = nc.tensor.matmul(ps[q:q + 32, 6, o:o + SLOT], vs[:, par, b, :],
                                                    pts[:, hp, b * SLOT:(b + 1) * SLOT], start=True, stop=True,
                                                    skip_group_check=True)
                    last.then_inc(s_pv, 1)
                    pe.wait_ge(s_at, g + 1)
                    pe.wait_ge(s_x1t, g * KD)
                    for k in range(KD):
                        last = nc.tensor.matmul(ps[:, 7, 0:D], at[:, k, :], wo[:, k, :], start=(k == 0),
                                                stop=(k == KD - 1))
                    last.then_inc(s_y, 1)
                    pe.wait_ge(s_xn, g + 1)
                    for k in range(KD):
                        last = nc.tensor.transpose(ps[:, 7, D + k * P:D + (k + 1) * P], xn[:, k * P:(k + 1) * P],
                                                   C("ident"))
                    last.then_inc(s_xr, 1)

                scores(0, 0)
                def body(i):
                    scores(i, 1)
                    rest(i, 0)
                    scores(i + 1, 0)
                    rest(i, 1)

                body(0)
                with pe.Fori(1, GR // 2 - 1) as i:
                    body(i)
                scores(GR // 2 - 1, 1)
                rest(GR // 2 - 1, 0)
                rest(GR // 2 - 1, 1)

            @block.vector
            def _(dve):
                def soft(i, par):
                    g = i * 2 + par
                    dve.wait_ge(s_s1, g + 1)
                    dve.wait_ge(s_ex, g)
                    for k in range(KD):
                        nc.vector.scalar_tensor_tensor(
                            out=sm[:, k * HB:(k + 1) * HB, :],
                            in0=ps[:, 2 * par + k, 0:HB * T].rearrange("p (h n) -> p h n", n=T), scalar=DH ** -0.5,
                            in1=C("causal").unsqueeze(1).to_broadcast([P, HB, T]), op0=ALU.mult,
                            op1=ALU.add).then_inc(s_sm, 1)
                    dve.wait_ge(s_sm, (g + 1) * 2)
                    nc.vector.reduce_max(mx[:], sm[:], AX.X).then_inc(s_mx, 1)
                    dve.wait_ge(s_mx, g + 1)
                    nc.vector.tensor_tensor(sm[:], sm[:], mx[:].unsqueeze(2).to_broadcast([P, H, T]),
                                            ALU.subtract).then_inc(s_sb, 1)
                    dve.wait_ge(s_ex, g + 1)
                    nc.vector.reduce_sum(den[:, par, :], pe_[:, par, :, :], AX.X).then_inc(s_dn, 1)
                    dve.wait_ge(s_dn, g + 1)
                    nc.vector.reciprocal(rden[:, par, :], den[:, par, :]).then_inc(s_rd, 1)

                def norm(i, par):
                    g = i * 2 + par
                    dve.wait_ge(s_y, g + 1)
                    nc.vector.tensor_tensor(y[:], ps[:, 7, 0:D], X[:, bass.ds(g, 1), :].rearrange("p a d -> p (a d)"),
                                            ALU.add).then_inc(s_ya, 1)
                    dve.wait_ge(s_ya, g + 1)
                    nc.vector.bn_stats(st[:], y[:]).then_inc(s_bn, 1)
                    dve.wait_ge(s_z, 1)
                    dve.wait_ge(s_bn, g + 1)
                    nc.vector.bn_aggr(mv[:], st[:]).then_inc(s_ag, 1)
                    dve.wait_ge(s_ag, g + 1)
                    nc.vector.tensor_scalar_add(va[:], mv[:, 1:2], EPS).then_inc(s_va, 1)
                    dve.wait_ge(s_pw, g + 1)
                    dve.wait_ge(s_xst, g)
                    dve.wait_ge(s_xr, g)
                    nc.vector.tensor_scalar(xn[:], y[:], mv[:, 0:1], rs[:, 0:1], ALU.subtract,
                                            ALU.mult).then_inc(s_xn, 1)

                soft(0, 0)
                def body(i):
                    soft(i, 1)
                    norm(i, 0)
                    soft(i + 1, 0)
                    norm(i, 1)

                body(0)
                with dve.Fori(1, GR // 2 - 1) as i:
                    body(i)
                soft(GR // 2 - 1, 1)
                norm(GR // 2 - 1, 0)
                norm(GR // 2 - 1, 1)

            @block.scalar
            def _(act):
                def soft(i, par):
                    g = i * 2 + par
                    act.wait_ge(s_sb, g + 1)
                    nc.scalar.activation(pe_[:, par, :, :], sm[:], ACT.Exp).then_inc(s_ex, 1)
                    act.wait_ge(s_v, g + 1)
                    nc.scalar.activation(vs[:, par, :, :].rearrange("p b n -> p (b n)"), ps[:, 6, 256:320],
                                         ACT.Copy).then_inc(s_vs, 1)

                def rest(i, par):
                    g = i * 2 + par
                    for j in range(2):
                        act.wait_ge(s_t1, g * 2 + j + 1)
                        if j == 0:
                            act.wait_ge(s_pv, g)
                        nc.scalar.activation(pts[:, 4 * j:4 * j + 4, :].rearrange("p a n -> p (a n)"), ps[:, 4 + j, :],
                                             ACT.Copy).then_inc(s_pt, 1)
                    act.wait_ge(s_pv, g + 1)
                    act.wait_ge(s_y, g)
                    nc.scalar.activation(at[:].rearrange("p a n -> p (a n)"), ps[:, 6, 0:256],
                                         ACT.Copy).then_inc(s_at, 1)
                    act.wait_ge(s_xn, g + 1)
                    nc.scalar.activation(X[:, bass.ds(g, 1), :].rearrange("p a d -> p (a d)"), xn[:],
                                         ACT.Copy).then_inc(s_xst, 1)
                    act.wait_ge(s_xr, g + 1)
                    for k in range(KD):
                        last = nc.scalar.activation(
                            X1T[:, k, bass.ds(g * PR, PR)].rearrange("p (b n) -> p b n", n=T),
                            ps[:, 7, D + k * P:D + (k + 1) * P].rearrange("p (b n) -> p b n", n=SLOT)[:, :, 0:T],
                            ACT.Copy)
                        last.then_inc(s_x1t, 1)

                soft(0, 0)
                def body(i):
                    soft(i, 1)
                    rest(i, 0)
                    soft(i + 1, 0)
                    rest(i, 1)

                body(0)
                with act.Fori(1, GR // 2 - 1) as i:
                    body(i)
                soft(GR // 2 - 1, 1)
                rest(GR // 2 - 1, 0)
                rest(GR // 2 - 1, 1)


COPIER = (("D", "A", "D"), ("D", "A", "A"))
STEPS = 2 * NP


def copies(engine, step, unit):
    order = [COPIER[j % 2][u] for j in range(STEPS) for u in range(NU)]
    return order[:step * NU + unit + 1].count(engine)


def cross_attention(nc, a):
    with ExitStack() as ctx:
        def sb(name, shape, dt=F32):
            return ctx.enter_context(nc.sbuf_tensor(name, shape, dt))

        def sem(name):
            return ctx.enter_context(nc.semaphore(name))

        cst, X, X1T, ps = a["cst"], a["X"], a["X1T"], a["ps"]

        def C(name, rows=P):
            lo, hi = CONST[name]
            return cst[0:rows, lo:hi]

        cT = sb("ctxT", [P, 2, KD, SK])
        cN = sb("ctxN", [KT, 2, NT, D])
        qbd = sb("qbd", [P, 2, KD, HB, T])
        pr = sb("probs", [PR, 2, SK])
        pt = sb("probsT", [KT, 2, NT, 4, PR])
        mx = sb("mx2", [PR, 2, NU + 1])
        nmx = sb("nmx2", [PR, 2])
        fill = sb("fill", [PR, TAIL])
        sums = sb("sums2", [PR, 2, NP, NU])
        ssum = sb("ssum2", [PR, 2, NP])
        om = sb("om", [P, KD, 4, T])
        aT = sb("aT", [P, KD, 2, SLOT])
        rden = sb("rden2", [P, H])
        y0 = sb("y2a", [P, D])
        y = sb("y2", [P, D])
        st = sb("st2", [P, 6])
        mv = sb("mv2", [P, 2])
        va = sb("va2", [P, 1])
        mh = sb("mh2", [P, 1])
        rs = sb("rs2", [P, 1])

        s_cT = [sem("cT_loaded0"), sem("cT_loaded1")]
        s_cN = [sem("cN_loaded0"), sem("cN_loaded1")]
        s_q = sem("qbd_ready")
        s_s = sem("unit_scored")
        s_tail, s_mx, s_nmx = sem("tail_masked"), sem("unit_max"), sem("pair_max")
        s_ex, s_t = sem("unit_exp"), sem("unit_turned")
        s_cp = {"A": sem("unit_copied_act"), "D": sem("unit_copied_dve")}
        s_pv, s_om, s_aT, s_ss = sem("half_attended"), sem("om_ready"), sem("aT_ready"), sem("ssum_ready")
        s_rs, s_at = sem("sums_moved"), sem("attended_turned")
        s_rd, s_y0, s_y, s_bn, s_ag = sem("rden2_ready"), sem("y0_ready"), sem("y2_ready"), sem("bn2"), sem("ag2")
        s_va, s_pw, s_x2 = sem("va2_ready"), sem("rstd2_ready"), sem("x2_ready")
        s_k = sem("fill_ready")
        per = {e: copies(e, STEPS - 1, NU - 1) for e in "AD"}
        O, W, M = 6, 7, 0

        with nc.Block() as block:
            @block.sync
            def _(sp):
                def load(i, par):
                    n = i * 2 + par
                    for k in range(KD):
                        sp.dma_start(cT[:, par, k, :], a["ctxT"][bass.ds(n, 1), k * P:(k + 1) * P, :]
                                     .rearrange("a p s -> p (a s)")).then_inc(s_cT[par], 16)

                def load_natural(i, par):
                    n = i * 2 + par
                    sp.dma_start(cN[:, par, :, :], a["ctx"][bass.ds(n, 1), :, :]
                                 .rearrange("a (t p) d -> p (a t) d", p=KT)).then_inc(s_cN[par], 16)

                for par in range(2):
                    load(0, par)
                    load_natural(0, par)
                with sp.Fori(1, GR) as i:
                    for par in range(2):
                        sp.wait_ge(s_s, (i * 2 + par - 1) * NP * NU)
                        load(i, par)
                        sp.wait_ge(s_pv, (i * 2 + par - 1) * 2)
                        load_natural(i, par)

            @block.gpsimd
            def _(pool):
                nc.gpsimd.memset(mh[:], -0.5)

                def queries(i, par):
                    n = i * 2 + par
                    for k in range(KD):
                        nc.gpsimd.tensor_tensor(
                            qbd[:, par, k, :, :], X1T[:, k:k + 1, bass.ds(n * T, T)].to_broadcast([P, HB, T]),
                            C("head4").unsqueeze(2).to_broadcast([P, HB, T]), ALU.mult).then_inc(s_q, 1)

                def deviation(i):
                    pool.wait_ge(s_va, i + 1)
                    nc.gpsimd.tensor_tensor(rs[:], va[:], mh[:], ALU.pow).then_inc(s_pw, 1)

                queries(0, 0)
                queries(0, 1)
                with pool.Fori(0, GR - 1) as i:
                    for par in range(2):
                        pool.wait_ge(s_s, (i * 2 + par + 1) * NP * NU)
                        queries(i + 1, par)
                    deviation(i)
                deviation(GR - 1)

            @block.tensor
            def _(pe):
                def scores(i, j, u):
                    if j == STEPS:
                        i, j = i + 1, 0
                    par, p = j // NP, j % NP
                    k = p // 4
                    if u == 0 and p == 0:
                        pe.wait_ge(s_cT[par], (i + 1) * 16 * KD)
                        pe.wait_ge(s_q, (i * 2 + par + 1) * KD)
                    n = j * NU + u - 3
                    if not (isinstance(i, int) and i * STEPS * NU + n < 1):
                        pe.wait_ge(s_ex, i * (STEPS * NU) + n)
                    last = nc.tensor.matmul(
                        ps[0:PR, (j * NU + u) % 4, 0:UN],
                        qbd[:, par, k, 2 * (p % 4):2 * (p % 4) + 2, :].rearrange("p h n -> p (h n)"),
                        cT[:, par, k, u * UN:(u + 1) * UN], start=True, stop=True)
                    last.then_inc(s_s, 1)

                def turn(i, j, u):
                    par, p = j // NP, j % NP
                    pe.wait_ge(s_ex, i * (STEPS * NU) + j * NU + u + 1)
                    n = j * NU + u - 2
                    if n >= 0:
                        e = COPIER[(n // NU) % 2][n % NU]
                        pe.wait_ge(s_cp[e], i * per[e] + copies(e, n // NU, n % NU))
                    for t in range(TU):
                        last = nc.tensor.transpose(ps[0:KT, 4 + (j * NU + u) % 2, t * PR:(t + 1) * PR],
                                                   pr[:, j % 2, u * UN + t * KT:u * UN + (t + 1) * KT],
                                                   cst[0:PR, 0:PR])
                    last.then_inc(s_t, 1)

                def values(i, half):
                    par, g2 = half // 2, half % 2
                    if g2 == 0:
                        pe.wait_ge(s_cN[par], (i + 1) * 16)
                        pe.wait_ge(s_om, i * 2 + par)
                    for e in "AD":
                        pe.wait_ge(s_cp[e], i * per[e] + copies(e, 4 * half + 3, NU - 1))
                    for t in range(NT):
                        for qp in range(2):
                            c = (2 * g2 + qp) * 64
                            last = nc.tensor.matmul(ps[64 * qp:64 * (qp + 1), O, g2 * 2 * PR:(g2 + 1) * 2 * PR],
                                                    cN[:, par, t, c:c + 64],
                                                    pt[:, half % 2, t, 2 * qp:2 * qp + 2, :]
                                                    .rearrange("p a n -> p (a n)"),
                                                    start=(t == 0), stop=(t == NT - 1), skip_group_check=True)
                    last.then_inc(s_pv, 1)

                def move_sums(i, par):
                    pe.wait_ge(s_ss, i * 2 + par + 1)
                    if par == 0:
                        pe.wait_ge(s_rd, i)
                        pe.wait_ge(s_y0, i)
                    for hp in range(2):
                        last = nc.tensor.matmul(ps[SLOT * par:SLOT * (par + 1), W, D + hp * NP:D + (hp + 1) * NP],
                                                C("sel", PR)[:, hp * SLOT:(hp + 1) * SLOT], ssum[:, par, :],
                                                start=True, stop=True, skip_group_check=True)
                    last.then_inc(s_rs, 1)

                def body(i, last_body):
                    for j in range(STEPS):
                        if not (last_body and j == STEPS - 1):
                            scores(i, j + 1, 0)
                            scores(i, j + 1, 1)
                        turn(i, j, 0)
                        if not (last_body and j == STEPS - 1):
                            scores(i, j + 1, 2)
                        turn(i, j, 1)
                        if j in (4, 8, 12):
                            values(i, j // 4 - 1)
                        turn(i, j, 2)
                        if j == 9:
                            move_sums(i, 0)
                    values(i, 3)
                    move_sums(i, 1)
                    pe.wait_ge(s_aT, i * 2 + 2)
                    for k in range(KD):
                        last = nc.tensor.transpose(ps[:, W, k * P:(k + 1) * P],
                                                   aT[:, k, :, :].rearrange("p b n -> p (b n)"), C("ident"))
                    last.then_inc(s_at, 1)

                for u in range(NU):
                    scores(0, 0, u)
                body(0, False)
                with pe.Fori(1, GR - 1) as i:
                    body(i, False)
                body(GR - 1, True)

            def copy_unit(i, j, u, eng, emit, name):
                eng.wait_ge(s_t, i * (STEPS * NU) + j * NU + u + 1)
                half = (j // 4) % 2
                emit(pt[:, half, u * TU:(u + 1) * TU, j % 4, :],
                     ps[0:KT, 4 + (j * NU + u) % 2, 0:TU * PR].rearrange("p (t n) -> p t n", n=PR)
                     ).then_inc(s_cp[name], 1)

            @block.vector
            def _(dve):
                def maxima(i, j):
                    if j == STEPS:
                        i, j = i + 1, 0
                    n = i * STEPS + j
                    for u in range(NU):
                        dve.wait_ge(s_s, n * NU + u + 1)
                        free = UN if u < NU - 1 else UN - TAIL
                        bank = (j * NU + u) % 4
                        nc.vector.reduce_max(mx[:, j % 2, u:u + 1], ps[0:PR, bank, 0:free], AX.X).then_inc(s_mx, 1)
                    nc.vector.copy_predicated(ps[0:PR, bank, UN - TAIL:UN], C("tail", PR).bitcast(I32),
                                              fill[:]).then_inc(s_tail, 1)
                    dve.wait_ge(s_tail, n + 1)
                    nc.vector.reduce_max(mx[:, j % 2, NU:NU + 1], ps[0:PR, bank, UN - TAIL:UN],
                                         AX.X).then_inc(s_mx, 1)
                    dve.wait_ge(s_mx, (n + 1) * (NU + 1))
                    nc.vector.tensor_reduce(nmx[:, j % 2:j % 2 + 1], mx[:, j % 2, :], AX.X, ALU.max,
                                            negate=True).then_inc(s_nmx, 1)

                def evacuate(i, par):
                    n = i * 2 + par
                    dve.wait_ge(s_pv, (n + 1) * 2)
                    nc.vector.tensor_tensor(om[:].rearrange("p a h n -> p (a h) n"),
                                            ps[:, O, 0:KD * 4 * T].rearrange("p (a n) -> p a n", n=T),
                                            cst_own.unsqueeze(2).to_broadcast([P, KD * 4, T]),
                                            ALU.mult).then_inc(s_om, 1)
                    dve.wait_ge(s_om, n + 1)
                    if par == 0:
                        dve.wait_ge(s_at, i)
                    nc.vector.reduce_sum(aT[:, :, par, 0:T], om[:].rearrange("p a h n -> p a n h"),
                                         AX.X).then_inc(s_aT, 1)
                    dve.wait_ge(s_ex, (n + 1) * NP * NU)
                    nc.vector.reduce_sum(ssum[:, par, :], sums[:, par, :, :], AX.X).then_inc(s_ss, 1)

                def norm(i):
                    dve.wait_ge(s_rs, (i + 1) * 2)
                    dve.wait_ge(s_at, i + 1)
                    nc.vector.reciprocal(rden[:].rearrange("p (a b) -> p b a", b=2),
                                         ps[:, W, D:D + H].rearrange("p (b a) -> p b a", b=2)).then_inc(s_rd, 1)
                    dve.wait_ge(s_rd, i + 1)
                    nc.vector.tensor_tensor(y0[:].rearrange("p (h d) -> p h d", d=DH),
                                            ps[:, W, 0:D].rearrange("p (h d) -> p h d", d=DH),
                                            rden[:].unsqueeze(2).to_broadcast([P, H, DH]), ALU.mult).then_inc(s_y0, 1)
                    dve.wait_ge(s_y0, i + 1)
                    nc.vector.tensor_tensor(y[:], y0[:], X[:, bass.ds(i, 1), :].rearrange("p a d -> p (a d)"),
                                            ALU.add).then_inc(s_y, 1)
                    dve.wait_ge(s_y, i + 1)
                    nc.vector.bn_stats(st[:], y[:]).then_inc(s_bn, 1)
                    dve.wait_ge(s_k, 2)
                    dve.wait_ge(s_bn, i + 1)
                    nc.vector.bn_aggr(mv[:], st[:]).then_inc(s_ag, 1)
                    dve.wait_ge(s_ag, i + 1)
                    nc.vector.tensor_scalar_add(va[:], mv[:, 1:2], EPS).then_inc(s_va, 1)
                    dve.wait_ge(s_pw, i + 1)
                    nc.vector.tensor_scalar(X[:, bass.ds(i, 1), :].rearrange("p a d -> p (a d)"), y[:], mv[:, 0:1],
                                            rs[:, 0:1], ALU.subtract, ALU.mult).then_inc(s_x2, 1)

                cst_own = cst[:, CONST["own"][0]:CONST["own"][1]]
                nc.vector.memset(fill[:], MASKED).then_inc(s_k, 1)
                nc.vector.memset(aT[:], 0.0).then_inc(s_k, 1)
                dve.wait_ge(s_k, 2)

                def body(i, last_body):
                    for j in range(STEPS):
                        if not (last_body and j == STEPS - 1):
                            maxima(i, j + 1)
                        for u in range(NU):
                            if COPIER[j % 2][u] == "D":
                                copy_unit(i, j, u, dve, nc.vector.tensor_copy, "D")
                        if j == 8:
                            evacuate(i, 0)
                    evacuate(i, 1)
                    norm(i)

                maxima(0, 0)
                body(0, False)
                with dve.Fori(1, GR - 1) as i:
                    body(i, False)
                body(GR - 1, True)

            @block.scalar
            def _(act):
                def emit(dst, src):
                    return nc.scalar.activation(dst, src, ACT.Copy)

                def exponentials(i, j):
                    if j == STEPS:
                        i, j = i + 1, 0
                    n = i * STEPS + j
                    act.wait_ge(s_nmx, n + 1)
                    if not (isinstance(i, int) and n < 2):
                        act.wait_ge(s_t, (n - 1) * NU)
                    for u in range(NU):
                        nc.scalar.activation(pr[:, j % 2, u * UN:(u + 1) * UN], ps[0:PR, (j * NU + u) % 4, 0:UN],
                                             ACT.Exp, bias=nmx[:, j % 2:j % 2 + 1],
                                             accum_out=sums[:, j // NP, j % NP, u:u + 1]).then_inc(s_ex, 1)

                def body(i, last_body):
                    for j in range(STEPS):
                        for u in range(NU):
                            if COPIER[j % 2][u] == "A":
                                copy_unit(i, j, u, act, emit, "A")
                        if not (last_body and j == STEPS - 1):
                            exponentials(i, j + 1)

                exponentials(0, 0)
                body(0, False)
                with act.Fori(1, GR - 1) as i:
                    body(i, False)
                body(GR - 1, True)


def feed_forward(nc, a):
    with ExitStack() as ctx:
        def sb(name, shape, dt=F32):
            return ctx.enter_context(nc.sbuf_tensor(name, shape, dt))

        def sem(name):
            return ctx.enter_context(nc.semaphore(name))

        cst, X, ps = a["cst"], a["X"], a["ps"]

        def C(name, rows=P):
            lo, hi = CONST[name]
            return cst[0:rows, lo:hi]

        w13 = sb("w13", [P, 2, KD, FP])
        a13 = sb("a13", [P, 2, KD, E * R])
        b13 = sb("b13", [P, 2, FP])
        step13 = sb("step13", [P, 2, E, FP])
        a2 = sb("a2", [P, NF, E, 32])
        b2 = sb("b2", [P, 2, D])
        w2 = sb("w2", [P, NF, D])
        gate = sb("gate", [P, KD, E])
        xc = sb("xc", [P, CG, D])
        xT = sb("x2T", [P, KD, CG, 2, SLOT])
        lg = sb("logits", [P, CG, E])
        l2 = sb("logits2", [P, CG, E])
        eq = sb("eq", [P, CG, E])
        cand = sb("cand", [P, CG, E])
        oh = [sb(f"first{n}", [P, CG, E]) for n in range(2)]
        top = [sb(f"top{n}", [P, CG]) for n in range(2)]
        idx = sb("idx", [P, CG])
        dif = sb("dif", [P, CG])
        tt = sb("tt", [P, CG])
        t1 = sb("t1", [P, CG])
        r1 = sb("r1", [P, CG])
        r2 = sb("r2", [P, CG])
        wA = sb("wA", [P, CG, E])
        wB = sb("wB", [P, CG, E])
        wr = sb("wr", [P, CG, E])
        wT = sb("wT", [CG * E, P])
        wbd = sb("wbd", [CG * E, CG, 2, T])
        we = sb("we", [P, E, CT])
        us = sb("us", [P, 2, CT])
        si = sb("silu", [P, 2, CT])
        pg = sb("gated", [P, 2, CT])
        wt = sb("weighted", [P, 4, CT])
        acc = sb("acc", [P, NF, CT])
        u2 = sb("u2", [P, 2, CT])
        y = sb("y3", [P, D])
        st = sb("st3", [P, 6])
        mv = sb("mv3", [P, 2])
        va = sb("va3", [P, 1])
        mh = sb("mh3", [P, 1])
        rs = sb("rs3", [P, 1])
        ob = sb("ob", [P, 2, D])

        s_w, s_stp, s_low = sem("weights_loaded"), sem("steps_ready"), sem("low_ready")
        s_xc, s_xr, s_xT = sem("xc_ready"), sem("x2_turned"), sem("x2T_ready")
        s_lp, s_lg, s_r, s_e = sem("logits_done"), sem("logits_out"), sem("router"), sem("router_exp")
        s_wt, s_wT, s_bd = sem("weights_turned"), sem("wT_ready"), sem("wbd_ready")
        s_wp, s_we = sem("we_done"), sem("we_ready")
        s_up, s_us = sem("u_done"), sem("us_ready")
        s_h, s_si, s_pg, s_wg, s_ac, s_u2 = (sem("hidden"), sem("silu_ready"), sem("gated_ready"),
                                             sem("weighted_ready"), sem("acc_ready"), sem("u2_done"))
        s_u2s = sem("u2_out")
        s_o, s_y, s_bn, s_ag, s_va, s_pw, s_ob = (sem("out_done"), sem("y3_ready"), sem("bn3"), sem("ag3"),
                                                  sem("va3_ready"), sem("rstd3_ready"), sem("ob_ready"))
        s_st = [sem("stored0"), sem("stored1")]
        NR = 20
        FE = [(f, e) for f0 in range(0, NF, 2) for e in range(E) for f in (f0, f0 + 1)]
        NFE = len(FE)
        LAG = 2
        U2B, OB = 4, 6

        def sums_done(c, n):
            return c * NF * (E - 1) + sum(e > 0 for _, e in FE[:n + 1])


        with nc.Block() as block:
            @block.sync
            def _(sp):
                for dst, src in (
                        (w13[:], a["w13T"].rearrange("v (k p) n -> p v k n", p=P)),
                        (a13[:], a["a13T"].rearrange("v (k p) n -> p v k n", p=P)),
                        (b13[:], a["b13T"].rearrange("v p n -> p v n")),
                        (gate[:], a["gateT"].rearrange("(k p) n -> p k n", p=P)),
                        (a2[:], a["a2T"].rearrange("(k p) e n -> p k e n", p=P)),
                        (b2[:], a["b2T"].rearrange("b p n -> p b n")),
                        (w2[:], a["w2T"].rearrange("(k p) n -> p k n", p=P))):
                    sp.dma_start(dst, src).then_inc(s_w, 16)
                ov = a["out"].rearrange("(g two) t d -> two t g d", two=2)
                def chunk(c):
                    for gg in range(CG):
                        sp.wait_ge(s_ob, c * CG + gg + 1)
                        for par in range(2):
                            sp.dma_start(ov[par, :, bass.ds(c * CG + gg, 1), :].rearrange("t a d -> t (a d)"),
                                         ob[SLOT * par:SLOT * par + T, gg % 2, :]).then_inc(s_st[gg % 2], 16)

                chunk(0)
                with sp.Fori(1, NCH) as c:
                    chunk(c)
                for n in range(2):
                    sp.wait_ge(s_st[n], GR * 16)

            @block.gpsimd
            def _(pool):
                pool.wait_ge(s_low, 2)
                def chunk(c):
                    pool.wait_ge(s_y, c * CG)
                    nc.gpsimd.tensor_copy(xc[:], X[:, bass.ds(c * CG, CG), :]).then_inc(s_xc, 1)
                    for n, (f, e) in enumerate(FE):
                        w = FT[f][1]
                        pool.wait_ge(s_wg, c * NFE + n + 1)
                        if e == 1:
                            nc.gpsimd.tensor_tensor(acc[0:w, f, :], wt[0:w, (n - 2) % 4, :], wt[0:w, n % 4, :],
                                                    ALU.add).then_inc(s_ac, 1)
                        elif e > 1:
                            pool.wait_ge(s_ac, sums_done(c, n - 2))
                            nc.gpsimd.tensor_tensor(acc[0:w, f, :], acc[0:w, f, :], wt[0:w, n % 4, :],
                                                    ALU.add).then_inc(s_ac, 1)
                    for gg in range(CG):
                        pool.wait_ge(s_va, c * CG + gg + 1)
                        nc.gpsimd.tensor_tensor(rs[:], va[:], mh[:], ALU.pow).then_inc(s_pw, 1)

                chunk(0)
                with pool.Fori(1, NCH) as c:
                    chunk(c)
            @block.tensor
            def _(pe):
                pe.wait_ge(s_w, 16 * 7)
                pe.wait_ge(s_stp, 2 * E)
                def chunk(c):
                    pe.wait_ge(s_xc, c + 1)
                    for gg in range(CG):
                        for k in range(KD):
                            last = nc.tensor.transpose(ps[:, k, gg * P:(gg + 1) * P],
                                                       xc[:, gg, k * P:(k + 1) * P], C("ident"))
                    last.then_inc(s_xr, 1)
                    pe.wait_ge(s_xT, (c + 1) * KD)
                    for gg in range(CG):
                        for k in range(KD):
                            last = nc.tensor.matmul(ps[:, 2, gg * E:(gg + 1) * E],
                                                    xT[:, k, gg, :, :].rearrange("p b n -> p (b n)"),
                                                    gate[:, k, :], start=(k == 0), stop=(k == KD - 1),
                                                    skip_group_check=True)
                    last.then_inc(s_lp, 1)
                    for v in range(2):
                        for k in range(KD):
                            last = nc.tensor.matmul(ps[:, v, 0:CT], a13[:, v, k, :], xT[:, k, :, :, 0:T],
                                                    start=(k == 0), stop=(k == KD - 1))
                    last.then_inc(s_up, 1)
                    pe.wait_ge(s_r, (c + 1) * NR)
                    nc.tensor.transpose(ps[0:CG * E, 3, 0:P], wr[:].rearrange("p g e -> p (g e)"),
                                        C("ident")).then_inc(s_wt, 1)
                    pe.wait_ge(s_bd, c + 1)
                    for e in range(E):
                        if e >= 4:
                            pe.wait_ge(s_we, c * E + e - 3)
                        lo = CONST["expert"][0] + e
                        nc.tensor.matmul(ps[:, 4 + e % 4, 0:CT],
                                         cst[0:CG * E, lo:lo + 1].to_broadcast([CG * E, P]),
                                         wbd[:].rearrange("p g b n -> p (g b n)"), start=True,
                                         stop=True).then_inc(s_wp, 1)
                    pe.wait_ge(s_we, (c + 1) * E)
                    pe.wait_ge(s_us, (c + 1) * 2)

                    def down(n):
                        f, e = FE[n]
                        w = FT[f][1]
                        q = 32 * (e % 4)
                        pe.wait_ge(s_wg, c * NFE + n + 1)
                        nc.tensor.matmul(ps[q:q + 32, U2B + e // 4, 0:CT], a2[0:w, f, e, :], wt[0:w, n % 4, :],
                                         start=(f == 0), stop=(f == NF - 1), skip_group_check=True).then_inc(s_u2, 1)

                    for n, (f, e) in enumerate(FE):
                        f0, w = FT[f]
                        if e > 0:
                            pe.wait_ge(s_si, c * NFE + n - 1)
                            pe.wait_ge(s_pg, c * NFE + n - 1)
                        elif n >= 2:
                            pe.wait_ge(s_si, c * NFE + n - 1)
                            pe.wait_ge(s_pg, c * NFE + n - 1)
                        for v in range(2):
                            bank = 2 * (f % 2) + v
                            if e == 0:
                                for k in range(KD):
                                    nc.tensor.matmul(ps[0:w, bank, 0:CT], w13[:, v, k, f0:f0 + w],
                                                     xT[:, k, :, :, 0:T], start=(k == 0), stop=False,
                                                     skip_group_check=True)
                            last = nc.tensor.matmul(ps[0:w, bank, 0:CT], step13[:, v, e, f0:f0 + w], us[:, v, :],
                                                    start=False, stop=True, skip_group_check=True)
                        last.then_inc(s_h, 1)
                        if n >= LAG:
                            down(n - LAG)
                    for n in range(NFE - LAG, NFE):
                        down(n)
                    pe.wait_ge(s_ac, sums_done(c, NFE - 1))
                    pe.wait_ge(s_u2s, (c + 1) * 2)
                    for gg in range(CG):
                        for par in range(2):
                            cols = slice((2 * gg + par) * T, (2 * gg + par + 1) * T)
                            o = ps[SLOT * par:SLOT * par + T, OB + gg // 2, (gg % 2) * D:(gg % 2 + 1) * D]
                            for f in range(NF):
                                w = FT[f][1]
                                nc.tensor.matmul(o, acc[0:w, f, cols], w2[0:w, f, :], start=(f == 0), stop=False,
                                                 skip_group_check=True)
                            for h in range(2):
                                last = nc.tensor.matmul(o, u2[:, h, cols], b2[:, h, :], start=False, stop=(h == 1),
                                                        skip_group_check=True)
                        if gg % 2:
                            last.then_inc(s_o, 1)

                chunk(0)
                with pe.Fori(1, NCH) as c:
                    chunk(c)
            @block.scalar
            def _(act):
                def chunk(c):
                    act.wait_ge(s_xr, c + 1)
                    for k in range(KD):
                        nc.scalar.activation(xT[:, k, :, :, :].rearrange("p g b n -> p (g b n)"), ps[:, k, :],
                                             ACT.Copy).then_inc(s_xT, 1)
                    act.wait_ge(s_up, c + 1)
                    for v in range(2):
                        nc.scalar.activation(us[:, v, :], ps[:, v, 0:CT], ACT.Copy, scale=2.0).then_inc(s_us, 1)
                    act.wait_ge(s_r, c * NR + 10)
                    nc.scalar.activation(tt[:], dif[:], ACT.Exp).then_inc(s_e, 1)
                    act.wait_ge(s_wt, c + 1)
                    nc.scalar.activation(wT[:], ps[0:CG * E, 3, 0:P], ACT.Copy).then_inc(s_wT, 1)
                    for e in range(E):
                        act.wait_ge(s_wp, c * E + e + 1)
                        nc.scalar.activation(we[:, e, :], ps[:, 4 + e % 4, 0:CT], ACT.Copy).then_inc(s_we, 1)
                    for n, (f, e) in enumerate(FE):
                        w = FT[f][1]
                        act.wait_ge(s_h, c * NFE + n + 1)
                        if n >= 2:
                            act.wait_ge(s_pg, c * NFE + n - 1)
                        nc.scalar.activation(si[0:w, n % 2, :], ps[0:w, 2 * (f % 2), 0:CT],
                                             ACT.Silu).then_inc(s_si, 1)
                    act.wait_ge(s_u2, (c + 1) * NFE)
                    for h in range(2):
                        nc.scalar.activation(u2[:, h, :], ps[:, U2B + h, 0:CT], ACT.Copy,
                                             scale=2.0).then_inc(s_u2s, 1)

                chunk(0)
                with act.Fori(1, NCH) as c:
                    chunk(c)
            @block.vector
            def _(dve):
                nc.vector.memset(mh[:], -0.5).then_inc(s_low, 1)
                nc.vector.memset(ps[:, OB:OB + 2, :], 0.0).then_inc(s_low, 1)
                dve.wait_ge(s_low, 2)
                dve.wait_ge(s_w, 16 * 7)
                for v in range(2):
                    for e in range(E):
                        lo = CONST["step"][0] + e
                        nc.vector.tensor_scalar(step13[:, v, e, :], b13[:, v, :], cst[:, lo:lo + 1], None,
                                                ALU.mult).then_inc(s_stp, 1)
                def chunk(c):
                    count = [0]

                    def link(ins):
                        count[0] += 1
                        ins.then_inc(s_r, 1)
                        dve.wait_ge(s_r, c * NR + count[0])

                    v = nc.vector
                    wide = [P, CG, E]
                    dve.wait_ge(s_lp, c + 1)
                    link(v.tensor_copy(lg[:].rearrange("p g e -> p (g e)"), ps[:, 2, 0:CG * E]))
                    link(v.tensor_copy(l2[:], lg[:]))
                    for n in range(2):
                        src = l2
                        link(v.reduce_max(top[n][:], src[:], AX.X))
                        if n == 1:
                            link(v.tensor_tensor(dif[:], top[1][:], top[0][:], ALU.subtract))
                        link(v.tensor_tensor(eq[:], src[:], top[n][:].unsqueeze(2).to_broadcast(wide), ALU.is_equal))
                        link(v.scalar_tensor_tensor(out=cand[:], in0=eq[:], scalar=-float(E),
                                                    in1=C("iota").unsqueeze(1).to_broadcast(wide), op0=ALU.mult,
                                                    op1=ALU.add))
                        link(v.tensor_reduce(idx[:], cand[:], AX.X, ALU.min))
                        link(v.tensor_tensor(oh[n][:], cand[:], idx[:].unsqueeze(2).to_broadcast(wide), ALU.is_equal))
                        if n == 0:
                            link(v.scalar_tensor_tensor(out=l2[:], in0=oh[0][:], scalar=-3.0e38, in1=lg[:],
                                                        op0=ALU.mult, op1=ALU.add))
                    dve.wait_ge(s_e, c + 1)
                    link(v.tensor_scalar_add(t1[:], tt[:], 1.0))
                    link(v.reciprocal(r1[:], t1[:]))
                    link(v.tensor_tensor(wA[:], oh[0][:], r1[:].unsqueeze(2).to_broadcast(wide), ALU.mult))
                    link(v.tensor_tensor(r2[:], tt[:], r1[:], ALU.mult))
                    link(v.tensor_tensor(wB[:], oh[1][:], r2[:].unsqueeze(2).to_broadcast(wide), ALU.mult))
                    link(v.tensor_tensor(wr[:], wA[:], wB[:], ALU.add))
                    assert count[0] == NR, count[0]
                    dve.wait_ge(s_wT, c + 1)
                    v.tensor_tensor(
                        wbd[:].rearrange("p g b n -> p g b n"),
                        wT[:].rearrange("p (b n) -> p b n", n=SLOT)[:, :, 0:T].unsqueeze(1)
                        .to_broadcast([CG * E, CG, 2, T]),
                        C("grp", CG * E).unsqueeze(2).unsqueeze(3).to_broadcast([CG * E, CG, 2, T]),
                        ALU.mult).then_inc(s_bd, 1)
                    dve.wait_ge(s_we, (c + 1) * E)
                    for n, (f, e) in enumerate(FE):
                        w = FT[f][1]
                        dve.wait_ge(s_si, c * NFE + n + 1)
                        v.tensor_tensor(pg[0:w, n % 2, :], si[0:w, n % 2, :], ps[0:w, 2 * (f % 2) + 1, 0:CT],
                                        ALU.mult).then_inc(s_pg, 1)
                        dve.wait_ge(s_pg, c * NFE + n + 1)
                        if n >= 4:
                            dve.wait_ge(s_ac, sums_done(c, n - 4 + (2 if FE[n - 4][1] == 0 else 0)))
                            dve.wait_ge(s_u2, c * NFE + n - 3)
                        v.tensor_tensor(wt[0:w, n % 4, :], pg[0:w, n % 2, :], we[0:w, e, :],
                                        ALU.mult).then_inc(s_wg, 1)
                    for gg in range(CG):
                        g = c * CG + gg
                        if gg % 2 == 0:
                            dve.wait_ge(s_o, c * 2 + gg // 2 + 1)
                        dve.wait_ge(s_ob, g)
                        v.tensor_tensor(y[:], ps[:, OB + gg // 2, (gg % 2) * D:(gg % 2 + 1) * D], xc[:, gg, :],
                                        ALU.add).then_inc(s_y, 1)
                        dve.wait_ge(s_y, g + 1)
                        v.bn_stats(st[:], y[:]).then_inc(s_bn, 1)
                        dve.wait_ge(s_low, 2)
                        dve.wait_ge(s_bn, g + 1)
                        v.bn_aggr(mv[:], st[:]).then_inc(s_ag, 1)
                        dve.wait_ge(s_ag, g + 1)
                        v.tensor_scalar_add(va[:], mv[:, 1:2], EPS).then_inc(s_va, 1)
                        dve.wait_ge(s_pw, g + 1)
                        if gg >= 2:
                            dve.wait_ge(s_st[gg % 2], (c * 2 + gg // 2) * 32)
                        else:
                            dve.wait_ge(s_st[gg % 2], c * 64)
                        v.tensor_scalar(ob[:, gg % 2, :], y[:], mv[:, 0:1], rs[:, 0:1], ALU.subtract,
                                        ALU.mult).then_inc(s_ob, 1)

                chunk(0)
                with dve.Fori(1, NCH) as c:
                    chunk(c)
def program(nc, a, upto=3):
    with ExitStack() as ctx:
        a["cst"] = ctx.enter_context(nc.sbuf_tensor("cst", [P, CW], F32))
        a["X"] = ctx.enter_context(nc.sbuf_tensor("X", [P, GR, D], F32))
        a["ps"] = ctx.enter_context(nc.psum_tensor("ps", [P, 8, 512], F32))
        with nc.sbuf_tensor("X1T", [P, KD, B * T], F32) as X1T:
            a["X1T"] = X1T
            self_attention(nc, a)
            if upto >= 2:
                cross_attention(nc, a)
        if upto >= 3:
            feed_forward(nc, a)
        else:
            with nc.semaphore("dbg") as s, nc.Block() as block:
                @block.sync
                def _(sp):
                    ov = a["out"].rearrange("(g two) t d -> two t g d", two=2)
                    for par in range(2):
                        sp.dma_start(ov[par], a["X"][SLOT * par:SLOT * par + T, :, :]).then_inc(s, 16)
                    sp.wait_ge(s, 32)


def layouts(i):
    swap = np.arange(D) ^ 1
    wq, wk, wv = i["L0_attn_Wq"], i["L0_attn_Wk"], i["L0_attn_Wv"]
    z = np.zeros((D, DH), wv.dtype)
    t = np.ascontiguousarray

    def wide(m):
        return np.concatenate([m, np.zeros((*m.shape[:-1], FP - F), m.dtype)], -1)

    a2 = np.zeros((FP, E, 32), np.float32)
    a2[0:F, :, 0:R] = i["L0_ffn_a2"].transpose(2, 0, 1)
    b2 = np.zeros((2, 4, 32, D), np.float32)
    b2[:, :, 0:R, :] = i["L0_ffn_b2"].transpose(0, 2, 1).reshape(2, 4, R, D)
    return {
        "consts": constants(),
        "x": i["x"], "xT": t(i["x"].reshape(B * T, D).T),
        "ctx": i["ctx_2048"], "ctxT": t(i["ctx_2048"].transpose(0, 2, 1)),
        "wqT": t(np.stack([wq.T, wq[swap].T], 1)),
        "wkT": t(np.tile(wk, (HB, 1)).T),
        "wvT": t(np.stack([np.concatenate([wv.T, z], 1), np.concatenate([z, wv.T], 1)], 1)),
        "woT": t(i["L0_attn_Wo"].T),
        "gateT": t(i["L0_ffn_gate_w"].T),
        "w13T": wide(np.stack([i["L0_ffn_w1"].T, i["L0_ffn_w3"].T])),
        "a13T": t(np.stack([i["L0_ffn_a1"].reshape(E * R, D).T, i["L0_ffn_a3"].reshape(E * R, D).T])),
        "b13T": wide(np.stack([i["L0_ffn_b1"].transpose(0, 2, 1).reshape(E * R, F),
                            i["L0_ffn_b3"].transpose(0, 2, 1).reshape(E * R, F)])),
        "a2T": a2, "b2T": b2.reshape(2, P, D), "w2T": wide(i["L0_ffn_w2"]).T.copy(),
    }


def kernel(**inputs):
    import concourse.bacc as bacc
    from concourse.bass_utils import run_bass_kernel_spmd

    arrays = {f"in_{n}": a for n, a in layouts({n: np.asarray(v) for n, v in inputs.items()}).items()}
    nc = bacc.Bacc("TRN2", target_bir_lowering=False, num_devices=1)
    a = {n[3:]: nc.dram_tensor(n, v.shape, mybir.dt.from_np(v.dtype), kind="ExternalInput").ap()
         for n, v in arrays.items()}
    a["out"] = nc.dram_tensor("out_0", (B, T, D), F32, kind="ExternalOutput").ap()
    program(nc, a)
    r = run_bass_kernel_spmd(nc, [arrays], core_ids=[0])
    return r.results[0]["out_0"]
```

```python
import numpy as np
import concourse.bass as bass
from concourse import mybir
from contextlib import ExitStack

F32 = mybir.dt.float32
F32R = mybir.dt.float32r
I32 = mybir.dt.int32
ALU = mybir.AluOpType
ACT = mybir.ActivationFunctionType
AX = mybir.AxisListType

B, T, D = 32, 56, 256
H, DH = 16, 16
SK = 1500
F, E, R = 704, 8, 16
EPS = 1e-5
MASKED = -10000.0
NEG = -1e30
P = 128
KD = D // P
HB = H // KD
GR = B // 2
SLOT = 64
NCH = 4
CB = B // NCH
CT = CB * T
CG = CB // 2
KT = 125
NT = SK // KT
UN = 500
NU = SK // UN
TU = UN // KT
NP = H // 2
PR = 2 * T
TAIL = T - 1
NF = -(-F // P)
FP = NF * P
FT = [(f, P) for f in range(0, FP, P)]

CONST = {}
_at = 0
for _name, _width in (("ident", P), ("head", HB), ("head4", HB), ("causal", T), ("tail", TAIL), ("cos", D),
                      ("sin", D), ("sel", 2 * SLOT), ("step", E), ("iota", E), ("expert", E), ("grp", CG),
                      ("own", 2 * 4)):
    CONST[_name] = (_at, _at + _width)
    _at += _width
CW = _at


def constants():
    c = np.zeros((P, CW), np.float32)
    row = np.arange(P)

    def put(name, a):
        lo, hi = CONST[name]
        c[:a.shape[0], lo:hi] = a

    put("ident", np.eye(P))
    head = (row[:, None] // DH == np.arange(HB)[None, :]).astype(np.float32)
    put("head", head)
    put("head4", head * np.float32(DH ** -0.5))
    q = row % SLOT
    put("causal", np.where((np.arange(T)[None, :] > q[:, None]) & (q[:, None] < T), NEG, 0.0))
    qq = np.arange(PR) % T
    put("tail", (np.arange(TAIL)[None, :] >= qq[:, None]).astype(np.float32))
    half = DH // 2
    theta = np.float32(1.0) / np.float32(10000.0) ** (np.arange(0, half, 2, dtype=np.float32) / np.float32(half))
    freq = np.arange(H, dtype=np.float32)[:, None] * theta.astype(np.float32)[None, :]
    d = np.arange(D) % DH
    angle = freq[np.arange(D) // DH, (d % half) // 2]
    put("cos", np.tile(np.cos(angle), (P, 1)))
    put("sin", np.tile(np.sin(angle) * np.where(d % 2 == 0, -1, 1), (P, 1)))
    sel = np.zeros((PR, 2, SLOT), np.float32)
    for par in range(2):
        for s in range(SLOT):
            sel[par * T + (s if s < T else 0), par, s] = 1.0
    put("sel", sel.reshape(PR, 2 * SLOT))
    e = row // R
    put("step", (e[:, None] == np.arange(E)).astype(np.float32) - (e[:, None] == np.arange(E) - 1))
    put("iota", np.tile(np.arange(E, dtype=np.float32), (P, 1)))
    ge = np.arange(CG * E)
    put("expert", (ge[:, None] % E == np.arange(E)).astype(np.float32))
    put("grp", (ge[:, None] // E == np.arange(CG)).astype(np.float32))
    put("own", np.tile((row[:, None] % 64 // DH == np.arange(4)).astype(np.float32), (1, 2)))
    return c


def self_attention(nc, a):
    with ExitStack() as ctx:
        def sb(name, shape, dt=F32):
            return ctx.enter_context(nc.sbuf_tensor(name, shape, dt))

        def sem(name):
            return ctx.enter_context(nc.semaphore(name))

        cst, X, X1T = a["cst"], a["X"], a["X1T"]
        ps = a["ps"]

        def C(name, rows=P):
            lo, hi = CONST[name]
            return cst[0:rows, lo:hi]

        xT = sb("xT", [P, KD, B * T])
        wq = sb("wq", [P, KD, 2, D])
        wqr = sb("wq_turned", [P, KD, D])
        wk = sb("wk", [P, KD, P])
        wv = sb("wv", [P, KD, 2, 2 * DH])
        wo = sb("wo", [P, KD, D])
        qT = sb("qT", [P, KD, B * T])
        kT = sb("kT", [P, 1, B * T])
        m1 = sb("wq_cos", [P, KD, D])
        m2 = sb("wq_sin", [P, KD, D])
        qs = sb("qs", [P, 2, KD, 2, SLOT])
        xs = sb("xs", [P, 2, KD, 2, SLOT])
        kbd = sb("kbd", [P, 2, 2, HB, T])
        sm = sb("sm", [P, H, T])
        mx = sb("mx1", [P, H])
        pe_ = sb("p_exp", [P, 2, H, T])
        den = sb("den1", [P, 2, H])
        rden = sb("rden1", [P, 2, H])
        pn = sb("p_norm", [P, 2, H, SLOT])
        vs = sb("vs", [P, 2, 2, 2 * DH])
        pts = sb("pts", [P, NP, P])
        at = sb("at", [P, KD, P])
        y = sb("y1", [P, D])
        st = sb("st1", [P, 6])
        mv = sb("mv1", [P, 2])
        va = sb("va1", [P, 1])
        mh = sb("mh1", [P, 1])
        rs = sb("rs1", [P, 1])
        xn = sb("xn1", [P, D])

        s_c, s_x, s_xt, s_w = sem("c_loaded"), sem("x_loaded"), sem("xT_loaded"), sem("wqk_loaded")
        s_wo = sem("wvo_loaded")
        s_x0, s_z = sem("x_padded"), sem("pads_zero")
        s_prj, s_rot, s_rope, s_cp = sem("projected"), sem("rotated"), sem("turned_weights"), sem("copied")

        with nc.Block() as block:
            @block.sync
            def _(sp):
                sp.dma_start(cst[:], a["consts"]).then_inc(s_c, 16)
                sp.dma_start(wq[:], a["wqT"].rearrange("(k p) v n -> p k v n", p=P)).then_inc(s_w, 16)
                sp.dma_start(wk[:], a["wkT"].rearrange("(k p) n -> p k n", p=P)).then_inc(s_w, 16)
                sp.dma_start(xT[:], a["xT"].rearrange("(k p) n -> p k n", p=P)).then_inc(s_xt, 16)
                sp.dma_start(wv[:], a["wvT"].rearrange("(k p) v n -> p k v n", p=P)).then_inc(s_wo, 16)
                sp.dma_start(wo[:], a["woT"].rearrange("(k p) n -> p k n", p=P)).then_inc(s_wo, 16)
                sp.wait_ge(s_x0, 1)
                xv = a["x"].rearrange("(g two) t d -> two t g d", two=2)
                for par in range(2):
                    sp.dma_start(X[SLOT * par:SLOT * par + T, :, :], xv[par]).then_inc(s_x, 16)
                sp.wait_ge(s_wo, 32)
                sp.wait_ge(s_x, 32)

            @block.tensor
            def _(pe):
                pe.wait_ge(s_xt, 16)
                pe.wait_ge(s_w, 32)
                pe.wait_ge(s_rope, 1)
                for c in range(NCH):
                    for t in range(3):
                        if c >= 2:
                            pe.wait_ge(s_cp, (c - 2) * 3 + t + 1)
                        for k in range(KD):
                            w = wqr[:, k, t * P:(t + 1) * P] if t < 2 else wk[:, k, :]
                            last = nc.tensor.matmul(ps[:, (c % 2) * 3 + t, 0:CT], w, xT[:, k, c * CT:(c + 1) * CT],
                                                    start=(k == 0), stop=(k == KD - 1))
                        last.then_inc(s_prj, 1)

            @block.vector
            def _(dve):
                nc.vector.memset(X[:], 0.0).then_inc(s_x0, 1)
                nc.vector.memset(mh[:], -0.5).then_inc(s_z, 1)
                dve.wait_ge(s_c, 16)
                dve.wait_ge(s_w, 32)
                for v, (dst, tab) in enumerate(((m1, "cos"), (m2, "sin"))):
                    nc.vector.tensor_tensor(dst[:], wq[:, :, v, :], C(tab).unsqueeze(1).to_broadcast([P, KD, D]),
                                            ALU.mult).then_inc(s_rot, 1)
                dve.wait_ge(s_rot, 2)
                nc.vector.tensor_tensor(wqr[:], m1[:], m2[:], ALU.add).then_inc(s_rope, 1)

            @block.scalar
            def _(act):
                for c in range(NCH):
                    for t in range(3):
                        act.wait_ge(s_prj, c * 3 + t + 1)
                        dst = qT[:, t, c * CT:(c + 1) * CT] if t < 2 else kT[:, 0, c * CT:(c + 1) * CT]
                        nc.scalar.activation(dst, ps[:, (c % 2) * 3 + t, 0:CT], ACT.Copy).then_inc(s_cp, 1)

            @block.gpsimd
            def _(pool):
                nc.gpsimd.memset(qs[:], 0.0)
                nc.gpsimd.memset(xs[:], 0.0)
                nc.gpsimd.memset(pn[:], 0.0)
                nc.gpsimd.memset(at[:], 0.0)

        s_st, s_kb = sem("staged"), sem("kbd_ready")
        s_s1, s_v = sem("scores1"), sem("values1")
        s_sm, s_mx, s_sb, s_ex = sem("masked1"), sem("max1"), sem("shifted1"), sem("exp1")
        s_dn, s_rd, s_pn = sem("den1s"), sem("rden1s"), sem("normed1")
        s_vs, s_t1, s_pt = sem("vs_ready"), sem("probs_turned"), sem("pts_ready")
        s_pv, s_at, s_y = sem("attended"), sem("at_ready"), sem("projected_out")
        s_ya, s_bn, s_ag, s_va, s_pw = sem("y1_ready"), sem("bn1"), sem("ag1"), sem("va1s"), sem("rstd1")
        s_xn, s_xst, s_xr, s_x1t = sem("xn1_ready"), sem("x1_stored"), sem("x1_turned"), sem("x1T_ready")

        with nc.Block() as block:
            @block.gpsimd
            def _(pool):
                def stage(i, par):
                    g = i * 2 + par
                    for dst, src in ((qs, qT), (xs, xT)):
                        for k in range(KD):
                            nc.gpsimd.tensor_copy(dst[:, par, k, :, 0:T],
                                                  src[:, k, bass.ds(g * PR, PR)].rearrange("p (b n) -> p b n", n=T)
                                                  ).then_inc(s_st, 1)
                    for b in range(2):
                        nc.gpsimd.tensor_tensor(
                            kbd[:, par, b, :, :],
                            kT[:, 0:1, bass.ds(g * PR + b * T, T)].to_broadcast([P, HB, T]),
                            C("head").unsqueeze(2).to_broadcast([P, HB, T]), ALU.mult).then_inc(s_kb, 1)

                def finish(i, par):
                    g = i * 2 + par
                    pool.wait_ge(s_rd, g + 1)
                    nc.gpsimd.tensor_tensor(pn[:, par, :, 0:T], pe_[:, par, :, :],
                                            rden[:, par, :].unsqueeze(2).to_broadcast([P, H, T]),
                                            ALU.mult).then_inc(s_pn, 1)
                    pool.wait_ge(s_va, g + 1)
                    nc.gpsimd.tensor_tensor(rs[:], va[:], mh[:], ALU.pow).then_inc(s_pw, 1)

                stage(0, 0)
                stage(0, 1)
                def body(i):
                    for par in range(2):
                        finish(i, par)
                        pool.wait_ge(s_v, 2 * i + par + 1)
                        stage(i + 1, par)

                body(0)
                with pool.Fori(1, GR // 2 - 1) as i:
                    body(i)
                for par in range(2):
                    finish(GR // 2 - 1, par)

            @block.tensor
            def _(pe):
                def scores(i, par):
                    g = i * 2 + par
                    pe.wait_ge(s_st, (g + 1) * 2 * KD)
                    pe.wait_ge(s_kb, (g + 1) * 2)
                    for k in range(KD):
                        for b in range(2):
                            last = nc.tensor.matmul(ps[SLOT * b:SLOT * (b + 1), 2 * par + k, 0:HB * T],
                                                    qs[:, par, k, b, :], kbd[:, par, b, :, :].rearrange("p h n -> p (h n)"),
                                                    start=True, stop=True)
                    last.then_inc(s_s1, 1)
                    pe.wait_ge(s_wo, 32)
                    pe.wait_ge(s_vs, g)
                    for b in range(2):
                        for hp in range(2):
                            for k in range(KD):
                                last = nc.tensor.matmul(
                                    ps[SLOT * hp:SLOT * (hp + 1), 6, 256 + 32 * b:256 + 32 * (b + 1)],
                                    xs[:, par, k, b, :], wv[:, k, hp, :], start=(k == 0), stop=(k == KD - 1),
                                    skip_group_check=True)
                    last.then_inc(s_v, 1)

                def rest(i, par):
                    g = i * 2 + par
                    pe.wait_ge(s_pn, g + 1)
                    for hp in range(NP):
                        last = nc.tensor.transpose(ps[:, 4 + hp // 4, (hp % 4) * P:(hp % 4 + 1) * P],
                                                   pn[:, par, 2 * hp:2 * hp + 2, :].rearrange("p h n -> p (h n)"),
                                                   C("ident"))
                        if hp % 4 == 3:
                            last.then_inc(s_t1, 1)
                    pe.wait_ge(s_vs, g + 1)
                    pe.wait_ge(s_pt, (g + 1) * 2)
                    for hp in range(NP):
                        for b in range(2):
                            q = 32 * (hp % 4)
                            o = (hp // 4) * P + b * SLOT
                            last = nc.tensor.matmul(ps[q:q + 32, 6, o:o + SLOT], vs[:, par, b, :],
                                                    pts[:, hp, b * SLOT:(b + 1) * SLOT], start=True, stop=True,
                                                    skip_group_check=True)
                    last.then_inc(s_pv, 1)
                    pe.wait_ge(s_at, g + 1)
                    pe.wait_ge(s_x1t, g * KD)
                    for k in range(KD):
                        last = nc.tensor.matmul(ps[:, 7, 0:D], at[:, k, :], wo[:, k, :], start=(k == 0),
                                                stop=(k == KD - 1))
                    last.then_inc(s_y, 1)
                    pe.wait_ge(s_xn, g + 1)
                    for k in range(KD):
                        last = nc.tensor.transpose(ps[:, 7, D + k * P:D + (k + 1) * P], xn[:, k * P:(k + 1) * P],
                                                   C("ident"))
                    last.then_inc(s_xr, 1)

                scores(0, 0)
                def body(i):
                    scores(i, 1)
                    rest(i, 0)
                    scores(i + 1, 0)
                    rest(i, 1)

                body(0)
                with pe.Fori(1, GR // 2 - 1) as i:
                    body(i)
                scores(GR // 2 - 1, 1)
                rest(GR // 2 - 1, 0)
                rest(GR // 2 - 1, 1)

            @block.vector
            def _(dve):
                def soft(i, par):
                    g = i * 2 + par
                    dve.wait_ge(s_s1, g + 1)
                    dve.wait_ge(s_ex, g)
                    for k in range(KD):
                        nc.vector.scalar_tensor_tensor(
                            out=sm[:, k * HB:(k + 1) * HB, :],
                            in0=ps[:, 2 * par + k, 0:HB * T].rearrange("p (h n) -> p h n", n=T), scalar=DH ** -0.5,
                            in1=C("causal").unsqueeze(1).to_broadcast([P, HB, T]), op0=ALU.mult,
                            op1=ALU.add).then_inc(s_sm, 1)
                    dve.wait_ge(s_sm, (g + 1) * 2)
                    nc.vector.reduce_max(mx[:], sm[:], AX.X).then_inc(s_mx, 1)
                    dve.wait_ge(s_mx, g + 1)
                    nc.vector.tensor_tensor(sm[:], sm[:], mx[:].unsqueeze(2).to_broadcast([P, H, T]),
                                            ALU.subtract).then_inc(s_sb, 1)
                    dve.wait_ge(s_ex, g + 1)
                    nc.vector.reduce_sum(den[:, par, :], pe_[:, par, :, :], AX.X).then_inc(s_dn, 1)
                    dve.wait_ge(s_dn, g + 1)
                    nc.vector.reciprocal(rden[:, par, :], den[:, par, :]).then_inc(s_rd, 1)

                def norm(i, par):
                    g = i * 2 + par
                    dve.wait_ge(s_y, g + 1)
                    nc.vector.tensor_tensor(y[:], ps[:, 7, 0:D], X[:, bass.ds(g, 1), :].rearrange("p a d -> p (a d)"),
                                            ALU.add).then_inc(s_ya, 1)
                    dve.wait_ge(s_ya, g + 1)
                    nc.vector.bn_stats(st[:], y[:]).then_inc(s_bn, 1)
                    dve.wait_ge(s_z, 1)
                    dve.wait_ge(s_bn, g + 1)
                    nc.vector.bn_aggr(mv[:], st[:]).then_inc(s_ag, 1)
                    dve.wait_ge(s_ag, g + 1)
                    nc.vector.tensor_scalar_add(va[:], mv[:, 1:2], EPS).then_inc(s_va, 1)
                    dve.wait_ge(s_pw, g + 1)
                    dve.wait_ge(s_xst, g)
                    dve.wait_ge(s_xr, g)
                    nc.vector.tensor_scalar(xn[:], y[:], mv[:, 0:1], rs[:, 0:1], ALU.subtract,
                                            ALU.mult).then_inc(s_xn, 1)

                soft(0, 0)
                def body(i):
                    soft(i, 1)
                    norm(i, 0)
                    soft(i + 1, 0)
                    norm(i, 1)

                body(0)
                with dve.Fori(1, GR // 2 - 1) as i:
                    body(i)
                soft(GR // 2 - 1, 1)
                norm(GR // 2 - 1, 0)
                norm(GR // 2 - 1, 1)

            @block.scalar
            def _(act):
                def soft(i, par):
                    g = i * 2 + par
                    act.wait_ge(s_sb, g + 1)
                    nc.scalar.activation(pe_[:, par, :, :], sm[:], ACT.Exp).then_inc(s_ex, 1)
                    act.wait_ge(s_v, g + 1)
                    nc.scalar.activation(vs[:, par, :, :].rearrange("p b n -> p (b n)"), ps[:, 6, 256:320],
                                         ACT.Copy).then_inc(s_vs, 1)

                def rest(i, par):
                    g = i * 2 + par
                    for j in range(2):
                        act.wait_ge(s_t1, g * 2 + j + 1)
                        if j == 0:
                            act.wait_ge(s_pv, g)
                        nc.scalar.activation(pts[:, 4 * j:4 * j + 4, :].rearrange("p a n -> p (a n)"), ps[:, 4 + j, :],
                                             ACT.Copy).then_inc(s_pt, 1)
                    act.wait_ge(s_pv, g + 1)
                    act.wait_ge(s_y, g)
                    nc.scalar.activation(at[:].rearrange("p a n -> p (a n)"), ps[:, 6, 0:256],
                                         ACT.Copy).then_inc(s_at, 1)
                    act.wait_ge(s_xn, g + 1)
                    nc.scalar.activation(X[:, bass.ds(g, 1), :].rearrange("p a d -> p (a d)"), xn[:],
                                         ACT.Copy).then_inc(s_xst, 1)
                    act.wait_ge(s_xr, g + 1)
                    for k in range(KD):
                        last = nc.scalar.activation(
                            X1T[:, k, bass.ds(g * PR, PR)].rearrange("p (b n) -> p b n", n=T),
                            ps[:, 7, D + k * P:D + (k + 1) * P].rearrange("p (b n) -> p b n", n=SLOT)[:, :, 0:T],
                            ACT.Copy)
                        last.then_inc(s_x1t, 1)

                soft(0, 0)
                def body(i):
                    soft(i, 1)
                    rest(i, 0)
                    soft(i + 1, 0)
                    rest(i, 1)

                body(0)
                with act.Fori(1, GR // 2 - 1) as i:
                    body(i)
                soft(GR // 2 - 1, 1)
                rest(GR // 2 - 1, 0)
                rest(GR // 2 - 1, 1)


COPIER = (("D", "A", "D"), ("D", "A", "D"))
STEPS = 2 * NP


def copies(engine, step, unit):
    order = [COPIER[j % 2][u] for j in range(STEPS) for u in range(NU)]
    return order[:step * NU + unit + 1].count(engine)


def cross_attention(nc, a):
    with ExitStack() as ctx:
        def sb(name, shape, dt=F32):
            return ctx.enter_context(nc.sbuf_tensor(name, shape, dt))

        def sem(name):
            return ctx.enter_context(nc.semaphore(name))

        cst, X, X1T, ps = a["cst"], a["X"], a["X1T"], a["ps"]

        def C(name, rows=P):
            lo, hi = CONST[name]
            return cst[0:rows, lo:hi]

        cT = sb("ctxT", [P, KD, SK])
        kh = sb("keys_high", [P, KD, SK], F32R)
        kq = sb("keys_split", [P, 2, 4, SK], F32R)
        cN = sb("ctxN", [KT, 2, NT, D])
        qbd = sb("qbd", [P, KD, HB, T])
        qh = sb("queries_high", [P, KD, HB, T], F32R)
        qq = sb("queries_split", [P, 2, 2, 4, 4, T], F32R)
        pr = sb("probs", [PR, 2, SK])
        pt = sb("probsT", [KT, 2, NT, 4, PR])
        mx = sb("mx2", [PR, 2, NU + 1])
        nmx = sb("nmx2", [PR, 2])
        fill = sb("fill", [PR, TAIL])
        sums = sb("sums2", [PR, 2, NP, NU])
        ssum = sb("ssum2", [PR, 2, NP])
        om = sb("om", [P, KD, 4, T])
        aT = sb("aT", [P, KD, 2, SLOT])
        rden = sb("rden2", [P, H])
        y = sb("y2", [P, D])
        st = sb("st2", [P, 6])
        mv = sb("mv2", [P, 2])
        va = sb("va2", [P, 1])
        mh = sb("mh2", [P, 1])
        rs = sb("rs2", [P, 1])
        zero = sb("zero", [P, 1])

        s_cT = [sem("cT_loaded0"), sem("cT_loaded1")]
        s_kh, s_kl = sem("keys_high_ready"), sem("keys_low_ready")
        s_kd = [sem("keys_placed0"), sem("keys_placed1")]
        s_qd = [sem("queries_placed0"), sem("queries_placed1")]
        s_cN = [sem("cN_loaded0"), sem("cN_loaded1")]
        s_q, s_qh, s_ql = sem("qbd_ready"), sem("queries_high_ready"), sem("queries_low_ready")
        s_s = sem("unit_scored")
        s_tail, s_mx, s_nmx = sem("tail_masked"), sem("unit_max"), sem("pair_max")
        s_ex, s_t = sem("unit_exp"), sem("unit_turned")
        s_cp = {"A": sem("unit_copied_act"), "D": sem("unit_copied_dve")}
        s_pv, s_om, s_aT, s_ss = sem("half_attended"), sem("om_ready"), sem("aT_ready"), sem("ssum_ready")
        s_rs, s_at = sem("sums_moved"), sem("attended_turned")
        s_rd, s_y0, s_y, s_bn, s_ag = sem("rden2_ready"), sem("y0_ready"), sem("y2_ready"), sem("bn2"), sem("ag2")
        s_va, s_pw, s_x2 = sem("va2_ready"), sem("rstd2_ready"), sem("x2_ready")
        s_k, s_z = sem("fill_ready"), sem("zero_ready")
        per = {e: copies(e, STEPS - 1, NU - 1) for e in "AD"}
        TB, O = 6, 7

        with nc.Block() as block:
            @block.sync
            def _(sp):
                def load(n, k):
                    sp.dma_start(cT[:, k, :], a["ctxT"][bass.ds(n, 1), k * P:(k + 1) * P, :]
                                 .rearrange("a p s -> p (a s)")).then_inc(s_cT[k], 16)

                def load_natural(n, par):
                    sp.dma_start(cN[:, par, :, :], a["ctx"][bass.ds(n, 1), :, :]
                                 .rearrange("a (t p) d -> p (a t) d", p=KT)).then_inc(s_cN[par], 16)

                def place_queries(n, par, scored):
                    sp.wait_ge(s_ql, n + 1)
                    if scored is not None:
                        sp.wait_ge(s_s, scored)
                    for h in range(2):
                        for to in range(2):
                            rows, other = slice(64 * h, 64 * h + 64), slice(64 * to, 64 * to + 64)
                            sp.dma_start(qq[other, par, 0, h:4:2, :, :].bitcast(F32)
                                         .rearrange("p k h n -> p k (h n)"),
                                         qh[rows, :, 4 * h:4 * h + 4, :].bitcast(F32)
                                         .rearrange("p k h n -> p k (h n)")).then_inc(s_qd[par], 16)
                            sp.dma_start(qq[other, par, 1, h:4:2, :, :].bitcast(F32)
                                         .rearrange("p k h n -> p k (h n)"),
                                         qbd[rows, :, 4 * h:4 * h + 4, :]
                                         .rearrange("p k h n -> p k (h n)")).then_inc(s_qd[par], 16)

                def place_keys(n, par, last):
                    for k in range(KD):
                        sp.wait_ge(s_kl, n * KD + k + 1)
                        for h in range(2):
                            rows, other = slice(64 * h, 64 * h + 64), slice(64 * (1 - h), 64 * (1 - h) + 64)
                            sp.dma_start(kq[rows, par, 2 * k + h, :].bitcast(F32),
                                         kh[rows, k, :].bitcast(F32)).then_inc(s_kd[k], 16)
                            sp.dma_start(kq[other, par, 2 * k + h, :].bitcast(F32),
                                         cT[rows, k, :]).then_inc(s_kd[k], 16)
                        if not last:
                            sp.wait_ge(s_kd[k], (n + 1) * 64)
                            load(n + 1, k)

                def group(i, first, last):
                    for par in range(2):
                        n = i * 2 + par
                        place_queries(n, par, None if first else (n - 1) * NP * NU)
                        if not (first and par == 0):
                            if not (first or (par == 0 and isinstance(i, int) and i == 1)):
                                sp.wait_ge(s_pv, i * 4 - 4 + 2 * par)
                            load_natural(n - 1, 1 - par)
                        place_keys(n, par, last and par == 1)

                for k in range(KD):
                    load(0, k)
                group(0, True, False)
                group(1, False, False)
                with sp.Fori(2, GR - 1) as i:
                    group(i, False, False)
                group(GR - 1, False, True)
                sp.wait_ge(s_pv, (B - 2) * 2)
                load_natural(B - 1, 1)

            @block.gpsimd
            def _(pool):
                nc.gpsimd.memset(mh[:], -0.5)
                nc.gpsimd.memset(zero[:], 0.0).then_inc(s_z, 1)
                pool.wait_ge(s_z, 1)

                def queries(n, placed):
                    if placed is not None:
                        pool.wait_ge(*placed)
                    for k in range(KD):
                        nc.gpsimd.tensor_tensor(
                            qbd[:, k, :, :], X1T[:, k:k + 1, bass.ds(n * T, T)].to_broadcast([P, HB, T]),
                            C("head4").unsqueeze(2).to_broadcast([P, HB, T]), ALU.mult).then_inc(s_q, 1)
                    pool.wait_ge(s_q, (n + 1) * KD)
                    nc.gpsimd.tensor_tensor(qh[:].rearrange("p k h n -> p (k h n)"),
                                            qbd[:].rearrange("p k h n -> p (k h n)"),
                                            zero[:].to_broadcast([P, KD * HB * T]), ALU.add).then_inc(s_qh, 1)
                    pool.wait_ge(s_qh, n + 1)
                    nc.gpsimd.tensor_tensor(qbd[:], qbd[:], qh[:].bitcast(F32), ALU.subtract).then_inc(s_ql, 1)

                def keys(n):
                    for k in range(KD):
                        pool.wait_ge(s_cT[k], (n + 1) * 16)
                        nc.gpsimd.tensor_tensor(kh[:, k, :], cT[:, k, :], zero[:].to_broadcast([P, SK]),
                                                ALU.add).then_inc(s_kh, 1)
                        pool.wait_ge(s_kh, n * KD + k + 1)
                        nc.gpsimd.tensor_tensor(cT[:, k, :], cT[:, k, :], kh[:, k, :].bitcast(F32),
                                                ALU.subtract).then_inc(s_kl, 1)

                def deviation(i):
                    pool.wait_ge(s_va, i + 1)
                    nc.gpsimd.tensor_tensor(rs[:], va[:], mh[:], ALU.pow).then_inc(s_pw, 1)

                queries(0, None)
                keys(0)
                queries(1, (s_qd[0], 128))
                keys(1)

                def group(i, first):
                    queries(i * 2, (s_qd[1], i * 128))
                    keys(i * 2)
                    if not first:
                        deviation(i - 2)
                    queries(i * 2 + 1, (s_qd[0], (i + 1) * 128))
                    keys(i * 2 + 1)

                group(1, True)
                with pool.Fori(2, GR) as i:
                    group(i, False)
                deviation(GR - 2)
                deviation(GR - 1)

            @block.tensor
            def _(pe):
                def scores(i, j, u):
                    if j == STEPS:
                        i, j = i + 1, 0
                    par, p = j // NP, j % NP
                    if u == 0 and p == 0:
                        pe.wait_ge(s_qd[par], (i + 1) * 128)
                    if u == 0 and p % (NP // KD) == 0:
                        pe.wait_ge(s_kd[p // (NP // KD)], (i * 2 + par + 1) * 64)
                    n = j * NU + u - 5
                    if not (isinstance(i, int) and i * STEPS * NU + n < 1):
                        pe.wait_ge(s_ex, i * (STEPS * NU) + n)
                    for part in range(2):
                        last = nc.tensor.matmul(
                            ps[0:PR, (j % 2) * NU + u, 0:UN],
                            qq[:, par, part, p // 2, 2 * (p % 2):2 * (p % 2) + 2, :].rearrange("p h n -> p (h n)"),
                            kq[:, par, p // 2, u * UN:(u + 1) * UN], start=(part == 0), stop=(part == 1))
                    last.then_inc(s_s, 1)

                def turn(i, j, u):
                    pe.wait_ge(s_ex, i * (STEPS * NU) + j * NU + u + 1)
                    n = j * NU + u - 1
                    if n >= 0:
                        e = COPIER[(n // NU) % 2][n % NU]
                        pe.wait_ge(s_cp[e], i * per[e] + copies(e, n // NU, n % NU))
                    elif not (isinstance(i, int) and i == 0):
                        e = COPIER[1][NU - 1]
                        pe.wait_ge(s_cp[e], i * per[e])
                    for t in range(TU):
                        last = nc.tensor.transpose(ps[0:KT, TB, t * PR:(t + 1) * PR],
                                                   pr[:, j % 2, u * UN + t * KT:u * UN + (t + 1) * KT],
                                                   cst[0:PR, 0:PR])
                    last.then_inc(s_t, 1)

                def values(i, half, piece):
                    if half < 0:
                        i, half = i - 1, half + 4
                    par, g2 = half // 2, half % 2
                    if piece == 0:
                        if g2 == 0:
                            pe.wait_ge(s_cN[par], (i + 1) * 16)
                            pe.wait_ge(s_om, i * 2 + par)
                        for e in "AD":
                            pe.wait_ge(s_cp[e], i * per[e] + copies(e, 4 * half + 3, NU - 1))
                    for qp in range(2):
                        c = (2 * g2 + qp) * 64
                        last = nc.tensor.matmul(ps[64 * qp:64 * (qp + 1), O, g2 * 2 * PR:(g2 + 1) * 2 * PR],
                                                cN[:, par, piece, c:c + 64],
                                                pt[:, half % 2, piece, 2 * qp:2 * qp + 2, :]
                                                .rearrange("p a n -> p (a n)"),
                                                start=(piece == 0), stop=(piece == NT - 1), skip_group_check=True)
                    if piece == NT - 1:
                        last.then_inc(s_pv, 1)

                def finish(i):
                    pe.wait_ge(s_ss, i * 2 + 2)
                    pe.wait_ge(s_aT, i * 2 + 2)
                    for par in range(2):
                        for hp in range(2):
                            nc.tensor.matmul(ps[SLOT * par:SLOT * (par + 1), TB, D + hp * NP:D + (hp + 1) * NP],
                                             C("sel", PR)[:, hp * SLOT:(hp + 1) * SLOT], ssum[:, par, :],
                                             start=True, stop=True, skip_group_check=True)
                    for k in range(KD):
                        last = nc.tensor.transpose(ps[:, TB, k * P:(k + 1) * P],
                                                   aT[:, k, :, :].rearrange("p b n -> p (b n)"), C("ident"))
                    last.then_inc(s_at, 1)

                def body(i, first, last_body):
                    for j in range(STEPS):
                        ahead = not (last_body and j == STEPS - 1)
                        behind = not (first and j < 4)

                        def piece(n):
                            if behind:
                                values(i, j // 4 - 1, (j % 4) * NU + n)

                        if ahead:
                            scores(i, j + 1, 0)
                        if j == 5 and not first:
                            e = COPIER[0][NU - 1]
                            pe.wait_ge(s_cp[e], i * per[e] + copies(e, 4, NU - 1))
                            finish(i - 1)
                            pe.wait_ge(s_y0, i)
                        turn(i, j, 0)
                        if ahead:
                            scores(i, j + 1, 1)
                            scores(i, j + 1, 2)
                        turn(i, j, 1)
                        piece(0)
                        piece(1)
                        turn(i, j, 2)
                        piece(2)

                for u in range(NU):
                    scores(0, 0, u)
                body(0, True, False)
                with pe.Fori(1, GR - 1) as i:
                    body(i, False, False)
                body(GR - 1, False, True)
                for piece in range(NT):
                    values(GR, -1, piece)
                finish(GR - 1)

            def copy_unit(i, j, u, eng, emit, name):
                eng.wait_ge(s_t, i * (STEPS * NU) + j * NU + u + 1)
                half = (j // 4) % 2
                emit(pt[:, half, u * TU:(u + 1) * TU, j % 4, :],
                     ps[0:KT, TB, 0:TU * PR].rearrange("p (t n) -> p t n", n=PR)
                     ).then_inc(s_cp[name], 1)

            @block.vector
            def _(dve):
                def maximum(i, j, u):
                    if j == STEPS:
                        i, j = i + 1, 0
                    n = i * STEPS + j
                    bank = (j % 2) * NU + u
                    dve.wait_ge(s_s, n * NU + u + 1)
                    free = UN if u < NU - 1 else UN - TAIL
                    nc.vector.reduce_max(mx[:, j % 2, u:u + 1], ps[0:PR, bank, 0:free], AX.X).then_inc(s_mx, 1)
                    if u == NU - 1:
                        nc.vector.copy_predicated(ps[0:PR, bank, UN - TAIL:UN], C("tail", PR).bitcast(I32),
                                                  fill[:]).then_inc(s_tail, 1)
                        dve.wait_ge(s_tail, n + 1)
                        nc.vector.reduce_max(mx[:, j % 2, NU:NU + 1], ps[0:PR, bank, UN - TAIL:UN],
                                             AX.X).then_inc(s_mx, 1)
                        dve.wait_ge(s_mx, (n + 1) * (NU + 1))
                        nc.vector.tensor_reduce(nmx[:, j % 2:j % 2 + 1], mx[:, j % 2, :], AX.X, ALU.max,
                                                negate=True).then_inc(s_nmx, 1)

                def evacuate(i, par):
                    n = i * 2 + par
                    dve.wait_ge(s_pv, (n + 1) * 2)
                    nc.vector.tensor_tensor(om[:].rearrange("p a h n -> p (a h) n"),
                                            ps[:, O, 0:KD * 4 * T].rearrange("p (a n) -> p a n", n=T),
                                            cst_own.unsqueeze(2).to_broadcast([P, KD * 4, T]),
                                            ALU.mult).then_inc(s_om, 1)
                    dve.wait_ge(s_om, n + 1)
                    if par == 0 and not (isinstance(i, int) and i == 0):
                        dve.wait_ge(s_at, i)
                    nc.vector.reduce_sum(aT[:, :, par, 0:T], om[:].rearrange("p a h n -> p a n h"),
                                         AX.X).then_inc(s_aT, 1)
                    dve.wait_ge(s_ex, (n + 1) * NP * NU)
                    nc.vector.reduce_sum(ssum[:, par, :], sums[:, par, :, :], AX.X).then_inc(s_ss, 1)

                def norm(i):
                    dve.wait_ge(s_at, i + 1)
                    nc.vector.reciprocal(rden[:].rearrange("p (a b) -> p b a", b=2),
                                         ps[:, TB, D:D + H].rearrange("p (b a) -> p b a", b=2)).then_inc(s_rd, 1)
                    dve.wait_ge(s_rd, i + 1)
                    nc.vector.tensor_tensor(y[:].rearrange("p (h d) -> p h d", d=DH),
                                            ps[:, TB, 0:D].rearrange("p (h d) -> p h d", d=DH),
                                            rden[:].unsqueeze(2).to_broadcast([P, H, DH]), ALU.mult).then_inc(s_y0, 1)

                def norm_stats(i):
                    dve.wait_ge(s_y0, i + 1)
                    nc.vector.tensor_tensor(y[:], y[:], X[:, bass.ds(i, 1), :].rearrange("p a d -> p (a d)"),
                                            ALU.add).then_inc(s_y, 1)
                    dve.wait_ge(s_y, i + 1)
                    nc.vector.bn_stats(st[:], y[:]).then_inc(s_bn, 1)
                    dve.wait_ge(s_k, 2)
                    dve.wait_ge(s_bn, i + 1)
                    nc.vector.bn_aggr(mv[:], st[:]).then_inc(s_ag, 1)
                    dve.wait_ge(s_ag, i + 1)
                    nc.vector.tensor_scalar_add(va[:], mv[:, 1:2], EPS).then_inc(s_va, 1)

                def norm_apply(i):
                    dve.wait_ge(s_pw, i + 1)
                    nc.vector.tensor_scalar(X[:, bass.ds(i, 1), :].rearrange("p a d -> p (a d)"), y[:], mv[:, 0:1],
                                            rs[:, 0:1], ALU.subtract, ALU.mult).then_inc(s_x2, 1)

                cst_own = cst[:, CONST["own"][0]:CONST["own"][1]]
                nc.vector.memset(fill[:], MASKED).then_inc(s_k, 1)
                nc.vector.memset(aT[:], 0.0).then_inc(s_k, 1)
                dve.wait_ge(s_k, 2)

                def body(i, first, last_body):
                    for j in range(STEPS):
                        if j == 4 and not first:
                            evacuate(i - 1, 1)
                        if j == 12:
                            evacuate(i, 0)
                        if j == 5 and not first:
                            norm(i - 1)
                        ahead = not (last_body and j == STEPS - 1)
                        for kind, u in (("max", 0), ("copy", 0), ("max", 1), ("max", 2), ("copy", 1), ("copy", 2)):
                            if kind == "max" and ahead:
                                maximum(i, j + 1, u)
                            if kind == "copy" and COPIER[j % 2][u] == "D":
                                copy_unit(i, j, u, dve, nc.vector.tensor_copy, "D")
                        if j == 5 and not first:
                            norm_stats(i - 1)
                        if j == 11 and not first:
                            norm_apply(i - 1)

                for u in range(NU):
                    maximum(0, 0, u)
                body(0, True, False)
                with dve.Fori(1, GR - 1) as i:
                    body(i, False, False)
                body(GR - 1, False, True)
                evacuate(GR - 1, 1)
                norm(GR - 1)
                norm_stats(GR - 1)
                norm_apply(GR - 1)

            @block.scalar
            def _(act):
                def emit(dst, src):
                    return nc.scalar.activation(dst, src, ACT.Copy)

                def exponentials(i, j):
                    if j == STEPS:
                        i, j = i + 1, 0
                    n = i * STEPS + j
                    act.wait_ge(s_nmx, n + 1)
                    if not (isinstance(i, int) and n < 2):
                        act.wait_ge(s_t, (n - 1) * NU)
                    for u in range(NU):
                        nc.scalar.activation(pr[:, j % 2, u * UN:(u + 1) * UN], ps[0:PR, (j % 2) * NU + u, 0:UN],
                                             ACT.Exp, bias=nmx[:, j % 2:j % 2 + 1],
                                             accum_out=sums[:, j // NP, j % NP, u:u + 1]).then_inc(s_ex, 1)

                def body(i, last_body):
                    for j in range(STEPS):
                        for u in range(NU):
                            if COPIER[j % 2][u] == "A":
                                copy_unit(i, j, u, act, emit, "A")
                        if not (last_body and j == STEPS - 1):
                            exponentials(i, j + 1)

                exponentials(0, 0)
                body(0, False)
                with act.Fori(1, GR - 1) as i:
                    body(i, False)
                body(GR - 1, True)


def feed_forward(nc, a):
    with ExitStack() as ctx:
        def sb(name, shape, dt=F32):
            return ctx.enter_context(nc.sbuf_tensor(name, shape, dt))

        def sem(name):
            return ctx.enter_context(nc.semaphore(name))

        cst, X, ps = a["cst"], a["X"], a["ps"]

        def C(name, rows=P):
            lo, hi = CONST[name]
            return cst[0:rows, lo:hi]

        w13 = sb("w13", [P, 2, KD, FP])
        a13 = sb("a13", [P, 2, KD, E * R])
        b13 = sb("b13", [P, 2, FP])
        step13 = sb("step13", [P, 2, E, FP])
        a2 = sb("a2", [P, NF, E, 32])
        b2 = sb("b2", [P, 2, D])
        w2 = sb("w2", [P, NF, D])
        gate = sb("gate", [P, KD, E])
        xc = sb("xc", [P, CG, D])
        xT = sb("x2T", [P, KD, CG, 2, SLOT])
        lg = sb("logits", [P, CG, E])
        l2 = sb("logits2", [P, CG, E])
        eq = sb("eq", [P, CG, E])
        cand = sb("cand", [P, CG, E])
        oh = [sb(f"first{n}", [P, CG, E]) for n in range(2)]
        top = [sb(f"top{n}", [P, CG]) for n in range(2)]
        idx = sb("idx", [P, CG])
        dif = sb("dif", [P, CG])
        tt = sb("tt", [P, CG])
        t1 = sb("t1", [P, CG])
        r1 = sb("r1", [P, CG])
        r2 = sb("r2", [P, CG])
        wA = sb("wA", [P, CG, E])
        wB = sb("wB", [P, CG, E])
        wr = sb("wr", [P, CG, E])
        wT = sb("wT", [CG * E, P])
        wbd = sb("wbd", [CG * E, CG, 2, T])
        we = sb("we", [P, E, CT])
        us = sb("us", [P, 2, CT])
        si = sb("silu", [P, 2, CT])
        pg = sb("gated", [P, 2, CT])
        wt = sb("weighted", [P, 4, CT])
        acc = sb("acc", [P, NF, CT])
        u2 = sb("u2", [P, 2, CT])
        y = sb("y3", [P, D])
        st = sb("st3", [P, 6])
        mv = sb("mv3", [P, 2])
        va = sb("va3", [P, 1])
        mh = sb("mh3", [P, 1])
        rs = sb("rs3", [P, 1])
        ob = sb("ob", [P, 2, D])

        s_w, s_stp, s_low = sem("weights_loaded"), sem("steps_ready"), sem("low_ready")
        s_xc, s_xr, s_xT = sem("xc_ready"), sem("x2_turned"), sem("x2T_ready")
        s_lp, s_lg, s_r, s_e = sem("logits_done"), sem("logits_out"), sem("router"), sem("router_exp")
        s_wt, s_wT, s_bd = sem("weights_turned"), sem("wT_ready"), sem("wbd_ready")
        s_wp, s_we = sem("we_done"), sem("we_ready")
        s_up, s_us = sem("u_done"), sem("us_ready")
        s_h, s_si, s_pg, s_wg, s_ac, s_u2 = (sem("hidden"), sem("silu_ready"), sem("gated_ready"),
                                             sem("weighted_ready"), sem("acc_ready"), sem("u2_done"))
        s_u2s = sem("u2_out")
        s_o, s_y, s_bn, s_ag, s_va, s_pw, s_ob = (sem("out_done"), sem("y3_ready"), sem("bn3"), sem("ag3"),
                                                  sem("va3_ready"), sem("rstd3_ready"), sem("ob_ready"))
        s_st = [sem("stored0"), sem("stored1")]
        NR = 20
        FE = [(f, e) for f0 in range(0, NF, 2) for e in range(E) for f in (f0, f0 + 1)]
        NFE = len(FE)
        LAG = 2
        U2B, OB = 4, 6

        def sums_done(c, n):
            return c * NF * (E - 1) + sum(e > 0 for _, e in FE[:n + 1])


        with nc.Block() as block:
            @block.sync
            def _(sp):
                for dst, src in (
                        (w13[:], a["w13T"].rearrange("v (k p) n -> p v k n", p=P)),
                        (a13[:], a["a13T"].rearrange("v (k p) n -> p v k n", p=P)),
                        (b13[:], a["b13T"].rearrange("v p n -> p v n")),
                        (gate[:], a["gateT"].rearrange("(k p) n -> p k n", p=P)),
                        (a2[:], a["a2T"].rearrange("(k p) e n -> p k e n", p=P)),
                        (b2[:], a["b2T"].rearrange("b p n -> p b n")),
                        (w2[:], a["w2T"].rearrange("(k p) n -> p k n", p=P))):
                    sp.dma_start(dst, src).then_inc(s_w, 16)
                ov = a["out"].rearrange("(g two) t d -> two t g d", two=2)
                def chunk(c):
                    for gg in range(CG):
                        sp.wait_ge(s_ob, c * CG + gg + 1)
                        for par in range(2):
                            sp.dma_start(ov[par, :, bass.ds(c * CG + gg, 1), :].rearrange("t a d -> t (a d)"),
                                         ob[SLOT * par:SLOT * par + T, gg % 2, :]).then_inc(s_st[gg % 2], 16)

                chunk(0)
                with sp.Fori(1, NCH) as c:
                    chunk(c)
                for n in range(2):
                    sp.wait_ge(s_st[n], GR * 16)

            @block.gpsimd
            def _(pool):
                pool.wait_ge(s_low, 2)
                def chunk(c):
                    pool.wait_ge(s_y, c * CG)
                    nc.gpsimd.tensor_copy(xc[:], X[:, bass.ds(c * CG, CG), :]).then_inc(s_xc, 1)
                    for n, (f, e) in enumerate(FE):
                        w = FT[f][1]
                        pool.wait_ge(s_wg, c * NFE + n + 1)
                        if e == 1:
                            nc.gpsimd.tensor_tensor(acc[0:w, f, :], wt[0:w, (n - 2) % 4, :], wt[0:w, n % 4, :],
                                                    ALU.add).then_inc(s_ac, 1)
                        elif e > 1:
                            pool.wait_ge(s_ac, sums_done(c, n - 2))
                            nc.gpsimd.tensor_tensor(acc[0:w, f, :], acc[0:w, f, :], wt[0:w, n % 4, :],
                                                    ALU.add).then_inc(s_ac, 1)
                    for gg in range(CG):
                        pool.wait_ge(s_va, c * CG + gg + 1)
                        nc.gpsimd.tensor_tensor(rs[:], va[:], mh[:], ALU.pow).then_inc(s_pw, 1)

                chunk(0)
                with pool.Fori(1, NCH) as c:
                    chunk(c)
            @block.tensor
            def _(pe):
                pe.wait_ge(s_w, 16 * 7)
                pe.wait_ge(s_stp, 2 * E)
                def chunk(c):
                    pe.wait_ge(s_xc, c + 1)
                    for gg in range(CG):
                        for k in range(KD):
                            last = nc.tensor.transpose(ps[:, k, gg * P:(gg + 1) * P],
                                                       xc[:, gg, k * P:(k + 1) * P], C("ident"))
                    last.then_inc(s_xr, 1)
                    pe.wait_ge(s_xT, (c + 1) * KD)
                    for gg in range(CG):
                        for k in range(KD):
                            last = nc.tensor.matmul(ps[:, 2, gg * E:(gg + 1) * E],
                                                    xT[:, k, gg, :, :].rearrange("p b n -> p (b n)"),
                                                    gate[:, k, :], start=(k == 0), stop=(k == KD - 1),
                                                    skip_group_check=True)
                    last.then_inc(s_lp, 1)
                    for v in range(2):
                        for k in range(KD):
                            last = nc.tensor.matmul(ps[:, v, 0:CT], a13[:, v, k, :], xT[:, k, :, :, 0:T],
                                                    start=(k == 0), stop=(k == KD - 1))
                    last.then_inc(s_up, 1)
                    pe.wait_ge(s_r, (c + 1) * NR)
                    nc.tensor.transpose(ps[0:CG * E, 3, 0:P], wr[:].rearrange("p g e -> p (g e)"),
                                        C("ident")).then_inc(s_wt, 1)
                    pe.wait_ge(s_bd, c + 1)
                    for e in range(E):
                        if e >= 4:
                            pe.wait_ge(s_we, c * E + e - 3)
                        lo = CONST["expert"][0] + e
                        nc.tensor.matmul(ps[:, 4 + e % 4, 0:CT],
                                         cst[0:CG * E, lo:lo + 1].to_broadcast([CG * E, P]),
                                         wbd[:].rearrange("p g b n -> p (g b n)"), start=True,
                                         stop=True).then_inc(s_wp, 1)
                    pe.wait_ge(s_we, (c + 1) * E)
                    pe.wait_ge(s_us, (c + 1) * 2)

                    def down(n):
                        f, e = FE[n]
                        w = FT[f][1]
                        q = 32 * (e % 4)
                        pe.wait_ge(s_wg, c * NFE + n + 1)
                        nc.tensor.matmul(ps[q:q + 32, U2B + e // 4, 0:CT], a2[0:w, f, e, :], wt[0:w, n % 4, :],
                                         start=(f == 0), stop=(f == NF - 1), skip_group_check=True).then_inc(s_u2, 1)

                    for n, (f, e) in enumerate(FE):
                        f0, w = FT[f]
                        if e > 0:
                            pe.wait_ge(s_si, c * NFE + n - 1)
                            pe.wait_ge(s_pg, c * NFE + n - 1)
                        elif n >= 2:
                            pe.wait_ge(s_si, c * NFE + n - 1)
                            pe.wait_ge(s_pg, c * NFE + n - 1)
                        for v in range(2):
                            bank = 2 * (f % 2) + v
                            if e == 0:
                                for k in range(KD):
                                    nc.tensor.matmul(ps[0:w, bank, 0:CT], w13[:, v, k, f0:f0 + w],
                                                     xT[:, k, :, :, 0:T], start=(k == 0), stop=False,
                                                     skip_group_check=True)
                            last = nc.tensor.matmul(ps[0:w, bank, 0:CT], step13[:, v, e, f0:f0 + w], us[:, v, :],
                                                    start=False, stop=True, skip_group_check=True)
                        last.then_inc(s_h, 1)
                        if n >= LAG:
                            down(n - LAG)
                    for n in range(NFE - LAG, NFE):
                        down(n)
                    pe.wait_ge(s_ac, sums_done(c, NFE - 1))
                    pe.wait_ge(s_u2s, (c + 1) * 2)
                    for gg in range(CG):
                        for par in range(2):
                            cols = slice((2 * gg + par) * T, (2 * gg + par + 1) * T)
                            o = ps[SLOT * par:SLOT * par + T, OB + gg // 2, (gg % 2) * D:(gg % 2 + 1) * D]
                            for f in range(NF):
                                w = FT[f][1]
                                nc.tensor.matmul(o, acc[0:w, f, cols], w2[0:w, f, :], start=(f == 0), stop=False,
                                                 skip_group_check=True)
                            for h in range(2):
                                last = nc.tensor.matmul(o, u2[:, h, cols], b2[:, h, :], start=False, stop=(h == 1),
                                                        skip_group_check=True)
                        if gg % 2:
                            last.then_inc(s_o, 1)

                chunk(0)
                with pe.Fori(1, NCH) as c:
                    chunk(c)
            @block.scalar
            def _(act):
                def chunk(c):
                    act.wait_ge(s_xr, c + 1)
                    for k in range(KD):
                        nc.scalar.activation(xT[:, k, :, :, :].rearrange("p g b n -> p (g b n)"), ps[:, k, :],
                                             ACT.Copy).then_inc(s_xT, 1)
                    act.wait_ge(s_up, c + 1)
                    for v in range(2):
                        nc.scalar.activation(us[:, v, :], ps[:, v, 0:CT], ACT.Copy, scale=2.0).then_inc(s_us, 1)
                    act.wait_ge(s_r, c * NR + 10)
                    nc.scalar.activation(tt[:], dif[:], ACT.Exp).then_inc(s_e, 1)
                    act.wait_ge(s_wt, c + 1)
                    nc.scalar.activation(wT[:], ps[0:CG * E, 3, 0:P], ACT.Copy).then_inc(s_wT, 1)
                    for e in range(E):
                        act.wait_ge(s_wp, c * E + e + 1)
                        nc.scalar.activation(we[:, e, :], ps[:, 4 + e % 4, 0:CT], ACT.Copy).then_inc(s_we, 1)
                    for n, (f, e) in enumerate(FE):
                        w = FT[f][1]
                        act.wait_ge(s_h, c * NFE + n + 1)
                        if n >= 2:
                            act.wait_ge(s_pg, c * NFE + n - 1)
                        nc.scalar.activation(si[0:w, n % 2, :], ps[0:w, 2 * (f % 2), 0:CT],
                                             ACT.Silu).then_inc(s_si, 1)
                    act.wait_ge(s_u2, (c + 1) * NFE)
                    for h in range(2):
                        nc.scalar.activation(u2[:, h, :], ps[:, U2B + h, 0:CT], ACT.Copy,
                                             scale=2.0).then_inc(s_u2s, 1)

                chunk(0)
                with act.Fori(1, NCH) as c:
                    chunk(c)
            @block.vector
            def _(dve):
                nc.vector.memset(mh[:], -0.5).then_inc(s_low, 1)
                nc.vector.memset(ps[:, OB:OB + 2, :], 0.0).then_inc(s_low, 1)
                dve.wait_ge(s_low, 2)
                dve.wait_ge(s_w, 16 * 7)
                for v in range(2):
                    for e in range(E):
                        lo = CONST["step"][0] + e
                        nc.vector.tensor_scalar(step13[:, v, e, :], b13[:, v, :], cst[:, lo:lo + 1], None,
                                                ALU.mult).then_inc(s_stp, 1)
                def chunk(c):
                    count = [0]

                    def link(ins):
                        count[0] += 1
                        ins.then_inc(s_r, 1)
                        dve.wait_ge(s_r, c * NR + count[0])

                    v = nc.vector
                    wide = [P, CG, E]
                    dve.wait_ge(s_lp, c + 1)
                    link(v.tensor_copy(lg[:].rearrange("p g e -> p (g e)"), ps[:, 2, 0:CG * E]))
                    link(v.tensor_copy(l2[:], lg[:]))
                    for n in range(2):
                        src = l2
                        link(v.reduce_max(top[n][:], src[:], AX.X))
                        if n == 1:
                            link(v.tensor_tensor(dif[:], top[1][:], top[0][:], ALU.subtract))
                        link(v.tensor_tensor(eq[:], src[:], top[n][:].unsqueeze(2).to_broadcast(wide), ALU.is_equal))
                        link(v.scalar_tensor_tensor(out=cand[:], in0=eq[:], scalar=-float(E),
                                                    in1=C("iota").unsqueeze(1).to_broadcast(wide), op0=ALU.mult,
                                                    op1=ALU.add))
                        link(v.tensor_reduce(idx[:], cand[:], AX.X, ALU.min))
                        link(v.tensor_tensor(oh[n][:], cand[:], idx[:].unsqueeze(2).to_broadcast(wide), ALU.is_equal))
                        if n == 0:
                            link(v.scalar_tensor_tensor(out=l2[:], in0=oh[0][:], scalar=-3.0e38, in1=lg[:],
                                                        op0=ALU.mult, op1=ALU.add))
                    dve.wait_ge(s_e, c + 1)
                    link(v.tensor_scalar_add(t1[:], tt[:], 1.0))
                    link(v.reciprocal(r1[:], t1[:]))
                    link(v.tensor_tensor(wA[:], oh[0][:], r1[:].unsqueeze(2).to_broadcast(wide), ALU.mult))
                    link(v.tensor_tensor(r2[:], tt[:], r1[:], ALU.mult))
                    link(v.tensor_tensor(wB[:], oh[1][:], r2[:].unsqueeze(2).to_broadcast(wide), ALU.mult))
                    link(v.tensor_tensor(wr[:], wA[:], wB[:], ALU.add))
                    assert count[0] == NR, count[0]
                    dve.wait_ge(s_wT, c + 1)
                    v.tensor_tensor(
                        wbd[:].rearrange("p g b n -> p g b n"),
                        wT[:].rearrange("p (b n) -> p b n", n=SLOT)[:, :, 0:T].unsqueeze(1)
                        .to_broadcast([CG * E, CG, 2, T]),
                        C("grp", CG * E).unsqueeze(2).unsqueeze(3).to_broadcast([CG * E, CG, 2, T]),
                        ALU.mult).then_inc(s_bd, 1)
                    dve.wait_ge(s_we, (c + 1) * E)
                    for n, (f, e) in enumerate(FE):
                        w = FT[f][1]
                        dve.wait_ge(s_si, c * NFE + n + 1)
                        v.tensor_tensor(pg[0:w, n % 2, :], si[0:w, n % 2, :], ps[0:w, 2 * (f % 2) + 1, 0:CT],
                                        ALU.mult).then_inc(s_pg, 1)
                        dve.wait_ge(s_pg, c * NFE + n + 1)
                        if n >= 4:
                            dve.wait_ge(s_ac, sums_done(c, n - 4 + (2 if FE[n - 4][1] == 0 else 0)))
                            dve.wait_ge(s_u2, c * NFE + n - 3)
                        v.tensor_tensor(wt[0:w, n % 4, :], pg[0:w, n % 2, :], we[0:w, e, :],
                                        ALU.mult).then_inc(s_wg, 1)
                    for gg in range(CG):
                        g = c * CG + gg
                        if gg % 2 == 0:
                            dve.wait_ge(s_o, c * 2 + gg // 2 + 1)
                        dve.wait_ge(s_ob, g)
                        v.tensor_tensor(y[:], ps[:, OB + gg // 2, (gg % 2) * D:(gg % 2 + 1) * D], xc[:, gg, :],
                                        ALU.add).then_inc(s_y, 1)
                        dve.wait_ge(s_y, g + 1)
                        v.bn_stats(st[:], y[:]).then_inc(s_bn, 1)
                        dve.wait_ge(s_low, 2)
                        dve.wait_ge(s_bn, g + 1)
                        v.bn_aggr(mv[:], st[:]).then_inc(s_ag, 1)
                        dve.wait_ge(s_ag, g + 1)
                        v.tensor_scalar_add(va[:], mv[:, 1:2], EPS).then_inc(s_va, 1)
                        dve.wait_ge(s_pw, g + 1)
                        if gg >= 2:
                            dve.wait_ge(s_st[gg % 2], (c * 2 + gg // 2) * 32)
                        else:
                            dve.wait_ge(s_st[gg % 2], c * 64)
                        v.tensor_scalar(ob[:, gg % 2, :], y[:], mv[:, 0:1], rs[:, 0:1], ALU.subtract,
                                        ALU.mult).then_inc(s_ob, 1)

                chunk(0)
                with dve.Fori(1, NCH) as c:
                    chunk(c)
def program(nc, a, upto=3):
    with ExitStack() as ctx:
        a["cst"] = ctx.enter_context(nc.sbuf_tensor("cst", [P, CW], F32))
        a["X"] = ctx.enter_context(nc.sbuf_tensor("X", [P, GR, D], F32))
        a["ps"] = ctx.enter_context(nc.psum_tensor("ps", [P, 8, 512], F32))
        with nc.sbuf_tensor("X1T", [P, KD, B * T], F32) as X1T:
            a["X1T"] = X1T
            self_attention(nc, a)
            if upto >= 2:
                cross_attention(nc, a)
        if upto >= 3:
            feed_forward(nc, a)
        else:
            with nc.semaphore("dbg") as s, nc.Block() as block:
                @block.sync
                def _(sp):
                    ov = a["out"].rearrange("(g two) t d -> two t g d", two=2)
                    for par in range(2):
                        sp.dma_start(ov[par], a["X"][SLOT * par:SLOT * par + T, :, :]).then_inc(s, 16)
                    sp.wait_ge(s, 32)


def layouts(i):
    swap = np.arange(D) ^ 1
    wq, wk, wv = i["L0_attn_Wq"], i["L0_attn_Wk"], i["L0_attn_Wv"]
    z = np.zeros((D, DH), wv.dtype)
    t = np.ascontiguousarray

    def wide(m):
        return np.concatenate([m, np.zeros((*m.shape[:-1], FP - F), m.dtype)], -1)

    a2 = np.zeros((FP, E, 32), np.float32)
    a2[0:F, :, 0:R] = i["L0_ffn_a2"].transpose(2, 0, 1)
    b2 = np.zeros((2, 4, 32, D), np.float32)
    b2[:, :, 0:R, :] = i["L0_ffn_b2"].transpose(0, 2, 1).reshape(2, 4, R, D)
    return {
        "consts": constants(),
        "x": i["x"], "xT": t(i["x"].reshape(B * T, D).T),
        "ctx": i["ctx_2048"], "ctxT": t(i["ctx_2048"].transpose(0, 2, 1)),
        "wqT": t(np.stack([wq.T, wq[swap].T], 1)),
        "wkT": t(np.tile(wk, (HB, 1)).T),
        "wvT": t(np.stack([np.concatenate([wv.T, z], 1), np.concatenate([z, wv.T], 1)], 1)),
        "woT": t(i["L0_attn_Wo"].T),
        "gateT": t(i["L0_ffn_gate_w"].T),
        "w13T": wide(np.stack([i["L0_ffn_w1"].T, i["L0_ffn_w3"].T])),
        "a13T": t(np.stack([i["L0_ffn_a1"].reshape(E * R, D).T, i["L0_ffn_a3"].reshape(E * R, D).T])),
        "b13T": wide(np.stack([i["L0_ffn_b1"].transpose(0, 2, 1).reshape(E * R, F),
                            i["L0_ffn_b3"].transpose(0, 2, 1).reshape(E * R, F)])),
        "a2T": a2, "b2T": b2.reshape(2, P, D), "w2T": wide(i["L0_ffn_w2"]).T.copy(),
    }


def kernel(**inputs):
    import concourse.bacc as bacc
    from concourse.bass_utils import run_bass_kernel_spmd

    arrays = {f"in_{n}": a for n, a in layouts({n: np.asarray(v) for n, v in inputs.items()}).items()}
    nc = bacc.Bacc("TRN2", target_bir_lowering=False, num_devices=1)
    a = {n[3:]: nc.dram_tensor(n, v.shape, mybir.dt.from_np(v.dtype), kind="ExternalInput").ap()
         for n, v in arrays.items()}
    a["out"] = nc.dram_tensor("out_0", (B, T, D), F32, kind="ExternalOutput").ap()
    program(nc, a)
    r = run_bass_kernel_spmd(nc, [arrays], core_ids=[0])
    return r.results[0]["out_0"]
```

```python
import numpy as np
import concourse.bass as bass
from concourse import mybir
from contextlib import ExitStack

F32 = mybir.dt.float32
F32R = mybir.dt.float32r
I32 = mybir.dt.int32
ALU = mybir.AluOpType
ACT = mybir.ActivationFunctionType
AX = mybir.AxisListType

B, T, D = 32, 56, 256
H, DH = 16, 16
SK = 1500
F, E, R = 704, 8, 16
EPS = 1e-5
MASKED = -10000.0
NEG = -1e30
P = 128
KD = D // P
HB = H // KD
GR = B // 2
SLOT = 64
NCH = 4
CB = B // NCH
CT = CB * T
CG = CB // 2
KT = 125
NT = SK // KT
UN = 500
NU = SK // UN
TU = UN // KT
NP = H // 2
PR = 2 * T
TAIL = T - 1
NF = -(-F // P)
FP = NF * P
FT = [(f, P) for f in range(0, FP, P)]

CONST = {}
_at = 0
for _name, _width in (("ident", P), ("head", HB), ("head4", HB), ("causal", T), ("tail", TAIL), ("cos", D),
                      ("sin", D), ("sel", 2 * SLOT), ("sign", 1), ("sign_low", 1), ("iota", E), ("expert", E), ("grp", CG),
                      ("own", 2 * 4)):
    CONST[_name] = (_at, _at + _width)
    _at += _width
CW = _at


def constants():
    c = np.zeros((P, CW), np.float32)
    row = np.arange(P)

    def put(name, a):
        lo, hi = CONST[name]
        c[:a.shape[0], lo:hi] = a

    put("ident", np.eye(P))
    head = (row[:, None] // DH == np.arange(HB)[None, :]).astype(np.float32)
    put("head", head)
    put("head4", head * np.float32(DH ** -0.5))
    q = row % SLOT
    put("causal", np.where((np.arange(T)[None, :] > q[:, None]) & (q[:, None] < T), NEG, 0.0))
    qq = np.arange(PR) % T
    put("tail", (np.arange(TAIL)[None, :] >= qq[:, None]).astype(np.float32))
    half = DH // 2
    theta = np.float32(1.0) / np.float32(10000.0) ** (np.arange(0, half, 2, dtype=np.float32) / np.float32(half))
    freq = np.arange(H, dtype=np.float32)[:, None] * theta.astype(np.float32)[None, :]
    d = np.arange(D) % DH
    angle = freq[np.arange(D) // DH, (d % half) // 2]
    put("cos", np.tile(np.cos(angle), (P, 1)))
    put("sin", np.tile(np.sin(angle) * np.where(d % 2 == 0, -1, 1), (P, 1)))
    sel = np.zeros((PR, 2, SLOT), np.float32)
    for par in range(2):
        for s in range(SLOT):
            sel[par * T + (s if s < T else 0), par, s] = 1.0
    put("sel", sel.reshape(PR, 2 * SLOT))
    sign = np.where(row % (2 * R) < R, -1.0, 1.0)
    put("sign", sign[:, None])
    put("sign_low", (sign * (row >= P // 2))[:, None])
    put("iota", np.tile(np.arange(E, dtype=np.float32), (P, 1)))
    ge = np.arange(CG * E)
    put("expert", (ge[:, None] % E == np.arange(E)).astype(np.float32))
    put("grp", (ge[:, None] // E == np.arange(CG)).astype(np.float32))
    put("own", np.tile((row[:, None] % 64 // DH == np.arange(4)).astype(np.float32), (1, 2)))
    return c


def self_attention(nc, a):
    with ExitStack() as ctx:
        def sb(name, shape, dt=F32):
            return ctx.enter_context(nc.sbuf_tensor(name, shape, dt))

        def sem(name):
            return ctx.enter_context(nc.semaphore(name))

        cst, X, X1T = a["cst"], a["X"], a["X1T"]
        ps = a["ps"]

        def C(name, rows=P):
            lo, hi = CONST[name]
            return cst[0:rows, lo:hi]

        xT = sb("xT", [P, KD, B * T])
        wq = sb("wq", [P, KD, 2, D])
        wqr = sb("wq_turned", [P, KD, D])
        wk = sb("wk", [P, KD, P])
        wv = sb("wv", [P, KD, 2, 2 * DH])
        wo = sb("wo", [P, KD, D])
        qT = sb("qT", [P, KD, B * T])
        kT = sb("kT", [P, 1, B * T])
        m1 = sb("wq_cos", [P, KD, D])
        m2 = sb("wq_sin", [P, KD, D])
        qs = sb("qs", [P, 2, KD, 2, SLOT])
        xs = sb("xs", [P, 2, KD, 2, SLOT])
        kbd = sb("kbd", [P, 2, 2, HB, T])
        sm = sb("sm", [P, H, T])
        mx = sb("mx1", [P, H])
        pe_ = sb("p_exp", [P, 2, H, T])
        den = sb("den1", [P, 2, H])
        rden = sb("rden1", [P, 2, H])
        pn = sb("p_norm", [P, 2, H, SLOT])
        vs = sb("vs", [P, 2, 2, 2 * DH])
        pts = sb("pts", [P, NP, P])
        at = sb("at", [P, KD, P])
        y = sb("y1", [P, D])
        st = sb("st1", [P, 6])
        mv = sb("mv1", [P, 2])
        va = sb("va1", [P, 1])
        mh = sb("mh1", [P, 1])
        rs = sb("rs1", [P, 1])
        xn = sb("xn1", [P, D])

        s_c, s_x, s_xt, s_w = sem("c_loaded"), sem("x_loaded"), sem("xT_loaded"), sem("wqk_loaded")
        s_wo = sem("wvo_loaded")
        s_x0, s_z = sem("x_padded"), sem("pads_zero")
        s_prj, s_rot, s_rope, s_cp = sem("projected"), sem("rotated"), sem("turned_weights"), sem("copied")

        with nc.Block() as block:
            @block.sync
            def _(sp):
                sp.dma_start(cst[:], a["consts"]).then_inc(s_c, 16)
                sp.dma_start(wq[:], a["wqT"].rearrange("(k p) v n -> p k v n", p=P)).then_inc(s_w, 16)
                sp.dma_start(wk[:], a["wkT"].rearrange("(k p) n -> p k n", p=P)).then_inc(s_w, 16)
                sp.dma_start(xT[:], a["xT"].rearrange("(k p) n -> p k n", p=P)).then_inc(s_xt, 16)
                sp.dma_start(wv[:], a["wvT"].rearrange("(k p) v n -> p k v n", p=P)).then_inc(s_wo, 16)
                sp.dma_start(wo[:], a["woT"].rearrange("(k p) n -> p k n", p=P)).then_inc(s_wo, 16)
                sp.wait_ge(s_x0, 1)
                xv = a["x"].rearrange("(g two) t d -> two t g d", two=2)
                for par in range(2):
                    sp.dma_start(X[SLOT * par:SLOT * par + T, :, :], xv[par]).then_inc(s_x, 16)
                sp.wait_ge(s_wo, 32)
                sp.wait_ge(s_x, 32)

            @block.tensor
            def _(pe):
                pe.wait_ge(s_xt, 16)
                pe.wait_ge(s_w, 32)
                pe.wait_ge(s_rope, 1)
                for c in range(NCH):
                    for t in range(3):
                        if c >= 2:
                            pe.wait_ge(s_cp, (c - 2) * 3 + t + 1)
                        for k in range(KD):
                            w = wqr[:, k, t * P:(t + 1) * P] if t < 2 else wk[:, k, :]
                            last = nc.tensor.matmul(ps[:, (c % 2) * 3 + t, 0:CT], w, xT[:, k, c * CT:(c + 1) * CT],
                                                    start=(k == 0), stop=(k == KD - 1))
                        last.then_inc(s_prj, 1)

            @block.vector
            def _(dve):
                nc.vector.memset(X[:], 0.0).then_inc(s_x0, 1)
                nc.vector.memset(mh[:], -0.5).then_inc(s_z, 1)
                dve.wait_ge(s_c, 16)
                dve.wait_ge(s_w, 32)
                for v, (dst, tab) in enumerate(((m1, "cos"), (m2, "sin"))):
                    nc.vector.tensor_tensor(dst[:], wq[:, :, v, :], C(tab).unsqueeze(1).to_broadcast([P, KD, D]),
                                            ALU.mult).then_inc(s_rot, 1)
                dve.wait_ge(s_rot, 2)
                nc.vector.tensor_tensor(wqr[:], m1[:], m2[:], ALU.add).then_inc(s_rope, 1)

            @block.scalar
            def _(act):
                for c in range(NCH):
                    for t in range(3):
                        act.wait_ge(s_prj, c * 3 + t + 1)
                        dst = qT[:, t, c * CT:(c + 1) * CT] if t < 2 else kT[:, 0, c * CT:(c + 1) * CT]
                        nc.scalar.activation(dst, ps[:, (c % 2) * 3 + t, 0:CT], ACT.Copy).then_inc(s_cp, 1)

            @block.gpsimd
            def _(pool):
                nc.gpsimd.memset(qs[:], 0.0)
                nc.gpsimd.memset(xs[:], 0.0)
                nc.gpsimd.memset(pn[:], 0.0)
                nc.gpsimd.memset(at[:], 0.0)

        s_st, s_kb = sem("staged"), sem("kbd_ready")
        s_s1, s_v = sem("scores1"), sem("values1")
        s_sm, s_mx, s_sb, s_ex = sem("masked1"), sem("max1"), sem("shifted1"), sem("exp1")
        s_dn, s_rd, s_pn = sem("den1s"), sem("rden1s"), sem("normed1")
        s_vs, s_t1, s_pt = sem("vs_ready"), sem("probs_turned"), sem("pts_ready")
        s_pv, s_at, s_y = sem("attended"), sem("at_ready"), sem("projected_out")
        s_ya, s_bn, s_ag, s_va, s_pw = sem("y1_ready"), sem("bn1"), sem("ag1"), sem("va1s"), sem("rstd1")
        s_xn, s_xst, s_xr, s_x1t = sem("xn1_ready"), sem("x1_stored"), sem("x1_turned"), sem("x1T_ready")

        with nc.Block() as block:
            @block.gpsimd
            def _(pool):
                def stage(i, par):
                    g = i * 2 + par
                    for dst, src in ((qs, qT), (xs, xT)):
                        for k in range(KD):
                            nc.gpsimd.tensor_copy(dst[:, par, k, :, 0:T],
                                                  src[:, k, bass.ds(g * PR, PR)].rearrange("p (b n) -> p b n", n=T)
                                                  ).then_inc(s_st, 1)
                    for b in range(2):
                        nc.gpsimd.tensor_tensor(
                            kbd[:, par, b, :, :],
                            kT[:, 0:1, bass.ds(g * PR + b * T, T)].to_broadcast([P, HB, T]),
                            C("head").unsqueeze(2).to_broadcast([P, HB, T]), ALU.mult).then_inc(s_kb, 1)

                def finish(i, par):
                    g = i * 2 + par
                    pool.wait_ge(s_rd, g + 1)
                    nc.gpsimd.tensor_tensor(pn[:, par, :, 0:T], pe_[:, par, :, :],
                                            rden[:, par, :].unsqueeze(2).to_broadcast([P, H, T]),
                                            ALU.mult).then_inc(s_pn, 1)

                def deviation(i, par):
                    g = i * 2 + par
                    pool.wait_ge(s_va, g + 1)
                    nc.gpsimd.tensor_tensor(rs[:], va[:], mh[:], ALU.pow).then_inc(s_pw, 1)

                stage(0, 0)
                stage(0, 1)
                pool.wait_ge(s_v, 1)
                stage(1, 0)

                def body(i):
                    finish(i, 0)
                    pool.wait_ge(s_v, 2 * i + 2)
                    stage(i + 1, 1)
                    deviation(i, 0)
                    finish(i, 1)
                    pool.wait_ge(s_v, 2 * i + 3)
                    stage(i + 2, 0)
                    deviation(i, 1)

                body(0)
                with pool.Fori(1, GR // 2 - 2) as i:
                    body(i)
                finish(GR // 2 - 2, 0)
                pool.wait_ge(s_v, GR - 2)
                stage(GR // 2 - 1, 1)
                deviation(GR // 2 - 2, 0)
                finish(GR // 2 - 2, 1)
                deviation(GR // 2 - 2, 1)
                for par in range(2):
                    finish(GR // 2 - 1, par)
                    deviation(GR // 2 - 1, par)

            @block.tensor
            def _(pe):
                def scores(i, par):
                    g = i * 2 + par
                    pe.wait_ge(s_st, (g + 1) * 2 * KD)
                    pe.wait_ge(s_kb, (g + 1) * 2)
                    for k in range(KD):
                        for b in range(2):
                            last = nc.tensor.matmul(ps[SLOT * b:SLOT * (b + 1), 2 * par + k, 0:HB * T],
                                                    qs[:, par, k, b, :], kbd[:, par, b, :, :].rearrange("p h n -> p (h n)"),
                                                    start=True, stop=True)
                    last.then_inc(s_s1, 1)
                    pe.wait_ge(s_wo, 32)
                    pe.wait_ge(s_vs, g)
                    for b in range(2):
                        for hp in range(2):
                            for k in range(KD):
                                last = nc.tensor.matmul(
                                    ps[SLOT * hp:SLOT * (hp + 1), 6, 256 + 32 * b:256 + 32 * (b + 1)],
                                    xs[:, par, k, b, :], wv[:, k, hp, :], start=(k == 0), stop=(k == KD - 1),
                                    skip_group_check=True)
                    last.then_inc(s_v, 1)

                def rest(i, par, first=False):
                    g = i * 2 + par
                    pe.wait_ge(s_pn, g + 1)
                    for hp in range(NP):
                        last = nc.tensor.transpose(ps[:, 4 + hp // 4, (hp % 4) * P:(hp % 4 + 1) * P],
                                                   pn[:, par, 2 * hp:2 * hp + 2, :].rearrange("p h n -> p (h n)"),
                                                   C("ident"))
                        if hp % 4 == 3:
                            last.then_inc(s_t1, 1)
                    if not first:
                        turn(g - 1)
                    pe.wait_ge(s_vs, g + 1)
                    pe.wait_ge(s_pt, (g + 1) * 2)
                    for hp in range(NP):
                        for b in range(2):
                            q = 32 * (hp % 4)
                            o = (hp // 4) * P + b * SLOT
                            last = nc.tensor.matmul(ps[q:q + 32, 6, o:o + SLOT], vs[:, par, b, :],
                                                    pts[:, hp, b * SLOT:(b + 1) * SLOT], start=True, stop=True,
                                                    skip_group_check=True)
                    last.then_inc(s_pv, 1)
                    pe.wait_ge(s_at, g + 1)
                    pe.wait_ge(s_x1t, g * KD)
                    for k in range(KD):
                        last = nc.tensor.matmul(ps[:, 7, 0:D], at[:, k, :], wo[:, k, :], start=(k == 0),
                                                stop=(k == KD - 1))
                    last.then_inc(s_y, 1)

                def turn(g):
                    pe.wait_ge(s_xn, g + 1)
                    for k in range(KD):
                        last = nc.tensor.transpose(ps[:, 7, D + k * P:D + (k + 1) * P], xn[:, k * P:(k + 1) * P],
                                                   C("ident"))
                    last.then_inc(s_xr, 1)

                scores(0, 0)

                def body(i, first):
                    scores(i, 1)
                    rest(i, 0, first)
                    scores(i + 1, 0)
                    rest(i, 1)

                body(0, True)
                with pe.Fori(1, GR // 2 - 1) as i:
                    body(i, False)
                scores(GR // 2 - 1, 1)
                rest(GR // 2 - 1, 0)
                rest(GR // 2 - 1, 1)
                turn(GR - 1)

            @block.vector
            def _(dve):
                def soft(i, par):
                    g = i * 2 + par
                    dve.wait_ge(s_s1, g + 1)
                    dve.wait_ge(s_ex, g)
                    for k in range(KD):
                        nc.vector.scalar_tensor_tensor(
                            out=sm[:, k * HB:(k + 1) * HB, :],
                            in0=ps[:, 2 * par + k, 0:HB * T].rearrange("p (h n) -> p h n", n=T), scalar=DH ** -0.5,
                            in1=C("causal").unsqueeze(1).to_broadcast([P, HB, T]), op0=ALU.mult,
                            op1=ALU.add).then_inc(s_sm, 1)
                    dve.wait_ge(s_sm, (g + 1) * 2)
                    nc.vector.reduce_max(mx[:], sm[:], AX.X).then_inc(s_mx, 1)
                    dve.wait_ge(s_mx, g + 1)
                    nc.vector.tensor_tensor(sm[:], sm[:], mx[:].unsqueeze(2).to_broadcast([P, H, T]),
                                            ALU.subtract).then_inc(s_sb, 1)
                    dve.wait_ge(s_ex, g + 1)
                    nc.vector.reduce_sum(den[:, par, :], pe_[:, par, :, :], AX.X).then_inc(s_dn, 1)
                    dve.wait_ge(s_dn, g + 1)
                    nc.vector.reciprocal(rden[:, par, :], den[:, par, :]).then_inc(s_rd, 1)

                def norm(i, par):
                    g = i * 2 + par
                    dve.wait_ge(s_y, g + 1)
                    nc.vector.tensor_tensor(y[:], ps[:, 7, 0:D], X[:, bass.ds(g, 1), :].rearrange("p a d -> p (a d)"),
                                            ALU.add).then_inc(s_ya, 1)
                    dve.wait_ge(s_ya, g + 1)
                    nc.vector.bn_stats(st[:], y[:]).then_inc(s_bn, 1)
                    dve.wait_ge(s_z, 1)
                    dve.wait_ge(s_bn, g + 1)
                    nc.vector.bn_aggr(mv[:], st[:]).then_inc(s_ag, 1)
                    dve.wait_ge(s_ag, g + 1)
                    nc.vector.tensor_scalar_add(va[:], mv[:, 1:2], EPS).then_inc(s_va, 1)
                    dve.wait_ge(s_pw, g + 1)
                    dve.wait_ge(s_xst, g)
                    dve.wait_ge(s_xr, g)
                    nc.vector.tensor_scalar(xn[:], y[:], mv[:, 0:1], rs[:, 0:1], ALU.subtract,
                                            ALU.mult).then_inc(s_xn, 1)

                soft(0, 0)
                def body(i):
                    soft(i, 1)
                    norm(i, 0)
                    soft(i + 1, 0)
                    norm(i, 1)

                body(0)
                with dve.Fori(1, GR // 2 - 1) as i:
                    body(i)
                soft(GR // 2 - 1, 1)
                norm(GR // 2 - 1, 0)
                norm(GR // 2 - 1, 1)

            @block.scalar
            def _(act):
                def soft(i, par):
                    g = i * 2 + par
                    act.wait_ge(s_sb, g + 1)
                    nc.scalar.activation(pe_[:, par, :, :], sm[:], ACT.Exp).then_inc(s_ex, 1)
                    act.wait_ge(s_v, g + 1)
                    nc.scalar.activation(vs[:, par, :, :].rearrange("p b n -> p (b n)"), ps[:, 6, 256:320],
                                         ACT.Copy).then_inc(s_vs, 1)

                def rest(i, par, first=False):
                    g = i * 2 + par
                    for j in range(2):
                        act.wait_ge(s_t1, g * 2 + j + 1)
                        if j == 0:
                            act.wait_ge(s_pv, g)
                        nc.scalar.activation(pts[:, 4 * j:4 * j + 4, :].rearrange("p a n -> p (a n)"), ps[:, 4 + j, :],
                                             ACT.Copy).then_inc(s_pt, 1)
                    if not first:
                        store(g - 1)
                    act.wait_ge(s_pv, g + 1)
                    act.wait_ge(s_y, g)
                    nc.scalar.activation(at[:].rearrange("p a n -> p (a n)"), ps[:, 6, 0:256],
                                         ACT.Copy).then_inc(s_at, 1)

                def store(g):
                    act.wait_ge(s_xn, g + 1)
                    nc.scalar.activation(X[:, bass.ds(g, 1), :].rearrange("p a d -> p (a d)"), xn[:],
                                         ACT.Copy).then_inc(s_xst, 1)
                    act.wait_ge(s_xr, g + 1)
                    for k in range(KD):
                        last = nc.scalar.activation(
                            X1T[:, k, bass.ds(g * PR, PR)].rearrange("p (b n) -> p b n", n=T),
                            ps[:, 7, D + k * P:D + (k + 1) * P].rearrange("p (b n) -> p b n", n=SLOT)[:, :, 0:T],
                            ACT.Copy)
                        last.then_inc(s_x1t, 1)

                soft(0, 0)

                def body(i, first):
                    rest(i, 0, first)
                    soft(i, 1)
                    rest(i, 1)
                    soft(i + 1, 0)

                body(0, True)
                with act.Fori(1, GR // 2 - 1) as i:
                    body(i, False)
                rest(GR // 2 - 1, 0)
                soft(GR // 2 - 1, 1)
                rest(GR // 2 - 1, 1)
                store(GR - 1)


COPIER = (("D", "A", "D"), ("D", "A", "D"))
STEPS = 2 * NP


def copies(engine, step, unit):
    order = [COPIER[j % 2][u] for j in range(STEPS) for u in range(NU)]
    return order[:step * NU + unit + 1].count(engine)


def cross_attention(nc, a):
    with ExitStack() as ctx:
        def sb(name, shape, dt=F32):
            return ctx.enter_context(nc.sbuf_tensor(name, shape, dt))

        def sem(name):
            return ctx.enter_context(nc.semaphore(name))

        cst, X, X1T, ps = a["cst"], a["X"], a["X1T"], a["ps"]

        def C(name, rows=P):
            lo, hi = CONST[name]
            return cst[0:rows, lo:hi]

        cT = sb("ctxT", [P, KD, SK])
        kh = sb("keys_high", [P, KD, SK], F32R)
        kq = sb("keys_split", [P, 2, 4, SK], F32R)
        cN = sb("ctxN", [KT, 2, NT, D])
        qbd = sb("qbd", [P, KD, HB, T])
        qh = sb("queries_high", [P, KD, HB, T], F32R)
        qq = sb("queries_split", [P, 2, 2, 4, 4, T], F32R)
        pr = sb("probs", [PR, 2, SK])
        pt = sb("probsT", [KT, 2, NT, 4, PR])
        mx = sb("mx2", [PR, 2, NU + 1])
        nmx = sb("nmx2", [PR, 2])
        fill = sb("fill", [PR, TAIL])
        sums = sb("sums2", [PR, 2, NP, NU])
        ssum = sb("ssum2", [PR, 2, NP])
        om = sb("om", [P, KD, 4, T])
        aT = sb("aT", [P, KD, 2, SLOT])
        rden = sb("rden2", [P, H])
        y = sb("y2", [P, D])
        st = sb("st2", [P, 6])
        mv = sb("mv2", [P, 2])
        va = sb("va2", [P, 1])
        mh = sb("mh2", [P, 1])
        rs = sb("rs2", [P, 1])
        zero = sb("zero", [P, 1])

        s_cT = [sem("cT_loaded0"), sem("cT_loaded1")]
        s_kh, s_kl = sem("keys_high_ready"), sem("keys_low_ready")
        s_kd = [sem("keys_placed0"), sem("keys_placed1")]
        s_qd = [sem("queries_placed0"), sem("queries_placed1")]
        s_cN = [sem("cN_loaded0"), sem("cN_loaded1")]
        s_q, s_qh, s_ql = sem("qbd_ready"), sem("queries_high_ready"), sem("queries_low_ready")
        s_s = sem("unit_scored")
        s_tail, s_mx, s_nmx = sem("tail_masked"), sem("unit_max"), sem("pair_max")
        s_ex, s_t = sem("unit_exp"), sem("unit_turned")
        s_cp = {"A": sem("unit_copied_act"), "D": sem("unit_copied_dve")}
        s_pv, s_om, s_aT, s_ss = sem("half_attended"), sem("om_ready"), sem("aT_ready"), sem("ssum_ready")
        s_rs, s_at = sem("sums_moved"), sem("attended_turned")
        s_rd, s_y0, s_y, s_bn, s_ag = sem("rden2_ready"), sem("y0_ready"), sem("y2_ready"), sem("bn2"), sem("ag2")
        s_va, s_pw, s_x2 = sem("va2_ready"), sem("rstd2_ready"), sem("x2_ready")
        s_k, s_z = sem("fill_ready"), sem("zero_ready")
        per = {e: copies(e, STEPS - 1, NU - 1) for e in "AD"}
        FINISH = 6
        TB, O = 6, 7

        with nc.Block() as block:
            @block.sync
            def _(sp):
                def load(n, k):
                    sp.dma_start(cT[:, k, :], a["ctxT"][bass.ds(n, 1), k * P:(k + 1) * P, :]
                                 .rearrange("a p s -> p (a s)")).then_inc(s_cT[k], 16)

                def load_natural(n, par):
                    sp.dma_start(cN[:, par, :, :], a["ctx"][bass.ds(n, 1), :, :]
                                 .rearrange("a (t p) d -> p (a t) d", p=KT)).then_inc(s_cN[par], 16)

                def place_queries(n, par, scored):
                    sp.wait_ge(s_ql, n + 1)
                    if scored is not None:
                        sp.wait_ge(s_s, scored)
                    for h in range(2):
                        for to in range(2):
                            rows, other = slice(64 * h, 64 * h + 64), slice(64 * to, 64 * to + 64)
                            sp.dma_start(qq[other, par, 0, h:4:2, :, :].bitcast(F32)
                                         .rearrange("p k h n -> p k (h n)"),
                                         qh[rows, :, 4 * h:4 * h + 4, :].bitcast(F32)
                                         .rearrange("p k h n -> p k (h n)")).then_inc(s_qd[par], 16)
                            sp.dma_start(qq[other, par, 1, h:4:2, :, :].bitcast(F32)
                                         .rearrange("p k h n -> p k (h n)"),
                                         qbd[rows, :, 4 * h:4 * h + 4, :]
                                         .rearrange("p k h n -> p k (h n)")).then_inc(s_qd[par], 16)

                def place_keys(n, par, last):
                    for k in range(KD):
                        sp.wait_ge(s_kl, n * KD + k + 1)
                        for h in range(2):
                            rows, other = slice(64 * h, 64 * h + 64), slice(64 * (1 - h), 64 * (1 - h) + 64)
                            sp.dma_start(kq[rows, par, 2 * k + h, :].bitcast(F32),
                                         kh[rows, k, :].bitcast(F32)).then_inc(s_kd[k], 16)
                            sp.dma_start(kq[other, par, 2 * k + h, :].bitcast(F32),
                                         cT[rows, k, :]).then_inc(s_kd[k], 16)
                        if not last:
                            sp.wait_ge(s_kd[k], (n + 1) * 64)
                            load(n + 1, k)

                def group(i, first, last):
                    for par in range(2):
                        n = i * 2 + par
                        place_queries(n, par, None if first else (n - 1) * NP * NU)
                        if not (first and par == 0):
                            if not (first or (par == 0 and isinstance(i, int) and i == 1)):
                                sp.wait_ge(s_pv, i * 4 - 4 + 2 * par)
                            load_natural(n - 1, 1 - par)
                        place_keys(n, par, last and par == 1)

                for k in range(KD):
                    load(0, k)
                group(0, True, False)
                group(1, False, False)
                with sp.Fori(2, GR - 1) as i:
                    group(i, False, False)
                group(GR - 1, False, True)
                sp.wait_ge(s_pv, (B - 2) * 2)
                load_natural(B - 1, 1)

            @block.gpsimd
            def _(pool):
                nc.gpsimd.memset(mh[:], -0.5)
                nc.gpsimd.memset(zero[:], 0.0).then_inc(s_z, 1)
                pool.wait_ge(s_z, 1)

                def queries(n, placed):
                    if placed is not None:
                        pool.wait_ge(*placed)
                    for k in range(KD):
                        nc.gpsimd.tensor_tensor(
                            qbd[:, k, :, :], X1T[:, k:k + 1, bass.ds(n * T, T)].to_broadcast([P, HB, T]),
                            C("head4").unsqueeze(2).to_broadcast([P, HB, T]), ALU.mult).then_inc(s_q, 1)
                    pool.wait_ge(s_q, (n + 1) * KD)
                    nc.gpsimd.tensor_tensor(qh[:].rearrange("p k h n -> p (k h n)"),
                                            qbd[:].rearrange("p k h n -> p (k h n)"),
                                            zero[:].to_broadcast([P, KD * HB * T]), ALU.add).then_inc(s_qh, 1)
                    pool.wait_ge(s_qh, n + 1)
                    nc.gpsimd.tensor_tensor(qbd[:], qbd[:], qh[:].bitcast(F32), ALU.subtract).then_inc(s_ql, 1)

                def keys(n):
                    for k in range(KD):
                        pool.wait_ge(s_cT[k], (n + 1) * 16)
                        nc.gpsimd.tensor_tensor(kh[:, k, :], cT[:, k, :], zero[:].to_broadcast([P, SK]),
                                                ALU.add).then_inc(s_kh, 1)
                        pool.wait_ge(s_kh, n * KD + k + 1)
                        nc.gpsimd.tensor_tensor(cT[:, k, :], cT[:, k, :], kh[:, k, :].bitcast(F32),
                                                ALU.subtract).then_inc(s_kl, 1)

                def deviation(i):
                    pool.wait_ge(s_va, i + 1)
                    nc.gpsimd.tensor_tensor(rs[:], va[:], mh[:], ALU.pow).then_inc(s_pw, 1)

                queries(0, None)
                keys(0)
                queries(1, (s_qd[0], 128))
                keys(1)

                def group(i, first):
                    queries(i * 2, (s_qd[1], i * 128))
                    keys(i * 2)
                    if not first:
                        deviation(i - 2)
                    queries(i * 2 + 1, (s_qd[0], (i + 1) * 128))
                    keys(i * 2 + 1)

                group(1, True)
                with pool.Fori(2, GR) as i:
                    group(i, False)
                deviation(GR - 2)
                deviation(GR - 1)

            @block.tensor
            def _(pe):
                def scores(i, j, u):
                    if j == STEPS:
                        i, j = i + 1, 0
                    par, p = j // NP, j % NP
                    if u == 0 and p == 0:
                        pe.wait_ge(s_qd[par], (i + 1) * 128)
                    if u == 0 and p % (NP // KD) == 0:
                        pe.wait_ge(s_kd[p // (NP // KD)], (i * 2 + par + 1) * 64)
                    n = j * NU + u - 5
                    if not (isinstance(i, int) and i * STEPS * NU + n < 1):
                        pe.wait_ge(s_ex, i * (STEPS * NU) + n)
                    for part in range(2):
                        last = nc.tensor.matmul(
                            ps[0:PR, (j % 2) * NU + u, 0:UN],
                            qq[:, par, part, p // 2, 2 * (p % 2):2 * (p % 2) + 2, :].rearrange("p h n -> p (h n)"),
                            kq[:, par, p // 2, u * UN:(u + 1) * UN], start=(part == 0), stop=(part == 1))
                    last.then_inc(s_s, 1)

                def turn(i, j, u):
                    pe.wait_ge(s_ex, i * (STEPS * NU) + j * NU + u + 1)
                    n = j * NU + u - 1
                    if n >= 0:
                        e = COPIER[(n // NU) % 2][n % NU]
                        pe.wait_ge(s_cp[e], i * per[e] + copies(e, n // NU, n % NU))
                    elif not (isinstance(i, int) and i == 0):
                        e = COPIER[1][NU - 1]
                        pe.wait_ge(s_cp[e], i * per[e])
                    for t in range(TU):
                        last = nc.tensor.transpose(ps[0:KT, TB, t * PR:(t + 1) * PR],
                                                   pr[:, j % 2, u * UN + t * KT:u * UN + (t + 1) * KT],
                                                   cst[0:PR, 0:PR])
                    last.then_inc(s_t, 1)

                def values(i, half, piece):
                    if half < 0:
                        i, half = i - 1, half + 4
                    par, g2 = half // 2, half % 2
                    if piece == 0:
                        if g2 == 0:
                            pe.wait_ge(s_cN[par], (i + 1) * 16)
                            pe.wait_ge(s_om, i * 2 + par)
                        for e in "AD":
                            pe.wait_ge(s_cp[e], i * per[e] + copies(e, 4 * half + 3, NU - 1))
                    for qp in range(2):
                        c = (2 * g2 + qp) * 64
                        last = nc.tensor.matmul(ps[64 * qp:64 * (qp + 1), O, g2 * 2 * PR:(g2 + 1) * 2 * PR],
                                                cN[:, par, piece, c:c + 64],
                                                pt[:, half % 2, piece, 2 * qp:2 * qp + 2, :]
                                                .rearrange("p a n -> p (a n)"),
                                                start=(piece == 0), stop=(piece == NT - 1), skip_group_check=True)
                    if piece == NT - 1:
                        last.then_inc(s_pv, 1)

                def finish(i):
                    pe.wait_ge(s_ss, i * 2 + 2)
                    pe.wait_ge(s_aT, i * 2 + 2)
                    for par in range(2):
                        for hp in range(2):
                            nc.tensor.matmul(ps[SLOT * par:SLOT * (par + 1), TB, D + hp * NP:D + (hp + 1) * NP],
                                             C("sel", PR)[:, hp * SLOT:(hp + 1) * SLOT], ssum[:, par, :],
                                             start=True, stop=True, skip_group_check=True)
                    for k in range(KD):
                        last = nc.tensor.transpose(ps[:, TB, k * P:(k + 1) * P],
                                                   aT[:, k, :, :].rearrange("p b n -> p (b n)"), C("ident"))
                    last.then_inc(s_at, 1)

                def body(i, first, last_body):
                    for j in range(STEPS):
                        ahead = not (last_body and j == STEPS - 1)
                        behind = not (first and j < 4)

                        def piece(n):
                            if behind:
                                values(i, j // 4 - 1, (j % 4) * NU + n)

                        if ahead:
                            scores(i, j + 1, 0)
                        if j == FINISH and not first:
                            e = COPIER[(FINISH - 1) % 2][NU - 1]
                            pe.wait_ge(s_cp[e], i * per[e] + copies(e, FINISH - 1, NU - 1))
                            finish(i - 1)
                            scores(i, j + 1, 1)
                            scores(i, j + 1, 2)
                            pe.wait_ge(s_y0, i)
                            turn(i, j, 0)
                        else:
                            turn(i, j, 0)
                            if ahead:
                                scores(i, j + 1, 1)
                                scores(i, j + 1, 2)
                        turn(i, j, 1)
                        piece(0)
                        piece(1)
                        turn(i, j, 2)
                        piece(2)

                for u in range(NU):
                    scores(0, 0, u)
                body(0, True, False)
                with pe.Fori(1, GR - 1) as i:
                    body(i, False, False)
                body(GR - 1, False, True)
                for piece in range(NT):
                    values(GR, -1, piece)
                finish(GR - 1)

            def copy_unit(i, j, u, eng, emit, name):
                eng.wait_ge(s_t, i * (STEPS * NU) + j * NU + u + 1)
                half = (j // 4) % 2
                emit(pt[:, half, u * TU:(u + 1) * TU, j % 4, :],
                     ps[0:KT, TB, 0:TU * PR].rearrange("p (t n) -> p t n", n=PR)
                     ).then_inc(s_cp[name], 1)

            @block.vector
            def _(dve):
                def maximum(i, j, u):
                    if j == STEPS:
                        i, j = i + 1, 0
                    n = i * STEPS + j
                    bank = (j % 2) * NU + u
                    dve.wait_ge(s_s, n * NU + u + 1)
                    free = UN if u < NU - 1 else UN - TAIL
                    nc.vector.reduce_max(mx[:, j % 2, u:u + 1], ps[0:PR, bank, 0:free], AX.X).then_inc(s_mx, 1)
                    if u == NU - 1:
                        nc.vector.copy_predicated(ps[0:PR, bank, UN - TAIL:UN], C("tail", PR).bitcast(I32),
                                                  fill[:]).then_inc(s_tail, 1)
                        dve.wait_ge(s_tail, n + 1)
                        nc.vector.reduce_max(mx[:, j % 2, NU:NU + 1], ps[0:PR, bank, UN - TAIL:UN],
                                             AX.X).then_inc(s_mx, 1)
                        dve.wait_ge(s_mx, (n + 1) * (NU + 1))
                        nc.vector.tensor_reduce(nmx[:, j % 2:j % 2 + 1], mx[:, j % 2, :], AX.X, ALU.max,
                                                negate=True).then_inc(s_nmx, 1)

                def evacuate(i, par):
                    n = i * 2 + par
                    dve.wait_ge(s_pv, (n + 1) * 2)
                    nc.vector.tensor_tensor(om[:].rearrange("p a h n -> p (a h) n"),
                                            ps[:, O, 0:KD * 4 * T].rearrange("p (a n) -> p a n", n=T),
                                            cst_own.unsqueeze(2).to_broadcast([P, KD * 4, T]),
                                            ALU.mult).then_inc(s_om, 1)

                def gather(i, par):
                    n = i * 2 + par
                    dve.wait_ge(s_om, n + 1)
                    if par == 0 and not (isinstance(i, int) and i == 0):
                        dve.wait_ge(s_at, i)
                    nc.vector.reduce_sum(aT[:, :, par, 0:T], om[:].rearrange("p a h n -> p a n h"),
                                         AX.X).then_inc(s_aT, 1)
                    dve.wait_ge(s_ex, (n + 1) * NP * NU)
                    nc.vector.reduce_sum(ssum[:, par, :], sums[:, par, :, :], AX.X).then_inc(s_ss, 1)

                def norm(i):
                    dve.wait_ge(s_at, i + 1)
                    nc.vector.reciprocal(rden[:].rearrange("p (a b) -> p b a", b=2),
                                         ps[:, TB, D:D + H].rearrange("p (b a) -> p b a", b=2)).then_inc(s_rd, 1)
                    dve.wait_ge(s_rd, i + 1)
                    nc.vector.tensor_tensor(y[:].rearrange("p (h d) -> p h d", d=DH),
                                            ps[:, TB, 0:D].rearrange("p (h d) -> p h d", d=DH),
                                            rden[:].unsqueeze(2).to_broadcast([P, H, DH]), ALU.mult).then_inc(s_y0, 1)

                def norm_stats(i):
                    dve.wait_ge(s_y0, i + 1)
                    nc.vector.tensor_tensor(y[:], y[:], X[:, bass.ds(i, 1), :].rearrange("p a d -> p (a d)"),
                                            ALU.add).then_inc(s_y, 1)
                    dve.wait_ge(s_y, i + 1)
                    nc.vector.bn_stats(st[:], y[:]).then_inc(s_bn, 1)
                    dve.wait_ge(s_k, 2)
                    dve.wait_ge(s_bn, i + 1)
                    nc.vector.bn_aggr(mv[:], st[:]).then_inc(s_ag, 1)
                    dve.wait_ge(s_ag, i + 1)
                    nc.vector.tensor_scalar_add(va[:], mv[:, 1:2], EPS).then_inc(s_va, 1)

                def norm_apply(i):
                    dve.wait_ge(s_pw, i + 1)
                    nc.vector.tensor_scalar(X[:, bass.ds(i, 1), :].rearrange("p a d -> p (a d)"), y[:], mv[:, 0:1],
                                            rs[:, 0:1], ALU.subtract, ALU.mult).then_inc(s_x2, 1)

                cst_own = cst[:, CONST["own"][0]:CONST["own"][1]]
                nc.vector.memset(fill[:], MASKED).then_inc(s_k, 1)
                nc.vector.memset(aT[:], 0.0).then_inc(s_k, 1)
                dve.wait_ge(s_k, 2)

                def body(i, first, last_body):
                    for j in range(STEPS):
                        half_done = (i - 1, 1) if j == 4 and not first else (i, 0) if j == 12 else None
                        ahead = not (last_body and j == STEPS - 1)
                        for kind, u in (("max", 0), ("copy", 0), ("max", 1), ("max", 2), ("copy", 1), ("copy", 2)):
                            if kind == "max" and ahead:
                                maximum(i, j + 1, u)
                                if u == 0 and j == FINISH and not first:
                                    norm(i - 1)
                            if kind == "copy" and COPIER[j % 2][u] == "D":
                                copy_unit(i, j, u, dve, nc.vector.tensor_copy, "D")
                                if u == 0 and half_done:
                                    evacuate(*half_done)
                        if half_done:
                            gather(*half_done)
                        if j == FINISH and not first:
                            norm_stats(i - 1)
                        if j == 11 and not first:
                            norm_apply(i - 1)

                for u in range(NU):
                    maximum(0, 0, u)
                body(0, True, False)
                with dve.Fori(1, GR - 1) as i:
                    body(i, False, False)
                body(GR - 1, False, True)
                evacuate(GR - 1, 1)
                gather(GR - 1, 1)
                norm(GR - 1)
                norm_stats(GR - 1)
                norm_apply(GR - 1)

            @block.scalar
            def _(act):
                def emit(dst, src):
                    return nc.scalar.activation(dst, src, ACT.Copy)

                def exponentials(i, j):
                    if j == STEPS:
                        i, j = i + 1, 0
                    n = i * STEPS + j
                    act.wait_ge(s_nmx, n + 1)
                    if not (isinstance(i, int) and n < 2):
                        act.wait_ge(s_t, (n - 1) * NU)
                    for u in range(NU):
                        nc.scalar.activation(pr[:, j % 2, u * UN:(u + 1) * UN], ps[0:PR, (j % 2) * NU + u, 0:UN],
                                             ACT.Exp, bias=nmx[:, j % 2:j % 2 + 1],
                                             accum_out=sums[:, j // NP, j % NP, u:u + 1]).then_inc(s_ex, 1)

                def body(i, last_body):
                    for j in range(STEPS):
                        for u in range(NU):
                            if COPIER[j % 2][u] == "A":
                                copy_unit(i, j, u, act, emit, "A")
                        if not (last_body and j == STEPS - 1):
                            exponentials(i, j + 1)

                exponentials(0, 0)
                body(0, False)
                with act.Fori(1, GR - 1) as i:
                    body(i, False)
                body(GR - 1, True)


def feed_forward(nc, a):
    RAW = 2
    RING = 8
    assert (NF - 2) * CT >= 2 * FP and 3 * D >= FP
    with ExitStack() as ctx:
        def sb(name, shape, dt=F32):
            return ctx.enter_context(nc.sbuf_tensor(name, shape, dt))

        def sem(name):
            return ctx.enter_context(nc.semaphore(name))

        cst, X, ps = a["cst"], a["X"], a["ps"]

        def C(name, rows=P):
            lo, hi = CONST[name]
            return cst[0:rows, lo:hi]

        w13 = sb("w13", [P, 2, KD, FP])
        a13 = sb("a13", [P, 2, KD, E * R])
        step13 = sb("step13", [P, 2, E, FP], F32R)
        raw = sb("step_raw", [P, 2, FP])
        stack = sb("stack", [P, E, 2, P], F32R)
        a2 = sb("a2", [P, NF, E, 32])
        b2 = sb("b2", [P, 2, D])
        w2 = sb("w2", [P, NF, D])
        gate = sb("gate", [P, KD, E])
        xc = sb("xc", [P, CG, D])
        xT = sb("x2T", [P, KD, CG, 2, SLOT])
        lg = sb("logits", [P, CG, E])
        l2 = sb("logits2", [P, CG, E])
        eq = sb("eq", [P, CG, E])
        cand = sb("cand", [P, CG, E])
        oh = [sb(f"first{n}", [P, CG, E]) for n in range(2)]
        top = [sb(f"top{n}", [P, CG]) for n in range(2)]
        idx = sb("idx", [P, CG])
        dif = sb("dif", [P, CG])
        tt = sb("tt", [P, CG])
        t1 = sb("t1", [P, CG])
        r1 = sb("r1", [P, CG])
        r2 = sb("r2", [P, CG])
        wA = sb("wA", [P, CG, E])
        wB = sb("wB", [P, CG, E])
        wr = sb("wr", [P, CG, E])
        wT = sb("wT", [CG * E, P])
        wbd = sb("wbd", [P, CG, 2, T])
        we = sb("we", [P, E, CT])
        uh = sb("u_high", [P, 2, CT], F32R)
        ul = sb("u_low", [P, 2, CT], F32R)
        um = sb("u_stacked", [P, 2, E, CT], F32R)
        si = sb("silu", [P, 2, CT])
        pg = sb("gated", [P, 3, CT])
        wt = sb("weighted", [P, RING, CT])
        acc = sb("acc", [P, NF, CT])
        u2 = raw[:, :, 0:CT]
        raws = [raw[:], acc[:].rearrange("p f n -> p (f n)")[:, 2 * CT:2 * CT + 2 * FP]
                .rearrange("p (v n) -> p v n", v=2)]
        ends = sb("ends", [P, 3, D], F32R)
        high = ends[:].rearrange("p a d -> p (a d)")
        y = ends[:, 0, :].bitcast(F32)
        ob = ends[:, 1:3, :].bitcast(F32)
        st = sb("st3", [P, 6])
        mv = sb("mv3", [P, 2])
        va = sb("va3", [P, 1])
        mh = sb("mh3", [P, 1])
        rs = sb("rs3", [P, 1])

        s_w0, s_w, s_low = sem("first_weights_loaded"), sem("weights_loaded"), sem("low_ready")
        s_bw = [sem(f"factors_loaded{n}") for n in range(RAW)]
        s_sk = sem("stack_ready")
        s_hi, s_stp = sem("step_high_ready"), sem("steps_ready")
        s_xc, s_xr, s_xT = sem("xc_ready"), sem("x2_turned"), sem("x2T_ready")
        s_lp, s_lg, s_r, s_e = sem("logits_done"), sem("logits_out"), sem("router"), sem("router_exp")
        s_wt, s_wT, s_bd = sem("weights_turned"), sem("wT_ready"), sem("wbd_ready")
        s_wp, s_we = sem("we_done"), sem("we_ready")
        s_up, s_uh, s_ul = sem("u_done"), sem("u_high_ready"), sem("u_low_ready")
        s_sp, s_um = sem("u_picked"), sem("u_stacked_ready")
        s_h, s_si, s_pg, s_wg, s_ac, s_u2 = (sem("hidden"), sem("silu_ready"), sem("gated_ready"),
                                             sem("weighted_ready"), sem("acc_ready"), sem("u2_done"))
        s_u2s = sem("u2_out")
        s_o, s_y, s_bn, s_ag, s_va, s_pw, s_ob = (sem("out_done"), sem("y3_ready"), sem("bn3"), sem("ag3"),
                                                  sem("va3_ready"), sem("rstd3_ready"), sem("ob_ready"))
        s_st = [sem("stored0"), sem("stored1")]
        NR = 20
        FE = [(f, e) for f0 in range(0, NF, 2) for e in range(E) for f in (f0, f0 + 1)]
        NFE = len(FE)
        LAG = 2
        NDN = NFE // 4
        U2B, OB = 4, 6
        EARLY = (2, 4)


        TURN = NFE - 15
        LOGITS = {TURN + 1: (0, 1), TURN + 2: (2, 3)}
        UP = {TURN + 3 + n: n for n in range(4)}
        SPLIT = TURN + 7
        PICK = {TURN + 8 + n: (n,) for n in range(5)} | {NFE - 2: (5, 6), NFE - 1: (7,)}

        def hb(f):
            return (0, 2, OB)[f % 3]

        def sums_done(c, n):
            return c * NF * (E - 1) + sum(e > 0 for _, e in FE[:n + 1])

        with nc.Block() as block:
            @block.sync
            def _(sp):
                for dst, src in (
                        (gate[:], a["gateT"].rearrange("(k p) n -> p k n", p=P)),
                        (a13[:], a["a13T"].rearrange("v (k p) n -> p v k n", p=P)),
                        (acc[:].rearrange("p f n -> p (f n)")[:, 0:E * 2 * P],
                         a["stack"].rearrange("p e v n -> p (e v n)"))):
                    sp.dma_start(dst, src).then_inc(s_w0, 16)
                sp.dma_start(w13[:], a["w13T"].rearrange("v (k p) n -> p v k n", p=P)).then_inc(s_w, 16)
                for e in range(RAW):
                    if e == 1:
                        sp.wait_ge(s_sk, 1)
                    sp.dma_start(raws[e], a["b13T"][:, :, e, :]).then_inc(s_bw[e], 16)
                for dst, src in (
                        (a2[:], a["a2T"].rearrange("(k p) e n -> p k e n", p=P)),
                        (b2[:], a["b2T"].rearrange("b p n -> p b n")),
                        (w2[:], a["w2T"].rearrange("(k p) n -> p k n", p=P))):
                    sp.dma_start(dst, src).then_inc(s_w, 16)
                for e in range(RAW, E):
                    sp.wait_ge(s_stp, 2 * (e - RAW + 1))
                    sp.dma_start(raws[e % RAW], a["b13T"][:, :, e, :]).then_inc(s_bw[e % RAW], 16)
                ov = a["out"].rearrange("(g two) t d -> two t g d", two=2)
                def chunk(c):
                    for gg in range(CG):
                        sp.wait_ge(s_ob, c * CG + gg + 1)
                        for par in range(2):
                            sp.dma_start(ov[par, :, bass.ds(c * CG + gg, 1), :].rearrange("t a d -> t (a d)"),
                                         ob[SLOT * par:SLOT * par + T, gg % 2, :]).then_inc(s_st[gg % 2], 16)

                chunk(0)
                with sp.Fori(1, NCH) as c:
                    chunk(c)
                for n in range(2):
                    sp.wait_ge(s_st[n], GR * 16)

            @block.gpsimd
            def _(pool):
                pool.wait_ge(s_low, 3)
                def copy_rows(c):
                    nc.gpsimd.tensor_copy(xc[:], X[:, bass.ds(c * CG, CG), :]).then_inc(s_xc, 1)

                def chunk(c, last_chunk):
                    for n, (f, e) in enumerate(FE):
                        if n == NFE // 3 and not last_chunk:
                            pool.wait_ge(s_xr, c + 1)
                            copy_rows(c + 1)
                        w = FT[f][1]
                        pool.wait_ge(s_wg, c * NFE + n + 1)
                        if e == 1:
                            nc.gpsimd.tensor_tensor(acc[0:w, f, :], wt[0:w, (n - 2) % RING, :], wt[0:w, n % RING, :],
                                                    ALU.add).then_inc(s_ac, 1)
                        elif e > 1:
                            pool.wait_ge(s_ac, sums_done(c, n - 2))
                            nc.gpsimd.tensor_tensor(acc[0:w, f, :], acc[0:w, f, :], wt[0:w, n % RING, :],
                                                    ALU.add).then_inc(s_ac, 1)
                    for gg in range(CG):
                        pool.wait_ge(s_va, c * CG + gg + 1)
                        nc.gpsimd.tensor_tensor(rs[:], va[:], mh[:], ALU.pow).then_inc(s_pw, 1)

                copy_rows(0)
                chunk(0, False)
                with pool.Fori(1, NCH - 1) as c:
                    chunk(c, False)
                chunk(NCH - 1, True)
            @block.tensor
            def _(pe):
                pe.wait_ge(s_w0, 16 * 3)

                def turn(c):
                    pe.wait_ge(s_xc, c + 1)
                    for gg in range(CG):
                        for k in range(KD):
                            last = nc.tensor.transpose(ps[:, k, gg * P:(gg + 1) * P],
                                                       xc[:, gg, k * P:(k + 1) * P], C("ident"))
                    last.then_inc(s_xr, 1)

                def logits(c, gg):
                    if gg == 0:
                        pe.wait_ge(s_xT, (c + 1) * KD)
                    for k in range(KD):
                        last = nc.tensor.matmul(ps[:, 0, gg * E:(gg + 1) * E],
                                                xT[:, k, gg, :, :].rearrange("p b n -> p (b n)"),
                                                gate[:, k, :], start=(k == 0), stop=(k == KD - 1),
                                                skip_group_check=True)
                    if gg == CG - 1:
                        last.then_inc(s_lp, 1)

                def up(c, n):
                    v, k = n // KD, n % KD
                    if n == KD:
                        pe.wait_ge(s_r, c * NR + 1)
                    last = nc.tensor.matmul(ps[:, 1 - v, 0:CT], a13[:, v, k, :],
                                            xT[:, k, :, :, 0:T], start=(k == 0), stop=(k == KD - 1),
                                            skip_group_check=True)
                    if n == 2 * KD - 1:
                        last.then_inc(s_up, 1)

                def pick(c, e, first=False):
                    if e == 0:
                        if first:
                            pe.wait_ge(s_sk, 1)
                        pe.wait_ge(s_ul, (c + 1) * 2)
                    for v in range(2):
                        n = e * 2 + v
                        if n >= 2:
                            pe.wait_ge(s_um, c * 2 * E + n - 1)
                        nc.tensor.matmul(ps[:, v, 0:CT], stack[:, e, 0, :], uh[:, v, :], start=True, stop=False)
                        nc.tensor.matmul(ps[:, v, 0:CT], stack[:, e, 1, :], ul[:, v, :], start=False,
                                         stop=True).then_inc(s_sp, 1)

                def weights(c):
                    pe.wait_ge(s_um, (c + 1) * 2 * E)
                    pe.wait_ge(s_r, (c + 1) * NR)
                    nc.tensor.transpose(ps[0:CG * E, 3, 0:P], wr[:].rearrange("p g e -> p (g e)"),
                                        C("ident")).then_inc(s_wt, 1)
                    pe.wait_ge(s_bd, c + 1)
                    for e in range(E):
                        if e >= 4:
                            pe.wait_ge(s_we, c * E + e - 3)
                        lo = CONST["expert"][0] + e
                        nc.tensor.matmul(ps[:, e % 4, 0:CT],
                                         cst[:, lo:lo + 1].to_broadcast([P, P]),
                                         wbd[:].rearrange("p g b n -> p (g b n)"), start=True,
                                         stop=True).then_inc(s_wp, 1)

                turn(0)
                for gg in range(CG):
                    logits(0, gg)
                for n in range(2 * KD):
                    up(0, n)
                for e in range(E):
                    pick(0, e, True)
                weights(0)
                pe.wait_ge(s_w, 16 * 4)

                def chunk(c, first, last_chunk):
                    pe.wait_ge(s_we, (c + 1) * E)

                    def base(f, v, k):
                        nc.tensor.matmul(ps[:, hb(f) + v, 0:CT], w13[:, v, k, f * P:(f + 1) * P],
                                         xT[:, k, :, :, 0:T], start=(k == 0), stop=False, skip_group_check=True)

                    def down(b):
                        n = 8 * (b // 2) + b % 2
                        pe.wait_ge(s_wg, c * NFE + n + 7)
                        for q in range(4):
                            f, e = FE[n + 2 * q]
                            last = nc.tensor.matmul(ps[32 * q:32 * q + 32, U2B + e // 4, 0:CT], a2[:, f, e, :],
                                                    wt[:, (n + 2 * q) % RING, :], start=(f == 0),
                                                    stop=(f == NF - 1), skip_group_check=True)
                        last.then_inc(s_u2, 1)

                    for n, (f, e) in enumerate(FE):
                        if n >= 2:
                            pe.wait_ge(s_si, c * NFE + n - 1)
                            pe.wait_ge(s_pg, c * NFE + n - 1)
                        if first and f == 0:
                            pe.wait_ge(s_stp, 2 * (e + 1))
                        if e == 0 and f not in EARLY:
                            for v in range(2):
                                for k in range(KD):
                                    base(f, v, k)
                        for v in range(2):
                            last = nc.tensor.matmul(ps[:, hb(f) + v, 0:CT], step13[:, v, e, f * P:(f + 1) * P],
                                                    um[:, v, e, :], start=False, stop=True, skip_group_check=True)
                        last.then_inc(s_h, 1)
                        if f % 2 == 0 and f + 2 in EARLY and 2 <= e < 2 + 2 * KD:
                            base(f + 2, (e - 2) // KD, (e - 2) % KD)
                        if n > 8 and n % 8 in (1, 2):
                            down((n // 8 - 1) * 2 + n % 8 - 1)
                        if not last_chunk:
                            if n == TURN:
                                turn(c + 1)
                            for gg in LOGITS.get(n, ()):
                                logits(c + 1, gg)
                            if n in UP:
                                up(c + 1, UP[n])
                            for expert in PICK.get(n, ()):
                                pick(c + 1, expert)
                    for b in range(NDN - 2, NDN):
                        down(b)
                    if not last_chunk:
                        pe.wait_ge(s_si, (c + 1) * NFE)
                        pe.wait_ge(s_pg, (c + 1) * NFE)
                        weights(c + 1)
                    pe.wait_ge(s_ac, sums_done(c, NFE - 1))
                    pe.wait_ge(s_u2s, (c + 1) * 2)
                    for gg in range(CG):
                        for f in range(NF + 2):
                            for par in range(2):
                                cols = slice((2 * gg + par) * T, (2 * gg + par + 1) * T)
                                o = ps[SLOT * par:SLOT * par + T, OB + gg // 2, (gg % 2) * D:(gg % 2 + 1) * D]
                                last = nc.tensor.matmul(o, acc[:, f, cols] if f < NF else u2[:, f - NF, cols],
                                                        w2[:, f, :] if f < NF else b2[:, f - NF, :],
                                                        start=(f == 0), stop=(f == NF + 1), skip_group_check=True)
                        if gg % 2:
                            last.then_inc(s_o, 1)

                chunk(0, True, False)
                with pe.Fori(1, NCH - 1) as c:
                    chunk(c, False, False)
                chunk(NCH - 1, False, True)
            @block.scalar
            def _(act):
                act.wait_ge(s_w0, 16 * 3)
                nc.scalar.activation(stack[:].rearrange("p e v n -> p (e v n)"),
                                     acc[:].rearrange("p f n -> p (f n)")[:, 0:E * 2 * P],
                                     ACT.Copy).then_inc(s_sk, 1)

                def rows(c):
                    act.wait_ge(s_xr, c + 1)
                    for k in range(KD):
                        nc.scalar.activation(xT[:, k, :, :, :].rearrange("p g b n -> p (g b n)"), ps[:, k, :],
                                             ACT.Copy).then_inc(s_xT, 1)

                def high_parts(c):
                    act.wait_ge(s_up, c + 1)
                    for v in range(2):
                        nc.scalar.activation(uh[:, v, :], ps[:, 1 - v, 0:CT], ACT.Copy,
                                             scale=2.0).then_inc(s_uh, 1)

                def picked(c, e):
                    for v in range(2):
                        act.wait_ge(s_sp, c * 2 * E + e * 2 + v + 1)
                        nc.scalar.activation(um[:, v, e, :], ps[:, v, 0:CT], ACT.Copy).then_inc(s_um, 1)

                def exponential(c):
                    act.wait_ge(s_r, c * NR + 10)
                    nc.scalar.activation(tt[:], dif[:], ACT.Exp).then_inc(s_e, 1)

                def weights(c):
                    act.wait_ge(s_wt, c + 1)
                    nc.scalar.activation(wT[:], ps[0:CG * E, 3, 0:P], ACT.Copy).then_inc(s_wT, 1)
                    for e in range(E):
                        act.wait_ge(s_wp, c * E + e + 1)
                        nc.scalar.activation(we[:, e, :], ps[:, e % 4, 0:CT], ACT.Copy).then_inc(s_we, 1)

                rows(0)
                high_parts(0)
                for e in range(E):
                    picked(0, e)
                exponential(0)
                weights(0)

                def chunk(c, last_chunk):
                    for n, (f, e) in enumerate(FE):
                        w = FT[f][1]
                        act.wait_ge(s_h, c * NFE + n + 1)
                        if n >= 2:
                            act.wait_ge(s_pg, c * NFE + n - 1)
                        nc.scalar.activation(si[0:w, n % 2, :], ps[0:w, hb(f), 0:CT],
                                             ACT.Silu).then_inc(s_si, 1)
                        if not last_chunk:
                            if n == TURN:
                                rows(c + 1)
                            if n == SPLIT:
                                high_parts(c + 1)
                            for expert in PICK.get(n, ()):
                                picked(c + 1, expert)
                    if not last_chunk:
                        exponential(c + 1)
                    act.wait_ge(s_u2, (c + 1) * NDN)
                    for h in range(2):
                        nc.scalar.activation(u2[:, h, :], ps[:, U2B + h, 0:CT], ACT.Copy,
                                             scale=2.0).then_inc(s_u2s, 1)
                    if not last_chunk:
                        act.wait_ge(s_wg, (c + 1) * NFE)
                        weights(c + 1)

                chunk(0, False)
                with act.Fori(1, NCH - 1) as c:
                    chunk(c, False)
                chunk(NCH - 1, True)
            @block.vector
            def _(dve):
                nc.vector.memset(mh[:], -0.5).then_inc(s_low, 1)
                nc.vector.memset(ps[:, OB:OB + 2, :], 0.0).then_inc(s_low, 1)
                nc.vector.memset(wbd[:], 0.0).then_inc(s_low, 1)
                dve.wait_ge(s_low, 3)

                def factors(e):
                    dve.wait_ge(s_bw[e % RAW], 16 * (e // RAW + 1))
                    for v in range(2):
                        n = e * 2 + v
                        if n:
                            dve.wait_ge(s_stp, n)
                        nc.vector.tensor_scalar(high, raws[e % RAW][:, v, :], C("sign_low"), None,
                                                ALU.mult).then_inc(s_hi, 1)
                        dve.wait_ge(s_hi, n + 1)
                        nc.vector.scalar_tensor_tensor(out=step13[:, v, e, :], in0=raws[e % RAW][:, v, :],
                                                       scalar=C("sign"), in1=high.bitcast(F32), op0=ALU.mult,
                                                       op1=ALU.subtract).then_inc(s_stp, 1)

                v = nc.vector
                wide = [P, CG, E]

                def chain(c, done):
                    count = [done]

                    def link(ins):
                        count[0] += 1
                        ins.then_inc(s_r, 1)
                        dve.wait_ge(s_r, c * NR + count[0])
                    return link, count

                def choose(c):
                    dve.wait_ge(s_lp, c + 1)
                    link, count = chain(c, 0)
                    link(v.tensor_copy(lg[:].rearrange("p g e -> p (g e)"), ps[:, 0, 0:CG * E]))
                    link(v.tensor_copy(l2[:], lg[:]))
                    for n in range(2):
                        link(v.reduce_max(top[n][:], l2[:], AX.X))
                        if n == 1:
                            link(v.tensor_tensor(dif[:], top[1][:], top[0][:], ALU.subtract))
                        link(v.tensor_tensor(eq[:], l2[:], top[n][:].unsqueeze(2).to_broadcast(wide), ALU.is_equal))
                        link(v.scalar_tensor_tensor(out=cand[:], in0=eq[:], scalar=-float(E),
                                                    in1=C("iota").unsqueeze(1).to_broadcast(wide), op0=ALU.mult,
                                                    op1=ALU.add))
                        link(v.tensor_reduce(idx[:], cand[:], AX.X, ALU.min))
                        link(v.tensor_tensor(oh[n][:], cand[:], idx[:].unsqueeze(2).to_broadcast(wide), ALU.is_equal))
                        if n == 0:
                            link(v.scalar_tensor_tensor(out=l2[:], in0=oh[0][:], scalar=-3.0e38, in1=lg[:],
                                                        op0=ALU.mult, op1=ALU.add))
                    assert count[0] == NR - 6, count[0]

                def low_parts(c):
                    for n in range(2):
                        dve.wait_ge(s_uh, c * 2 + n + 1)
                        v.scalar_tensor_tensor(out=ul[:, n, :], in0=ps[:, 1 - n, 0:CT], scalar=2.0,
                                               in1=uh[:, n, :].bitcast(F32), op0=ALU.mult,
                                               op1=ALU.subtract).then_inc(s_ul, 1)

                def weights(c):
                    dve.wait_ge(s_e, c + 1)
                    link, count = chain(c, NR - 6)
                    link(v.tensor_scalar_add(t1[:], tt[:], 1.0))
                    link(v.reciprocal(r1[:], t1[:]))
                    link(v.tensor_tensor(wA[:], oh[0][:], r1[:].unsqueeze(2).to_broadcast(wide), ALU.mult))
                    link(v.tensor_tensor(r2[:], tt[:], r1[:], ALU.mult))
                    link(v.tensor_tensor(wB[:], oh[1][:], r2[:].unsqueeze(2).to_broadcast(wide), ALU.mult))
                    link(v.tensor_tensor(wr[:], wA[:], wB[:], ALU.add))
                    assert count[0] == NR, count[0]
                    dve.wait_ge(s_wT, c + 1)
                    v.tensor_tensor(
                        wbd[0:CG * E],
                        wT[:].rearrange("p (b n) -> p b n", n=SLOT)[:, :, 0:T].unsqueeze(1)
                        .to_broadcast([CG * E, CG, 2, T]),
                        C("grp", CG * E).unsqueeze(2).unsqueeze(3).to_broadcast([CG * E, CG, 2, T]),
                        ALU.mult).then_inc(s_bd, 1)

                choose(0)
                low_parts(0)
                weights(0)

                def chunk(c, first, last_chunk):
                    def weigh(n):
                        dve.wait_ge(s_pg, c * NFE + n + 1)
                        if n >= RING:
                            m = n - RING
                            dve.wait_ge(s_ac, sums_done(c, m + (2 if FE[m][1] == 0 else 0)))
                            dve.wait_ge(s_u2, c * NDN + m // 8 * 2 + m % 2 + 1)
                        v.tensor_tensor(wt[:, n % RING, :], pg[:, n % 3, :], we[:, FE[n][1], :],
                                        ALU.mult).then_inc(s_wg, 1)

                    if first:
                        factors(0)
                        factors(1)
                    dve.wait_ge(s_we, (c + 1) * E)
                    for n, (f, e) in enumerate(FE):
                        w = FT[f][1]
                        if first and f == 0 and e + 2 < E:
                            factors(e + 2)
                        if n >= 3:
                            dve.wait_ge(s_wg, c * NFE + n - 2)
                        dve.wait_ge(s_si, c * NFE + n + 1)
                        v.tensor_tensor(pg[:, n % 3, :], si[:, n % 2, :], ps[:, hb(f) + 1, 0:CT],
                                        ALU.mult).then_inc(s_pg, 1)
                        if n > 0:
                            weigh(n - 1)
                        if not last_chunk:
                            if n == TURN + 3:
                                choose(c + 1)
                            if n == SPLIT:
                                low_parts(c + 1)
                    weigh(NFE - 1)
                    if not last_chunk:
                        weights(c + 1)
                    for gg in range(CG):
                        g = c * CG + gg
                        if gg % 2 == 0:
                            dve.wait_ge(s_o, c * 2 + gg // 2 + 1)
                        dve.wait_ge(s_ob, g)
                        v.tensor_tensor(y, ps[:, OB + gg // 2, (gg % 2) * D:(gg % 2 + 1) * D], X[:, bass.ds(g, 1), :].rearrange("p a d -> p (a d)"),
                                        ALU.add).then_inc(s_y, 1)
                        dve.wait_ge(s_y, g + 1)
                        v.bn_stats(st[:], y).then_inc(s_bn, 1)
                        dve.wait_ge(s_low, 2)
                        dve.wait_ge(s_bn, g + 1)
                        v.bn_aggr(mv[:], st[:]).then_inc(s_ag, 1)
                        dve.wait_ge(s_ag, g + 1)
                        v.tensor_scalar_add(va[:], mv[:, 1:2], EPS).then_inc(s_va, 1)
                        dve.wait_ge(s_pw, g + 1)
                        if gg >= 2:
                            dve.wait_ge(s_st[gg % 2], (c * 2 + gg // 2) * 32)
                        else:
                            dve.wait_ge(s_st[gg % 2], c * 64)
                        v.tensor_scalar(ob[:, gg % 2, :], y, mv[:, 0:1], rs[:, 0:1], ALU.subtract,
                                        ALU.mult).then_inc(s_ob, 1)

                chunk(0, True, False)
                with dve.Fori(1, NCH - 1) as c:
                    chunk(c, False, False)
                chunk(NCH - 1, False, True)

def program(nc, a):
    with ExitStack() as ctx:
        a["cst"] = ctx.enter_context(nc.sbuf_tensor("cst", [P, CW], F32))
        a["X"] = ctx.enter_context(nc.sbuf_tensor("X", [P, GR, D], F32))
        a["ps"] = ctx.enter_context(nc.psum_tensor("ps", [P, 8, 512], F32))
        with nc.sbuf_tensor("X1T", [P, KD, B * T], F32) as X1T:
            a["X1T"] = X1T
            self_attention(nc, a)
            cross_attention(nc, a)
        feed_forward(nc, a)


def layouts(i):
    swap = np.arange(D) ^ 1
    wq, wk, wv = i["L0_attn_Wq"], i["L0_attn_Wk"], i["L0_attn_Wv"]
    z = np.zeros((D, DH), wv.dtype)
    t = np.ascontiguousarray

    def wide(m):
        return np.concatenate([m, np.zeros((*m.shape[:-1], FP - F), m.dtype)], -1)

    a2 = np.zeros((FP, E, 32), np.float32)
    a2[0:F, :, 0:R] = i["L0_ffn_a2"].transpose(2, 0, 1)
    b2 = np.zeros((2, 4, 32, D), np.float32)
    b2[:, :, 0:R, :] = i["L0_ffn_b2"].transpose(0, 2, 1).reshape(2, 4, R, D)
    b13 = np.zeros((4, 2, R, 2, E, FP), np.float32)
    for v, n in enumerate(("L0_ffn_b1", "L0_ffn_b3")):
        rows = i[n].transpose(2, 0, 1)
        b13[:, 1, :, v, :, 0:F] = rows
        b13[:, 0, :, v, 1:, 0:F] = rows[:, :-1]
    b13 = b13.reshape(P, 2, E, FP)
    stack = np.zeros((E, R, E, 2, 2, 2, 2, R), np.float32)
    for e in range(E):
        for m in range(2):
            if e - 1 + m >= 0:
                for part in range(2):
                    for n in range(2):
                        stack[e - 1 + m, range(R), e, part, n, part, m, range(R)] = 1.0
    stack = stack.reshape(P, E, 2, P)
    return {
        "consts": constants(),
        "x": i["x"], "xT": t(i["x"].reshape(B * T, D).T),
        "ctx": i["ctx_2048"], "ctxT": t(i["ctx_2048"].transpose(0, 2, 1)),
        "wqT": t(np.stack([wq.T, wq[swap].T], 1)),
        "wkT": t(np.tile(wk, (HB, 1)).T),
        "wvT": t(np.stack([np.concatenate([wv.T, z], 1), np.concatenate([z, wv.T], 1)], 1)),
        "woT": t(i["L0_attn_Wo"].T),
        "gateT": t(i["L0_ffn_gate_w"].T),
        "w13T": wide(np.stack([i["L0_ffn_w1"].T, i["L0_ffn_w3"].T])),
        "a13T": t(np.stack([i["L0_ffn_a1"].reshape(E * R, D).T, i["L0_ffn_a3"].reshape(E * R, D).T])),
        "b13T": b13, "stack": stack,
        "a2T": a2, "b2T": b2.reshape(2, P, D), "w2T": wide(i["L0_ffn_w2"]).T.copy(),
    }


def kernel(**inputs):
    import concourse.bacc as bacc
    from concourse.bass_utils import run_bass_kernel_spmd

    arrays = {f"in_{n}": a for n, a in layouts({n: np.asarray(v) for n, v in inputs.items()}).items()}
    nc = bacc.Bacc("TRN2", target_bir_lowering=False, num_devices=1)
    a = {n[3:]: nc.dram_tensor(n, v.shape, mybir.dt.from_np(v.dtype), kind="ExternalInput").ap()
         for n, v in arrays.items()}
    a["out"] = nc.dram_tensor("out_0", (B, T, D), F32, kind="ExternalOutput").ap()
    program(nc, a)
    r = run_bass_kernel_spmd(nc, [arrays], core_ids=[0])
    return r.results[0]["out_0"]
```
